# Optimizing a Trainium2 kernel written in Bass

```python
import numpy as np
import jax
import jax.numpy as jnp

def _softmax(x, axis=-1):
    return jax.nn.softmax(x, axis=axis)

def _gelu(x):
    return jax.nn.gelu(x, approximate=True)

def _silu(x):
    return jax.nn.silu(x)

def _sigmoid(x):
    return jax.nn.sigmoid(x)

def _layernorm(x, axis=-1, eps=1e-05):
    m = jnp.mean(x, axis=axis, keepdims=True)
    v = jnp.var(x, axis=axis, keepdims=True)
    return (x - m) / jnp.sqrt(v + eps)

def _scatter_add(tgt, idx, src, axis=0):
    return tgt.at[idx].add(src)

def _segment_sum(src, seg, n):
    return jax.ops.segment_sum(src, seg, n)
kernel_name = 'mk_adaln_d1_jaxref_r8_95688f'

def setup_inputs(seed: int=0):
    np.random.seed(seed)
    _w = jnp.asarray

    def _L0_attn_setup():
        import jax, jax.numpy as jnp
        import numpy as np
        EMBED_DIM = 128
        NUM_HEADS = 16
        HEAD_DIM = EMBED_DIM // NUM_HEADS
        FEATURE_EPS = 1e-06
        DEN_EPS = 1e-06
        key = jax.random.key(seed)
        k_x, k_qw, k_qb, k_ow, k_ob = jax.random.split(key, 5)
        b, l = (2, 256)
        x = jax.random.normal(k_x, (b, l, EMBED_DIM), dtype=jnp.float32)
        s = 1.0 / np.sqrt(EMBED_DIM)
        qkv_w = jax.random.uniform(k_qw, (3 * EMBED_DIM, EMBED_DIM), minval=-s, maxval=s, dtype=jnp.float32)
        qkv_b = jax.random.uniform(k_qb, (3 * EMBED_DIM,), minval=-s, maxval=s, dtype=jnp.float32)
        out_w = jax.random.uniform(k_ow, (EMBED_DIM, EMBED_DIM), minval=-s, maxval=s, dtype=jnp.float32)
        out_b = jax.random.uniform(k_ob, (EMBED_DIM,), minval=-s, maxval=s, dtype=jnp.float32)
        return {'x': x, 'qkv_w': qkv_w, 'qkv_b': qkv_b, 'out_w': out_w, 'out_b': out_b}
    _L0_attn_in = _L0_attn_setup()

    def _L0_ffn_setup():
        import jax, jax.numpy as jnp
        import numpy as np
        EPS = float(jnp.finfo(jnp.float32).eps)
        TOP_K = 2

        def rmsnorm(x, w):
            return x * jax.lax.rsqrt(jnp.mean(x * x, axis=-1, keepdims=True) + EPS) * w
        B, T, D_IN, D_MODEL, D_FF, D_OUT, E = (8, 128, 128, 128, 512, 128, 8)
        STD = 0.02
        key = jax.random.key(seed)
        ks = jax.random.split(key, 8)
        return {'s': jax.random.normal(ks[0], (B, T, D_IN), dtype=jnp.float32), 'W_in': STD * jax.random.normal(ks[1], (D_MODEL, D_IN), dtype=jnp.float32), 'in_norm_w': jnp.ones((D_MODEL,), dtype=jnp.float32), 'Wr': STD * jax.random.normal(ks[2], (E, D_MODEL), dtype=jnp.float32), 'expert_bias': jnp.zeros((E,), dtype=jnp.float32), 'Wg': STD * jax.random.normal(ks[3], (E, D_FF, D_MODEL), dtype=jnp.float32), 'Wu': STD * jax.random.normal(ks[4], (E, D_FF, D_MODEL), dtype=jnp.float32), 'Wd': STD * jax.random.normal(ks[5], (E, D_MODEL, D_FF), dtype=jnp.float32), 'enorm_w': jnp.ones((E, D_MODEL), dtype=jnp.float32), 'out_norm_w': jnp.ones((D_MODEL,), dtype=jnp.float32), 'W_out': STD * jax.random.normal(ks[6], (D_OUT, D_MODEL), dtype=jnp.float32)}
    _L0_ffn_in = _L0_ffn_setup()
    _L0_c = _w((lambda *s: np.random.randn(*s).astype(np.float32) * 0.05)(16, 128))
    _L0_wmod = _w((lambda *s: np.random.randn(*s).astype(np.float32) * 0.05)(128, 6 * 128) * 128 ** (-0.5))
    _d = {'L0_attn_x': _L0_attn_in['x'], 'L0_attn_qkv_w': _L0_attn_in['qkv_w'], 'L0_attn_qkv_b': _L0_attn_in['qkv_b'], 'L0_attn_out_w': _L0_attn_in['out_w'], 'L0_attn_out_b': _L0_attn_in['out_b'], 'L0_ffn_W_in': _L0_ffn_in['W_in'], 'L0_ffn_in_norm_w': _L0_ffn_in['in_norm_w'], 'L0_ffn_Wr': _L0_ffn_in['Wr'], 'L0_ffn_expert_bias': _L0_ffn_in['expert_bias'], 'L0_ffn_Wg': _L0_ffn_in['Wg'], 'L0_ffn_Wu': _L0_ffn_in['Wu'], 'L0_ffn_Wd': _L0_ffn_in['Wd'], 'L0_ffn_enorm_w': _L0_ffn_in['enorm_w'], 'L0_ffn_out_norm_w': _L0_ffn_in['out_norm_w'], 'L0_ffn_W_out': _L0_ffn_in['W_out'], 'L0_c': _L0_c, 'L0_wmod': _L0_wmod}
    _x0 = _d['L0_attn_x']
    _d['L0_attn_x'] = jax.random.normal(jax.random.fold_in(jax.random.key(seed), 1), (16, 256, 128), dtype=_x0.dtype)
    del _x0
    return _d

def reference(L0_attn_x, L0_attn_qkv_w, L0_attn_qkv_b, L0_attn_out_w, L0_attn_out_b, L0_ffn_W_in, L0_ffn_in_norm_w, L0_ffn_Wr, L0_ffn_expert_bias, L0_ffn_Wg, L0_ffn_Wu, L0_ffn_Wd, L0_ffn_enorm_w, L0_ffn_out_norm_w, L0_ffn_W_out, L0_c, L0_wmod):

    def _L0_attn_ref(x, qkv_w, qkv_b, out_w, out_b):
        import jax, jax.numpy as jnp
        import numpy as np
        EMBED_DIM = 128
        NUM_HEADS = 16
        HEAD_DIM = EMBED_DIM // NUM_HEADS
        FEATURE_EPS = 1e-06
        DEN_EPS = 1e-06
        b, l, e = x.shape
        qkv = (x @ qkv_w.T + qkv_b).reshape(b, l, 3, NUM_HEADS, HEAD_DIM)
        qkv = jnp.transpose(qkv, (2, 0, 3, 1, 4))
        q, k, v = (qkv[0], qkv[1], qkv[2])
        q = jax.nn.relu(q) + FEATURE_EPS
        k = jax.nn.relu(k) + FEATURE_EPS
        kv = jnp.cumsum(jnp.einsum('bhld,bhle->bhlde', k, v), axis=2)
        k_cum = jnp.cumsum(k, axis=2)
        num = jnp.einsum('bhld,bhlde->bhle', q, kv)
        den = jnp.maximum(jnp.einsum('bhld,bhld->bhl', q, k_cum)[..., None], DEN_EPS)
        out = num / den
        out = jnp.transpose(out, (0, 2, 1, 3)).reshape(b, l, e)
        return out @ out_w.T + out_b

    def _L0_ffn_ref(s, W_in, in_norm_w, Wr, expert_bias, Wg, Wu, Wd, enorm_w, out_norm_w, W_out):
        import jax, jax.numpy as jnp
        import numpy as np
        EPS = float(jnp.finfo(jnp.float32).eps)
        TOP_K = 2

        def rmsnorm(x, w):
            return x * jax.lax.rsqrt(jnp.mean(x * x, axis=-1, keepdims=True) + EPS) * w
        B, T, _ = s.shape
        x = s.reshape(B * T, -1)
        h = rmsnorm(x @ W_in.T, in_norm_w)
        logits = h @ Wr.T
        _, idx = jax.lax.top_k(logits + expert_bias, TOP_K)
        sel = jnp.take_along_axis(logits, idx, axis=-1)
        g_topk = jax.nn.softmax(sel, axis=-1)
        N = logits.shape[0]
        gates = jnp.zeros_like(logits).at[jnp.arange(N)[:, None], idx].set(g_topk)
        out = jnp.zeros_like(h)
        for e in range(Wg.shape[0]):
            gate = jax.nn.silu(h @ Wg[e].T)
            up = h @ Wu[e].T
            oe = rmsnorm(gate * up @ Wd[e].T, enorm_w[e])
            out = out + gates[:, e:e + 1] * oe
        s_hat = rmsnorm(out, out_norm_w) @ W_out.T
        return s_hat.reshape(B, T, -1)
    x = L0_attn_x
    mod = (_silu(L0_c) @ L0_wmod).reshape(L0_c.shape[0], 6, 1, -1)
    sa, ca, ga, sb, cb, gb = (mod[:, 0], mod[:, 1], mod[:, 2], mod[:, 3], mod[:, 4], mod[:, 5])
    ga = (2 * (ga >= 0) - 1) * jnp.maximum(jnp.abs(ga), 0.25)
    gb = (2 * (gb >= 0) - 1) * jnp.maximum(jnp.abs(gb), 0.25)
    h = _layernorm(x, axis=-1) * (1 + ca) + sa
    x = x + ga * _L0_attn_ref(h, L0_attn_qkv_w, L0_attn_qkv_b, L0_attn_out_w, L0_attn_out_b)
    h = _layernorm(x, axis=-1) * (1 + cb) + sb
    x = x + gb * _L0_ffn_ref(h, L0_ffn_W_in, L0_ffn_in_norm_w, L0_ffn_Wr, L0_ffn_expert_bias, L0_ffn_Wg, L0_ffn_Wu, L0_ffn_Wd, L0_ffn_enorm_w, L0_ffn_out_norm_w, L0_ffn_W_out)
    return x

_drawn_inputs = setup_inputs


def setup_inputs(seed=0):
    import zlib

    import numpy as np

    out = dict(_drawn_inputs(seed))
    spreads = {'L0_ffn_in_norm_w': (1.0, 0.565),
     'L0_ffn_expert_bias': (0.0, 0.1),
     'L0_ffn_enorm_w': (1.0, 0.6),
     'L0_ffn_out_norm_w': (1.0, 0.6)}
    factors = {'L0_attn_qkv_w': 3.028,
     'L0_attn_qkv_b': 5.772,
     'L0_attn_out_w': 2.783,
     'L0_attn_out_b': 3.998}
    for name, (base, spread) in spreads.items():
        noise = np.random.default_rng([zlib.crc32(name.encode()), seed]).standard_normal(out[name].shape)
        drawn = base * np.exp(spread * noise) if base else spread * noise
        out[name] = jnp.asarray(drawn.astype(out[name].dtype))
    for name, factor in factors.items():
        out[name] = (out[name] * factor).astype(out[name].dtype)
    return out
```

```python
from contextlib import ExitStack

import numpy as np

import concourse.bass as bass
from concourse import mybir

F32 = mybir.dt.float32
F16 = mybir.dt.float16
I32 = mybir.dt.int32
U32 = mybir.dt.uint32
ALU = mybir.AluOpType
ACT = mybir.ActivationFunctionType
AX = mybir.AxisListType

P = 128
B, L, D = 16, 256, 128
H, HD = 16, 8
NT = L // P
TOK = B * L
E, F, K = 8, 512, 2
FC = F // P
HE = HD + 1
STATE = H * HE * HD
HEADS = [(0, 5), (5, 10), (10, 16)]
REGION = TOK + P
TILES = 72
SPARE = TILES - TOK * K // P
HROWS = E * REGION + SPARE * P
YROWS = TOK * K + (E + SPARE) * P
HW = D + 1
YW = D + 1
LN_EPS = 1e-5
F_EPS = 1e-6
RMS_EPS = float(np.finfo(np.float32).eps)
HSCALE = 2.0 ** 11
SA, CA, GA, SB, CB, GB = range(6)

C_ID, C_TRI, C_ONES, C_STRICT = 0, P, 2 * P, 3 * P
C_REG, C_IOTA, C_TAIL = 4 * P, 4 * P + E, 4 * P + 2 * E
C_J = 4 * P + 3 * E
C_LOW = C_J + TOK // P
C_T = C_LOW + E * E
C_END = C_T + TILES


def shape_constants():
    c = np.zeros((P, C_END), np.float32)
    p = np.arange(P)
    c[:, C_ID:C_ID + P] = np.eye(P)
    c[:, C_TRI:C_TRI + P] = p[:, None] <= p[None, :]
    c[:, C_ONES:C_ONES + P] = 1
    c[:, C_STRICT:C_STRICT + P] = p[:, None] < p[None, :]
    c[:, C_REG:C_REG + E] = np.arange(E) * REGION
    c[:, C_IOTA:C_IOTA + E] = np.arange(E)
    c[:, C_TAIL:C_TAIL + E] = np.arange(E) * REGION + p[:, None]
    c[:, C_J:C_J + TOK // P] = np.arange(TOK // P) * P
    c[:, C_LOW:C_LOW + E * E] = (np.arange(E)[:, None] > np.arange(E)[None, :]).ravel()
    c[:, C_T:C_T + TILES] = np.arange(TILES)
    token = np.arange(TOK // P)[None, :, None] * P + p[:, None, None]
    place = (token * K + np.arange(K)).reshape(P, -1).astype(np.uint32)
    filler = (TOK * K + np.arange(E + SPARE)[None, :] * P + p[:, None]).astype(np.uint32)
    return c, place, filler


def block_kernel(nc, x, cT, wmod, qkv_wT, qkv_b, out_wT, out_b, w_inT, in_norm, wrT, e_bias, wguT, wdT,
                 e_norm, out_norm, w_outT, consts, place, filler, out):
    ctx = ExitStack()
    with ctx:
        def sb(name, shape, dt=F32):
            return ctx.enter_context(nc.sbuf_tensor(name, shape, dt))

        def sem(name):
            return ctx.enter_context(nc.semaphore(name))

        def two(name):
            return [sem(f"{name}{i}") for i in range(2)]

        def four(name):
            return [sem(f"{name}{i}") for i in range(4)]

        hbuf = nc.dram_tensor("dispatched", [HROWS, HW], U32, kind="Internal").ap()
        ybuf = nc.dram_tensor("expert_rows", [YROWS, YW], F32, kind="Internal").ap()

        x_all = sb("x_all", [P, B * L])
        cst = sb("cst", [P, C_END])
        place_sb = sb("place_sb", [P, B * NT * K], U32)
        fill = sb("fill", [P, E + SPARE, HW], U32)
        ident, tri, ones, strict = (cst[:, c:c + P] for c in (C_ID, C_TRI, C_ONES, C_STRICT))
        cT_sb = sb("cT_sb", [P, B])
        sc = sb("sc", [P, B])
        wmod_sb = sb("wmod_sb", [P, 6 * D])
        wqkv = sb("wqkv", [P, 3 * D])
        bqkv = sb("bqkv", [1, 3 * D])
        wo = sb("wo", [P, D])
        bo = sb("bo", [1, D])
        w_in = sb("w_in", [P, D])
        innorm = sb("innorm", [P, 1])
        wr = sb("wr", [P, E])
        wrn = sb("wrn", [P, E])
        ebias = sb("ebias", [P, E])
        wgu = sb("wgu", [P, 2 * E * F])
        w_hi = sb("w_hi", [P, 2 * E * F], F16)
        w_lo = sb("w_lo", [P, 2 * E * F], F16)
        wd = sb("wd", [P, E * FC * D])
        enorm = sb("enorm", [P, E * D])
        onorm = sb("onorm", [P, 1])
        wout = sb("wout", [P, D])
        woutn = sb("woutn", [P, D])
        mod_cols = sb("mod_cols", [P, 4 * B])
        gates_bc = sb("gates_bc", [P, B * 2 * D])
        eps_ln = sb("eps_ln", [P, 1])
        eps_f = sb("eps_f", [P, 1])
        eps_rms = sb("eps_rms", [P, 1])
        lsel_all = sb("lsel_all", [P, B * NT * K])
        ldiff = sb("ldiff", [P, B * NT])
        gate_all = sb("gate_all", [P, B * NT, K])

        early = w_lo[:].bitcast(F32)
        gaob = early[0:1, 0:B * D]
        early_hi = w_hi[:].bitcast(F32)
        clamp_a, clamp_s = (early_hi[:, i * 4 * D:(i + 1) * 4 * D] for i in range(2))

        st = sb("st", [P, 2, NT, 6])
        mv = sb("mv", [P, 2, NT, 2])
        sd = sb("sd", [P, 2, NT])
        rs = sb("rs", [P, 2, NT])
        xn = sb("xn", [P, 2, NT, D])
        hT = sb("hT", [P, 2, L])
        qk_raw = sb("qk_raw", [P, 2, NT, 2 * D])
        q = sb("q", [P, 2, NT, D])
        v = sb("v", [P, 2, NT, D])
        kv = sb("kv", [P, 2, NT, STATE])
        prod = sb("prod", [P, NT, STATE])
        nd = sb("nd", [P, NT * H, HE])
        den = sb("den", [P, NT * H])
        rden = sb("rden", [P, NT * H])
        attn = sb("attn", [P, 2, NT, D])
        attnT = sb("attnT", [P, 2, L])
        wo_ga = sb("wo_ga", [P, 2, D])
        st2 = sb("st2", [P, 2, NT, 6])
        mv2 = sb("mv2", [P, 2, NT, 2])
        sd2 = sb("sd2", [P, 2, NT])
        rs2 = sb("rs2", [P, 2, NT])
        xn2 = sb("xn2", [P, 2, NT, D])
        h2T = sb("h2T", [P, 2, L])
        junk = sb("junk", [P, D])
        ssq = sb("ssq", [P, 2, NT])
        rms = sb("rms", [P, 2, NT])
        rr = sb("rr", [P, 2, NT])
        rrs = sb("rrs", [P, 2, NT])
        uT = sb("uT", [P, 2, L])
        rows = sb("rows", [P, 2, NT, K, HW], U32)
        rows16 = rows[:].bitcast(F16)
        lr = sb("lr", [P, 2, NT, E])
        score = sb("score", [P, 2, NT, E])
        m8 = sb("m8", [P, 2, NT, 8])
        i8 = sb("i8", [P, 2, NT, 8], U32)
        i8f = sb("i8f", [P, 2, NT, K])
        oh = sb("oh", [P, 2, NT, K, E])
        ohl = sb("ohl", [P, 2, NT, K, E])
        chosen = sb("chosen", [P, 2, NT, E])
        chosen2 = sb("chosen2", [P, 2, E])
        count = sb("count", [P, 2, E])
        slot = sb("slot", [P, 2, NT, E])
        ohs = sb("ohs", [P, 2, NT, K, E])
        posf = sb("posf", [P, 2, NT, K])
        pos = sb("pos", [P, 2, NT * K], U32)

        spare = prod[0:1].rearrange("o t s -> o (t s)")
        tcmp, tge, tgn = (spare[:, a:a + n * m].rearrange("o (n m) -> o n m", m=m) for a, n, m in (
            (0, E, TOK // P), (E * TOK // P, TILES, E), (E * TOK // P + TILES * E, TILES, E)))
        wmax = sb("wmax", [P, 1])
        wmax_all = sb("wmax_all", [P, 1])
        wpow = sb("wpow", [P, 1])
        wscale = sb("wscale", [P, 1])
        descale = sb("descale", [P, 1])
        total = sb("total", [P, E])
        tail_f = sb("tail_f", [P, E])
        tail = sb("tail", [P, E], U32)
        ntile = sb("ntile", [1, E])
        tlow = sb("tlow", [1, E, E])
        tstart = sb("tstart", [1, E])
        tend = sb("tend", [1, E])
        texp = sb("texp", [1, TILES])
        tfirst = sb("tfirst", [1, TILES])
        trel = sb("trel", [1, TILES])
        trow_f = sb("trow_f", [1, TILES])
        tile_row = sb("tile_row", [1, TILES], I32)
        tile_expert = sb("tile_expert", [1, TILES], I32)

        slots = sb("slots", [P, 4, HW], U32)
        slots16 = slots[:].bitcast(F16)
        ident16 = sb("ident16", [P, P], F16)
        hT3 = sb("hT3", [P, 2, 2 * P], F16)
        sg, gu = (kv[:, i].rearrange("p t s -> p (t s)")[:, 0:2 * F].rearrange("p (j f) -> p j f", f=F)
                  for i in range(2))
        yt = sb("yt", [P, 4, YW])
        junk3 = sb("junk3", [P, D])

        rms4 = sb("rms4", [P, 2, NT, K])
        rinv4 = sb("rinv4", [P, 2, NT, K])
        coef = sb("coef", [P, 2, NT, K])
        ssq4 = sb("ssq4", [P, 2, NT])
        rms5 = sb("rms5", [P, 2, NT])
        rinv5 = sb("rinv5", [P, 2, NT])
        wout_gb = sb("wout_gb", [P, 2, D])
        half, mix, mixT, ob = (wgu[:, i * 2 * L:(i + 1) * 2 * L].rearrange("p (j t d) -> p j t d", j=2, t=NT)
                               for i in range(4))
        mixT = mixT.rearrange("p j t d -> p j (t d)")
        yb = wgu[:, 8 * L:8 * L + 2 * NT * K * YW].rearrange("p (j t w) -> p j t w", j=2, t=NT)

        bk = [ctx.enter_context(nc.psum_tensor(f"bank{i}", [P, 512], F32)) for i in range(8)]
        CUM = bk[0:3]
        LNT, QKV, PROJ, FFN, UB = bk[3:8]

        x_first, x_rest, c_ld, w_ld, moe_ld, fill_ld = (
            sem(n) for n in ("x_first", "x_rest", "c_ld", "w_ld", "moe_ld", "fill_ld"))
        eps_set, cst_set, fill_set = sem("eps_set"), sem("cst_set"), sem("fill_set")
        sc_done, modcol_ps, modcol_done = sem("sc_done"), sem("modcol_ps"), sem("modcol_done")
        gate_ps, clamp_1, clamp_2, clamp_3, gate_done, gaob_done = (
            sem(n) for n in ("gate_ps", "clamp_1", "clamp_2", "clamp_3", "gate_done", "gaob_done"))
        w_small = sem("w_small")
        ln_mv, ln_sd, ln_rs, xn_done = (sem(n) for n in ("ln_mv", "ln_sd", "ln_rs", "xn_done"))
        xnT_ps, hT_done = sem("xnT_ps"), sem("hT_done")
        qkv_ps = [sem(f"qkv_ps_{t}") for t in range(NT)]
        raw_done = [sem(f"raw_done_{t}") for t in range(NT)]
        qkv_done = [sem(f"qkv_done_{t}") for t in range(NT)]
        kv_done = [sem(f"kv_done_{t}") for t in range(NT)]
        cum_ps = [[sem(f"cum_ps_{t}_{c}") for c in range(3)] for t in range(NT)]
        cum_used = [[sem(f"cum_used_{t}_{c}") for c in range(3)] for t in range(NT)]
        nd_done, den_done, rden_done, attn_done = (sem(n) for n in ("nd_done", "den_done", "rden_done", "attn_done"))
        attnT_ps, attnT_done, wo_done, x1_ps, x1_done = (
            sem(n) for n in ("attnT_ps", "attnT_done", "wo_done", "x1_ps", "x1_done"))
        ln2_mv, ln2_sd, ln2_rs, xn2_done = (
            sem(n) for n in ("ln2_mv", "ln2_sd", "ln2_rs", "xn2_done"))
        xn2T_ps, h2T_done, u_ps, uT_done, ssq_done, rms_done, rr_done, rrs_done = (
            sem(n) for n in ("xn2T_ps", "h2T_done", "u_ps", "uT_done", "ssq_done", "rms_done", "rr_done", "rrs_done"))
        hi_done, lo_done, rows_done, place_done = (
            sem(n) for n in ("hi_done", "lo_done", "rows_done", "place_done"))
        ln_st, ln2_st = two("ln_st"), sem("ln2_st")
        scattered, yb_ld, stored = two("scattered"), two("yb_ld"), two("stored")
        logit_ps, lr_done, score_done, max_done, idx_done, idxf_done, oh_done = (
            sem(n) for n in ("logit_ps", "lr_done", "score_done", "max_done", "idx_done", "idxf_done", "oh_done"))
        chosen_done, chosen2_done, count_done, ohl_done, lsel_done = (
            sem(n) for n in ("chosen_done", "chosen2_done", "count_done", "ohl_done", "lsel_done"))
        rank_ps, slot_done, ohs_done, posf_done, pos_done = (
            sem(n) for n in ("rank_ps", "slot_done", "ohs_done", "posf_done", "pos_done"))
        ph2, total_ps, tail_done, table_done, tail_scat, wmax_done, wall_done, wscale_done, whi_done, wlo_done = (
            sem(n) for n in ("ph2", "total_ps", "tail_done", "table_done", "tail_scat", "wmax_done", "wall_done",
                             "wscale_done", "whi_done", "wlo_done"))
        gate_diff, gate_sig = sem("gate_diff"), sem("gate_sig")
        slot_ld, y_scat, y_done = four("slot_ld"), four("y_scat"), four("y_done")
        slotT_ps, hT3_done, g_ps, u3_ps, sg_done, gu_done, y_ps, ysq_done = (
            sem(n) for n in ("slotT_ps", "hT3_done", "g_ps", "u3_ps", "sg_done", "gu_done", "y_ps", "ysq_done"))
        rms4_done, rinv4_done, coef_done, half_done, mix_done, mixT_ps, mixT_done = (
            sem(n) for n in ("rms4_done", "rinv4_done", "coef_done", "half_done", "mix_done", "mixT_ps",
                             "mixT_done"))
        ssq4_done, rms5_done, rinv5_done, wgb_done, o_ps, ob_done = (
            sem(n) for n in ("ssq4_done", "rms5_done", "rinv5_done", "wgb_done", "o_ps", "ob_done"))

        block = ctx.enter_context(nc.Block())

        def again(n):
            return not (isinstance(n, int) and n <= 1)

        def pipelined(eng, step):
            def at(s):
                return (s, s % 2, s // 2 + 1) if 0 <= s < B else None
            for s in range(4):
                step(at(s), at(s - 1), at(s - 2), at(s - 3))
            with eng.Fori(3, B // 2 + 1) as m:
                step((2 * m - 2, 0, m), (2 * m - 3, 1, m - 1), (2 * m - 4, 0, m - 1), (2 * m - 5, 1, m - 2))
                step((2 * m - 1, 1, m), (2 * m - 2, 0, m), (2 * m - 3, 1, m - 1), (2 * m - 4, 0, m - 1))
            for s in range(B, B + 3):
                step(at(s), at(s - 1), at(s - 2), at(s - 3))

        @block.sync
        def _(sp):
            xv = x.rearrange("b (t p) d -> p (b t) d", p=P)
            xs = x_all[:].rearrange("p (n d) -> p n d", d=D)
            sp.dma_start(xs[:, 0:2 * NT, :], xv[:, 0:2 * NT, :]).then_inc(x_first, 16)
            sp.dma_start(cT_sb[:], cT).then_inc(c_ld, 16)
            sp.dma_start(cst[:], consts).then_inc(c_ld, 16)
            sp.dma_start(wmod_sb[:], wmod).then_inc(c_ld, 16)
            sp.dma_start(wqkv[:], qkv_wT).then_inc(w_ld, 16)
            sp.dma_start(bqkv[:], qkv_b).then_inc(w_ld, 16)
            sp.dma_start(wo[:], out_wT).then_inc(w_ld, 16)
            sp.dma_start(bo[:], out_b).then_inc(w_ld, 16)
            sp.dma_start(w_in[:], w_inT).then_inc(w_ld, 16)
            sp.dma_start(innorm[:], in_norm).then_inc(w_ld, 16)
            sp.dma_start(wr[:], wrT).then_inc(w_ld, 16)
            sp.dma_start(ebias[:], e_bias.to_broadcast([P, E])).then_inc(w_ld, 16)
            sp.dma_start(place_sb[:], place).then_inc(w_ld, 16)
            sp.dma_start(onorm[:], out_norm).then_inc(w_ld, 16)
            sp.dma_start(wout[:], w_outT).then_inc(w_ld, 16)
            sp.dma_start(xs[:, 2 * NT:, :], xv[:, 2 * NT:, :]).then_inc(x_rest, 16)
            sp.dma_start(wgu[:], wguT).then_inc(moe_ld, 16)
            sp.dma_start(wd[:], wdT).then_inc(moe_ld, 16)
            sp.dma_start(enorm[:], e_norm.to_broadcast([P, E * D])).then_inc(moe_ld, 16)
            sp.wait_ge(fill_set, 1)
            sp.dma_start(fill[:, :, D:HW], filler.unsqueeze(2), allow_slow_non_contiguous=True).then_inc(fill_ld, 16)
            sp.wait_ge(fill_ld, 16)
            sp.dma_start(hbuf[E * REGION:HROWS, :].rearrange("(j p) w -> p j w", p=P),
                         fill[:, E:, :]).then_inc(fill_ld, 16)
            sp.wait_ge(fill_ld, 32)

            sp.wait_ge(scattered[0], 16 * NT * K * (B // 2))
            sp.wait_ge(scattered[1], 16 * NT * K * (B // 2))
            sp.wait_ge(tail_scat, 16 * E)
            sp.wait_ge(table_done, 1)

            def load_tile(t, s, n):
                row = sp.value_load(tile_row[0:1, bass.ds(t, 1)], min_val=0, max_val=HROWS - P)
                if again(n):
                    sp.wait_ge(y_scat[s], 16 * (n - 1))
                sp.dma_start(slots[:, s, :], hbuf[bass.ds(row, P), :]).then_inc(slot_ld[s], 16)

            for s in range(4):
                load_tile(s, s, 1)
            with sp.Fori(1, TILES // 4) as i:
                for s in range(4):
                    load_tile(4 * i + s, s, i + 1)

            for s in range(4):
                sp.wait_ge(y_scat[s], 16 * (TILES // 4))

            def load_rows(b, p, n):
                if again(n):
                    sp.wait_ge(mix_done, b - 1)
                sp.dma_start(yb[:, p], ybuf[bass.ds(b * (L * K), L * K), :].rearrange(
                    "(t p k) w -> p t (k w)", p=P, k=K)).then_inc(yb_ld[p], 16)

            def store(b, p, n):
                sp.wait_ge(ob_done, b + 1)
                sp.dma_start(out[bass.ds(b, 1), :, :].rearrange("o (t p) d -> p (o t) d", p=P),
                             ob[:, p]).then_inc(stored[p], 16)

            load_rows(0, 0, 1)
            load_rows(1, 1, 1)
            with sp.Fori(1, B // 2) as i:
                for p in range(2):
                    load_rows(2 * i + p, p, i + 1)
                    store(2 * i - 2 + p, p, i)
            for p in range(2):
                store(B - 2 + p, p, B // 2)
            for p in range(2):
                sp.wait_ge(stored[p], 16 * (B // 2))

        @block.gpsimd
        def _(pool):
            nc.gpsimd.memset(eps_ln[:], LN_EPS)
            nc.gpsimd.memset(eps_f[:], F_EPS)
            nc.gpsimd.memset(eps_rms[:], RMS_EPS).then_inc(eps_set, 1)
            nc.gpsimd.memset(fill[:], 0).then_inc(fill_set, 1)

            def alone():
                pool.wait_ge(eps_set, 1)

            def step(a, bb, _c, d):
                if d is not None:
                    done = d[0] + 1 if isinstance(d[0], int) else pool.snap(d[0] + 1)
                if bb is not None:
                    b, p, n = bb
                    if again(n):
                        pool.wait_ge(x1_ps, b - 1)
                    else:
                        pool.wait_ge(gate_done, B // 2)
                        pool.wait_ge(w_ld, 16 * 11)
                    nc.gpsimd.tensor_tensor(wo_ga[:, p, :], wo[:], gates_bc[:, bass.ds(b * 2 * D, D)],
                                            ALU.mult).then_inc(wo_done, 1)
                if d is not None:
                    b, p, n = d
                    alone()
                    pool.wait_ge(pos_done, done)
                    pool.wait_ge(rows_done, done)
                    pool.wait_ge(place_done, done)
                    for t in range(NT):
                        for k in range(K):
                            pool.indirect_dma_start(
                                hbuf, bass.IndirectOffsetOnAxis(ap=pos[:, p, t * K + k:t * K + k + 1], axis=0),
                                rows[:, p, t, k, :], None).then_inc(scattered[p], 16)
                if a is not None:
                    b, p, n = a
                    for t in range(NT):
                        pool.wait_ge(qkv_done[t], b + 1)
                        kvt = kv[:, p, t, :].rearrange("p (h e d) -> p h e d", e=HE, d=HD)
                        k_in = kvt[:, :, HD:HE, :].to_broadcast([P, H, HD, HD])
                        v_in = v[:, p, t, :].rearrange("p (h e) -> p h e", e=HD).unsqueeze(3)
                        nc.gpsimd.tensor_tensor(kvt[:, :, 0:HD, :], k_in, v_in.to_broadcast([P, H, HD, HD]),
                                                ALU.mult).then_inc(kv_done[t], 1)

            pipelined(pool, step)

            pool.wait_ge(wmax_done, 1)
            nc.gpsimd.partition_all_reduce(wmax_all[:], wmax[:], P, bass.bass_isa.ReduceOp.max).then_inc(wall_done, 1)
            pool.wait_ge(tail_done, 1)
            pool.wait_ge(fill_ld, 32)
            for e in range(E):
                pool.indirect_dma_start(hbuf, bass.IndirectOffsetOnAxis(ap=tail[:, e:e + 1], axis=0),
                                        fill[:, e, :], None).then_inc(tail_scat, 16)

            def send(s, n):
                alone()
                pool.wait_ge(y_done[s], n)
                pool.indirect_dma_start(ybuf, bass.IndirectOffsetOnAxis(ap=slots[:, s, D:HW], axis=0),
                                        yt[:, s, :], None).then_inc(y_scat[s], 16)

            with pool.Fori(1, TILES // 4 + 1) as n:
                for s in range(4):
                    send(s, n)

            def fold(b, p, n):
                if again(n):
                    pool.wait_ge(o_ps, b - 1)
                nc.gpsimd.tensor_tensor(wout_gb[:, p, :], woutn[:], gates_bc[:, bass.ds(b * 2 * D + D, D)],
                                        ALU.mult).then_inc(wgb_done, 1)

            pool.wait_ge(w_small, 2)
            for p in range(2):
                fold(p, p, 1)
            with pool.Fori(1, B // 2) as i:
                for p in range(2):
                    fold(2 * i + p, p, i + 1)

        @block.scalar
        def _(act):
            act.wait_ge(c_ld, 48)
            nc.scalar.activation(sc[:], cT_sb[:], ACT.Silu).then_inc(sc_done, 1)
            act.wait_ge(eps_set, 1)

            def step(a, bb, c, _d):
                if c is not None:
                    b, p, n = c
                    act.wait_ge(ln2_mv, b + 1)
                    nc.scalar.activation(sd2[:, p, :], mv2[:, p, :, 1], ACT.Sqrt,
                                         bias=eps_ln[:]).then_inc(ln2_sd, 1)
                if a is not None:
                    b, p, n = a
                    act.wait_ge(ln_mv, b + 1)
                    nc.scalar.activation(sd[:, p, :], mv[:, p, :, 1], ACT.Sqrt,
                                         bias=eps_ln[:]).then_inc(ln_sd, 1)
                if c is not None:
                    b, p, n = c
                    act.wait_ge(xn2T_ps, b + 1)
                    nc.scalar.activation(h2T[:, p, :], FFN[:, 0:L], ACT.Identity,
                                         bias=mod_cols[:, bass.ds(2 * B + b, 1)],
                                         scale=mod_cols[:, bass.ds(3 * B + b, 1)]).then_inc(h2T_done, 1)
                if a is not None:
                    b, p, n = a
                    if not again(n):
                        act.wait_ge(modcol_done, 1)
                    act.wait_ge(xnT_ps, b + 1)
                    nc.scalar.activation(hT[:, p, :], LNT[:, 0:L], ACT.Identity,
                                         bias=mod_cols[:, bass.ds(b, 1)],
                                         scale=mod_cols[:, bass.ds(B + b, 1)]).then_inc(hT_done, 1)
                    for t in range(NT):
                        act.wait_ge(qkv_ps[t], b + 1)
                        if again(n):
                            act.wait_ge(kv_done[t], b - 1)
                            for cc in range(3):
                                act.wait_ge(cum_used[NT - 1][cc], b - 1)
                        nc.scalar.activation(qk_raw[:, p, t, :], QKV[:, 0:2 * D], ACT.Relu).then_inc(raw_done[t], 1)
                        nc.scalar.activation(v[:, p, t, :], QKV[:, 2 * D:3 * D], ACT.Copy)
                        act.wait_ge(raw_done[t], b + 1)
                        nc.scalar.activation(q[:, p, t, :], qk_raw[:, p, t, 0:D], ACT.Identity, bias=eps_f[:])
                        nc.scalar.activation(
                            kv[:, p, t, :].rearrange("p (h e d) -> p h e d", e=HE, d=HD)[:, :, HD, :],
                            qk_raw[:, p, t, D:2 * D].rearrange("p (h d) -> p h d", d=HD), ACT.Identity,
                            bias=eps_f[:]).then_inc(qkv_done[t], 1)
                if c is not None:
                    b, p, n = c
                    act.wait_ge(u_ps, b + 1)
                    nc.scalar.activation(uT[:, p, :], FFN[:, 0:L], ACT.Copy).then_inc(uT_done, 1)
                    for t in range(NT):
                        last = nc.scalar.activation(junk[:], UB[:, t * D:(t + 1) * D], ACT.Square,
                                                    accum_out=ssq[:, p, t:t + 1])
                        last.then_inc(ssq_done, 1)
                        act.wait_ge(ssq_done, NT * b + t + 1)
                    nc.scalar.activation(rms[:, p, :], ssq[:, p, :], ACT.Sqrt, bias=eps_rms[:],
                                         scale=1.0 / D).then_inc(rms_done, 1)
                    act.wait_ge(rrs_done, b + 1)
                    if again(n):
                        act.wait_ge(scattered[p], 16 * NT * K * (n - 1))
                    for t in range(NT):
                        last = nc.scalar.activation(rows16[:, p, t, 0, 0:D], UB[:, t * D:(t + 1) * D], ACT.Copy,
                                                    scale=rrs[:, p, t:t + 1])
                    last.then_inc(hi_done, 1)
                if bb is not None:
                    b, p, n = bb
                    act.wait_ge(attnT_ps, b + 1)
                    nc.scalar.activation(attnT[:, p, :], PROJ[:, 0:L], ACT.Copy).then_inc(attnT_done, 1)

            pipelined(act, step)

            act.wait_ge(wscale_done, 2)
            nc.scalar.activation(w_hi[:], wgu[:], ACT.Copy, scale=wscale[:]).then_inc(whi_done, 1)
            act.wait_ge(gate_diff, 1)
            nc.scalar.activation(gate_all[:, :, 0], ldiff[:], ACT.Sigmoid)
            nc.scalar.activation(gate_all[:, :, 1], ldiff[:], ACT.Sigmoid, scale=-1.0).then_inc(gate_sig, 1)

            def gate(t, s, n):
                act.wait_ge(g_ps, t + 1)
                if s >= 2 or again(n):
                    act.wait_ge(gu_done, t - 1)
                nc.scalar.activation(sg[:, s % 2, :], bk[2 + s % 2][:], ACT.Silu, scale=descale[:]).then_inc(sg_done, 1)

            def square(t, s, n):
                act.wait_ge(y_ps, t + 1)
                if again(n):
                    act.wait_ge(y_scat[s], 16 * (n - 1))
                if not (s == 0 and not again(n)):
                    act.wait_ge(ysq_done, t)
                nc.scalar.activation(junk3[:], bk[6 + s % 2][:, 0:D], ACT.Square,
                                     accum_out=yt[:, s, D:YW]).then_inc(ysq_done, 1)

            gate(0, 0, 1)
            for s in range(1, 4):
                gate(s, s, 1)
                square(s - 1, s - 1, 1)
            with act.Fori(1, TILES // 4) as i:
                for s in range(4):
                    gate(4 * i + s, s, i + 1)
                    square(4 * i + s - 1, (s + 3) % 4, i + 1 if s else i)
            square(TILES - 1, 3, TILES // 4)

            def stage_d(b, p, n):
                act.wait_ge(yb_ld[p], 16 * n)
                nc.scalar.activation(rms4[:, p], yb[:, p].rearrange("p t (k w) -> p t k w", k=K)[:, :, :, D], ACT.Sqrt,
                                     bias=eps_rms[:], scale=1.0 / D).then_inc(rms4_done, 1)

            def stage_e(b, p, n):
                act.wait_ge(mix_done, b + 1)
                for t in range(NT):
                    nc.scalar.activation(junk[:], mix[:, p, t, :], ACT.Square,
                                         accum_out=ssq4[:, p, t:t + 1]).then_inc(ssq4_done, 1)
                    act.wait_ge(ssq4_done, NT * b + t + 1)
                nc.scalar.activation(rms5[:, p, :], ssq4[:, p, :], ACT.Sqrt, bias=eps_rms[:],
                                     scale=1.0 / D).then_inc(rms5_done, 1)
                act.wait_ge(mixT_ps, b + 1)
                nc.scalar.activation(mixT[:, p, :], bk[p][:, 0:L], ACT.Copy).then_inc(mixT_done, 1)

            stage_d(0, 0, 1)
            stage_d(1, 1, 1)
            stage_e(0, 0, 1)
            with act.Fori(1, B // 2) as i:
                stage_d(2 * i, 0, i + 1)
                stage_e(2 * i - 1, 1, i)
                stage_d(2 * i + 1, 1, i + 1)
                stage_e(2 * i, 0, i + 1)
            stage_e(B - 1, 1, B // 2)

        @block.vector
        def _(dve):
            dve.wait_ge(w_ld, 16 * 11)
            nc.vector.tensor_scalar(wrn[:], wr[:], innorm[:], None, ALU.mult).then_inc(w_small, 1)
            nc.vector.tensor_scalar(woutn[:], wout[:], onorm[:], None, ALU.mult).then_inc(w_small, 1)
            nc.vector.memset(count[:, 0, :], 0.0).then_inc(w_small, 1)
            dve.wait_ge(modcol_ps, 1)
            mc = mod_cols[:].rearrange("p (g k b) -> p g k b", g=2, k=2)
            mp = UB[:, 0:4 * B].rearrange("p (g k b) -> p g k b", g=2, k=2)
            nc.vector.tensor_copy(mc[:, :, 0, :], mp[:, :, 0, :])
            nc.vector.tensor_scalar(mc[:, :, 1, :], mp[:, :, 1, :], 1.0, None, ALU.add).then_inc(modcol_done, 1)

            def clamp_gates(i):
                dve.wait_ge(gate_ps, i + 1)
                g = CUM[i % 2][:]
                if i:
                    dve.wait_ge(gate_done, i)
                nc.vector.tensor_scalar(clamp_a, g, -1.0, 0.25, ALU.mult, ALU.max).then_inc(clamp_1, 1)
                nc.vector.tensor_scalar(clamp_s, g, 0.0, 2.0, ALU.is_ge, ALU.mult).then_inc(clamp_2, 1)
                dve.wait_ge(clamp_1, i + 1)
                nc.vector.tensor_tensor(clamp_a, clamp_a, g, ALU.max).then_inc(clamp_3, 1)
                dve.wait_ge(clamp_2, i + 1)
                dve.wait_ge(clamp_3, i + 1)
                nc.vector.scalar_tensor_tensor(gates_bc[:, i * 4 * D:(i + 1) * 4 * D], clamp_s, -1.0, clamp_a,
                                               ALU.add, ALU.mult).then_inc(gate_done, 1)

            for i in range(B // 2):
                clamp_gates(i)
            dve.wait_ge(gate_done, B // 2)
            nc.vector.tensor_tensor(
                gaob.rearrange("o (b d) -> o b d", d=D),
                gates_bc[0:1, :].rearrange("o (b g d) -> o b g d", g=2, d=D)[:, :, 0, :],
                bo[:].unsqueeze(1).to_broadcast([1, B, D]), ALU.mult).then_inc(gaob_done, 1)

            def alone():
                dve.wait_ge(w_small, 3)

            def norm_stats(b, st_, mv_, st_done, st_count, mv_done, p):
                for t in range(NT):
                    last = nc.vector.bn_stats(st_[:, p, t, :], x_all[:, bass.ds(b * L + t * P, P)])
                last.then_inc(st_done, 1)
                alone()
                dve.wait_ge(st_done, st_count)
                for t in range(NT):
                    last = nc.vector.bn_aggr(mv_[:, p, t, :], st_[:, p, t, :])
                last.then_inc(mv_done, 1)

            def norm_apply(b, mv_, sd_, rs_, xn_, sd_done, rs_done, done, p, n):
                dve.wait_ge(sd_done, b + 1)
                nc.vector.reciprocal(rs_[:, p, :], sd_[:, p, :]).then_inc(rs_done, 1)
                dve.wait_ge(rs_done, b + 1)
                for t in range(NT):
                    last = nc.vector.tensor_scalar(xn_[:, p, t, :], x_all[:, bass.ds(b * L + t * P, P)],
                                                   mv_[:, p, t, 0:1], rs_[:, p, t:t + 1], ALU.subtract, ALU.mult)
                last.then_inc(done, 1)

            def step(a, bb, c, _d):
                if c is not None:
                    b, p, n = c
                    alone()
                    dve.wait_ge(x1_done, b + 1)
                    norm_stats(b, st2, mv2, ln2_st, b + 1, ln2_mv, p)
                if a is not None:
                    b, p, n = a
                    if isinstance(b, int):
                        dve.wait_ge(x_first if b < 2 else x_rest, 16)
                    norm_stats(b, st, mv, ln_st[p], n, ln_mv, p)
                if c is not None:
                    b, p, n = c
                    norm_apply(b, mv2, sd2, rs2, xn2, ln2_sd, ln2_rs, xn2_done, p, n)
                if a is not None:
                    b, p, n = a
                    norm_apply(b, mv, sd, rs, xn, ln_sd, ln_rs, xn_done, p, n)
                if bb is not None:
                    b, p, n = bb
                    if again(n) or p == 1:
                        dve.wait_ge(nd_done, b)
                    for t in range(NT):
                        for cc, (h0, h1) in enumerate(HEADS):
                            nh = h1 - h0
                            dve.wait_ge(cum_ps[t][cc], b + 1)
                            qh = q[:, p, t, h0 * HD:h1 * HD].rearrange("p (h d) -> p h d", d=HD).unsqueeze(2)
                            nc.vector.tensor_tensor(
                                prod[:, t, h0 * HE * HD:h1 * HE * HD].rearrange("p (h e d) -> p h e d", e=HE, d=HD),
                                CUM[cc][:, 0:nh * HE * HD].rearrange("p (h e d) -> p h e d", e=HE, d=HD),
                                qh.to_broadcast([P, nh, HE, HD]), ALU.mult).then_inc(cum_used[t][cc], 1)
                    for cc in range(3):
                        dve.wait_ge(cum_used[NT - 1][cc], b + 1)
                    nc.vector.tensor_reduce(nd[:], prod[:].rearrange("p t (s d) -> p (t s) d", d=HD).rearrange(
                        "p (h e) d -> p h e d", e=HE), AX.X, ALU.add).then_inc(nd_done, 1)
                    dve.wait_ge(nd_done, b + 1)
                    nc.vector.tensor_scalar(den[:], nd[:, :, HD], F_EPS, None, ALU.max).then_inc(den_done, 1)
                    dve.wait_ge(den_done, b + 1)
                    nc.vector.reciprocal(rden[:], den[:]).then_inc(rden_done, 1)
                    dve.wait_ge(rden_done, b + 1)
                    nc.vector.tensor_tensor(attn[:, p].rearrange("p t (h e) -> p (t h) e", e=HD), nd[:, :, 0:HD],
                                            rden[:].unsqueeze(2).to_broadcast([P, NT * H, HD]),
                                            ALU.mult).then_inc(attn_done, 1)
                if c is not None:
                    b, p, n = c
                    dve.wait_ge(rms_done, b + 1)
                    nc.vector.reciprocal(rr[:, p, :], rms[:, p, :]).then_inc(rr_done, 1)
                    dve.wait_ge(rr_done, b + 1)
                    nc.vector.tensor_scalar(rrs[:, p, :], rr[:, p, :], HSCALE, None, ALU.mult).then_inc(rrs_done, 1)
                    dve.wait_ge(logit_ps, b + 1)
                    nc.vector.tensor_tensor(lr[:, p], FFN[:, 0:NT * E].rearrange("p (t e) -> p t e", e=E),
                                            rr[:, p, :].unsqueeze(2).to_broadcast([P, NT, E]),
                                            ALU.mult).then_inc(lr_done, 1)
                    dve.wait_ge(lr_done, b + 1)
                    nc.vector.tensor_tensor(score[:, p], lr[:, p], ebias[:].unsqueeze(1).to_broadcast([P, NT, E]),
                                            ALU.add).then_inc(score_done, 1)
                    alone()
                    dve.wait_ge(score_done, b + 1)
                    for t in range(NT):
                        last = nc.vector.max(m8[:, p, t, :], score[:, p, t, :])
                    last.then_inc(max_done, 1)
                    alone()
                    dve.wait_ge(max_done, b + 1)
                    for t in range(NT):
                        last = nc.vector.max_index(i8[:, p, t, :], m8[:, p, t, :], score[:, p, t, :])
                    last.then_inc(idx_done, 1)
                    dve.wait_ge(idx_done, b + 1)
                    nc.vector.tensor_copy(i8f[:, p], i8[:, p, :, 0:K]).then_inc(idxf_done, 1)
                    dve.wait_ge(idxf_done, b + 1)
                    iota = cst[:, C_IOTA:C_IOTA + E].unsqueeze(1).unsqueeze(1).to_broadcast([P, NT, K, E])
                    nc.vector.tensor_tensor(oh[:, p], iota, i8f[:, p].unsqueeze(3).to_broadcast([P, NT, K, E]),
                                            ALU.is_equal).then_inc(oh_done, 1)
                    dve.wait_ge(oh_done, b + 1)
                    nc.vector.tensor_tensor(chosen[:, p], oh[:, p, :, 0, :], oh[:, p, :, 1, :],
                                            ALU.add).then_inc(chosen_done, 1)
                    nc.vector.tensor_tensor(ohl[:, p], oh[:, p], lr[:, p].unsqueeze(2).to_broadcast([P, NT, K, E]),
                                            ALU.mult).then_inc(ohl_done, 1)
                    dve.wait_ge(chosen_done, b + 1)
                    nc.vector.tensor_tensor(chosen2[:, p], chosen[:, p, 0, :], chosen[:, p, 1, :],
                                            ALU.add).then_inc(chosen2_done, 1)
                    dve.wait_ge(ohl_done, b + 1)
                    nc.vector.tensor_reduce(lsel_all[:, bass.ds(b * NT * K, NT * K)],
                                            ohl[:, p].rearrange("p t k e -> p (t k) e"), AX.X,
                                            ALU.add).then_inc(lsel_done, 1)
                    dve.wait_ge(hi_done, b + 1)
                    for t in range(NT):
                        last = nc.vector.scalar_tensor_tensor(
                            rows16[:, p, t, 0, D:2 * D], UB[:, t * D:(t + 1) * D], rrs[:, p, t:t + 1],
                            rows16[:, p, t, 0, 0:D], ALU.mult, ALU.subtract)
                    last.then_inc(lo_done, 1)
                    nc.vector.tensor_copy(rows[:, p, :, :, D:HW].rearrange("p t k o -> p (t k) o"),
                                          place_sb[:, bass.ds(b * NT * K, NT * K)].unsqueeze(2)).then_inc(place_done, 1)
                    dve.wait_ge(lo_done, b + 1)
                    nc.vector.tensor_copy(rows[:, p, :, 1, 0:D], rows[:, p, :, 0, 0:D]).then_inc(rows_done, 1)
                    dve.wait_ge(rank_ps, b + 1)
                    nc.vector.tensor_tensor(
                        slot[:, p], FFN[:, NT * E:2 * NT * E].rearrange("p (t e) -> p t e", e=E),
                        cst[:, C_REG:C_REG + E].unsqueeze(1).to_broadcast([P, NT, E]), ALU.add).then_inc(slot_done, 1)
                    dve.wait_ge(chosen2_done, b + 1)
                    nc.vector.tensor_tensor(count[:, 1 - p, :], count[:, p, :], chosen2[:, p],
                                            ALU.add).then_inc(count_done, 1)
                    dve.wait_ge(slot_done, b + 1)
                    nc.vector.tensor_tensor(ohs[:, p], oh[:, p], slot[:, p].unsqueeze(2).to_broadcast([P, NT, K, E]),
                                            ALU.mult).then_inc(ohs_done, 1)
                    dve.wait_ge(ohs_done, b + 1)
                    nc.vector.tensor_reduce(posf[:, p], ohs[:, p], AX.X, ALU.add).then_inc(posf_done, 1)
                    dve.wait_ge(posf_done, b + 1)
                    if again(n):
                        dve.wait_ge(scattered[p], 16 * NT * K * (n - 1))
                    nc.vector.tensor_copy(pos[:, p, :], posf[:, p].rearrange("p t k -> p (t k)")).then_inc(pos_done, 1)
                if bb is not None:
                    b, p, n = bb
                    dve.wait_ge(x1_ps, b + 1)
                    xb = x_all[:, bass.ds(b * L, L)]
                    nc.vector.tensor_tensor(xb, PROJ[:, 0:L], xb, ALU.add).then_inc(x1_done, 1)

            pipelined(dve, step)

            chain = [0]

            def then(ins):
                chain[0] += 1
                ins.then_inc(ph2, 1)
                dve.wait_ge(ph2, chain[0])

            dve.wait_ge(total_ps, 1)
            then(nc.vector.tensor_copy(total[:], bk[0][:, 0:E]))
            then(nc.vector.tensor_tensor(tail_f[:], total[:], cst[:, C_TAIL:C_TAIL + E], ALU.add))
            nc.vector.tensor_copy(tail[:], tail_f[:]).then_inc(tail_done, 1)
            nj = TOK // P
            then(nc.vector.tensor_tensor(tcmp, total[0:1, :].unsqueeze(2).to_broadcast([1, E, nj]),
                                         cst[0:1, C_J:C_J + nj].unsqueeze(1).to_broadcast([1, E, nj]), ALU.is_gt))
            then(nc.vector.tensor_reduce(ntile[:], tcmp, AX.X, ALU.add))
            then(nc.vector.tensor_tensor(tlow[:], cst[0:1, C_LOW:C_LOW + E * E].rearrange("o (a b) -> o a b", b=E),
                                         ntile[:].unsqueeze(1).to_broadcast([1, E, E]), ALU.mult))
            then(nc.vector.tensor_reduce(tstart[:], tlow[:], AX.X, ALU.add))
            then(nc.vector.tensor_tensor(tend[:], tstart[:], ntile[:], ALU.add))
            tt = cst[0:1, C_T:C_T + TILES]
            then(nc.vector.tensor_tensor(tge, tt.unsqueeze(2).to_broadcast([1, TILES, E]),
                                         tend[:].unsqueeze(1).to_broadcast([1, TILES, E]), ALU.is_ge))
            then(nc.vector.tensor_reduce(texp[:], tge, AX.X, ALU.add))
            then(nc.vector.tensor_tensor(tgn, tge, ntile[:].unsqueeze(1).to_broadcast([1, TILES, E]), ALU.mult))
            then(nc.vector.tensor_reduce(tfirst[:], tgn, AX.X, ALU.add))
            then(nc.vector.tensor_tensor(trel[:], tt, tfirst[:], ALU.subtract))
            then(nc.vector.tensor_scalar(trel[:], trel[:], float(P), None, ALU.mult))
            then(nc.vector.scalar_tensor_tensor(trow_f[:], texp[:], float(REGION), trel[:], ALU.mult, ALU.add))
            then(nc.vector.tensor_copy(tile_row[:], trow_f[:]))
            then(nc.vector.tensor_scalar(texp[:], texp[:], float(E - 1), None, ALU.min))
            nc.vector.tensor_copy(tile_expert[:], texp[:]).then_inc(table_done, 1)
            lv = lsel_all[:].rearrange("p (n k) -> p n k", k=K)
            nc.vector.tensor_tensor(ldiff[:], lv[:, :, 0], lv[:, :, 1], ALU.subtract).then_inc(gate_diff, 1)
            dve.wait_ge(moe_ld, 48)
            nc.vector.tensor_copy(ident16[:], ident)
            then(nc.vector.tensor_scalar(wgu[:], wgu[:], innorm[:], None, ALU.mult))
            nc.vector.tensor_reduce(wmax[:], wgu[:], AX.X, ALU.max, apply_absolute_value=True).then_inc(wmax_done, 1)
            dve.wait_ge(wall_done, 1)
            then(nc.vector.tensor_scalar(wmax_all[:], wmax_all[:], 1e-30, None, ALU.max))
            then(nc.vector.tensor_scalar(wpow[:].bitcast(I32), wmax_all[:].bitcast(I32), 0x7F800000, None,
                                         ALU.bitwise_and))
            then(nc.vector.reciprocal(wscale[:], wpow[:]))
            nc.vector.tensor_scalar(descale[:], wpow[:], 2.0 ** -14 / HSCALE, None, ALU.mult).then_inc(wscale_done, 1)
            nc.vector.tensor_scalar(wscale[:], wscale[:], 2.0 ** 14, None, ALU.mult).then_inc(wscale_done, 1)
            dve.wait_ge(whi_done, 1)
            nc.vector.scalar_tensor_tensor(w_lo[:], wgu[:], wscale[:], w_hi[:], ALU.mult,
                                           ALU.subtract).then_inc(wlo_done, 1)

            def put_hT(t, s, n):
                dve.wait_ge(slotT_ps, t + 1)
                if s >= 2 or again(n):
                    dve.wait_ge(u3_ps, t - 1)
                nc.vector.tensor_copy(hT3[:, s % 2, :], bk[s % 2][:].bitcast(F16)[:, 0:2 * P]).then_inc(hT3_done, 1)

            def gated(t, s, n):
                dve.wait_ge(u3_ps, t + 1)
                dve.wait_ge(sg_done, t + 1)
                if s >= 2 or again(n):
                    dve.wait_ge(y_ps, t - 1)
                nc.vector.scalar_tensor_tensor(gu[:, s % 2, :], bk[4 + s % 2][:], descale[:], sg[:, s % 2, :],
                                               ALU.mult, ALU.mult).then_inc(gu_done, 1)

            def weigh(t, s, n):
                ex = dve.value_load(tile_expert[0:1, bass.ds(t, 1)], min_val=0, max_val=E - 1)
                dve.wait_ge(ysq_done, t + 1)
                if again(n):
                    dve.wait_ge(y_scat[s], 16 * (n - 1))
                nc.vector.tensor_tensor(yt[:, s, 0:D], bk[6 + s % 2][:, 0:D], enorm[:, bass.ds(ex * D, D)],
                                        ALU.mult).then_inc(y_done[s], 1)

            put_hT(0, 0, 1)
            put_hT(1, 1, 1)
            gated(0, 0, 1)
            for s in range(1, 4):
                put_hT(s + 1, (s + 1) % 4, 1 if s < 3 else 2)
                gated(s, s, 1)
                weigh(s - 1, s - 1, 1)
            with dve.Fori(1, TILES // 4 - 1) as i:
                for s in range(4):
                    put_hT(4 * i + s + 1, (s + 1) % 4, i + 1 if s < 3 else i + 2)
                    gated(4 * i + s, s, i + 1)
                    weigh(4 * i + s - 1, (s + 3) % 4, i + 1 if s else i)
            last_n = TILES // 4
            for s in range(4):
                if s < 3:
                    put_hT(TILES - 4 + s + 1, s + 1, last_n)
                gated(TILES - 4 + s, s, last_n)
                weigh(TILES - 4 + s - 1, (s + 3) % 4, last_n if s else last_n - 1)
            weigh(TILES - 1, 3, last_n)

            def stage_d(b, p, n):
                dve.wait_ge(rms4_done, b + 1)
                nc.vector.reciprocal(rinv4[:, p], rms4[:, p]).then_inc(rinv4_done, 1)
                dve.wait_ge(rinv4_done, b + 1)
                nc.vector.tensor_tensor(coef[:, p].rearrange("p t k -> p (t k)"),
                                        rinv4[:, p].rearrange("p t k -> p (t k)"),
                                        gate_all[:].rearrange("p n k -> p (n k)")[:, bass.ds(b * NT * K, NT * K)],
                                        ALU.mult).then_inc(coef_done, 1)
                dve.wait_ge(coef_done, b + 1)
                for t in range(NT):
                    last = nc.vector.tensor_scalar(half[:, p, t, :], yb[:, p, t, 0:D], coef[:, p, t, 0:1], None, ALU.mult)
                last.then_inc(half_done, 1)
                dve.wait_ge(half_done, b + 1)
                if again(n):
                    dve.wait_ge(mixT_ps, b - 1)
                    dve.wait_ge(ssq4_done, NT * (b - 1))
                for t in range(NT):
                    last = nc.vector.scalar_tensor_tensor(mix[:, p, t, :], yb[:, p, t, YW:YW + D], coef[:, p, t, 1:2],
                                                          half[:, p, t, :], ALU.mult, ALU.add)
                last.then_inc(mix_done, 1)

            def stage_e(b, p, n):
                dve.wait_ge(rms5_done, b + 1)
                nc.vector.reciprocal(rinv5[:, p, :], rms5[:, p, :]).then_inc(rinv5_done, 1)
                dve.wait_ge(rinv5_done, b + 1)
                dve.wait_ge(o_ps, b + 1)
                if again(n):
                    dve.wait_ge(stored[p], 16 * (n - 1))
                for t in range(NT):
                    last = nc.vector.scalar_tensor_tensor(
                        ob[:, p, t, :], bk[2 + p][:, t * D:(t + 1) * D], rinv5[:, p, t:t + 1],
                        x_all[:, bass.ds(b * L + t * P, P)], ALU.mult, ALU.add)
                last.then_inc(ob_done, 1)

            dve.wait_ge(gate_sig, 1)
            stage_d(0, 0, 1)
            stage_d(1, 1, 1)
            stage_e(0, 0, 1)
            with dve.Fori(1, B // 2) as i:
                stage_d(2 * i, 0, i + 1)
                stage_e(2 * i - 1, 1, i)
                stage_d(2 * i + 1, 1, i + 1)
                stage_e(2 * i, 0, i + 1)
            stage_e(B - 1, 1, B // 2)

        @block.tensor
        def _(pe):
            mm = nc.tensor.matmul
            pe.wait_ge(sc_done, 1)
            for j, part in enumerate((SA, CA, SB, CB)):
                last = mm(UB[:, j * B:(j + 1) * B], wmod_sb[:, part * D:(part + 1) * D], sc[:], start=True, stop=True)
            last.then_inc(modcol_ps, 1)
            wv = wmod_sb[:].rearrange("p (g k d) -> p g k d", g=2, k=3)[:, :, 2, :]
            for i in range(B // 2):
                if i >= 2:
                    pe.wait_ge(gate_done, i - 1)
                for j in range(2):
                    b = 2 * i + j
                    last = mm(CUM[i % 2][:, j * 2 * D:(j + 1) * 2 * D].rearrange("p (g d) -> p g d", g=2),
                              sc[:, b:b + 1].to_broadcast([P, P]), wv, start=True, stop=True)
                last.then_inc(gate_ps, 1)

            def step(a, bb, c, _d):
                if c is not None:
                    b, p, n = c
                    pe.wait_ge(xn2_done, b + 1)
                    if not (isinstance(n, int) and n == 1 and p == 0):
                        pe.wait_ge(slot_done, b)
                    for t in range(NT):
                        last = nc.tensor.transpose(FFN[:, t * P:(t + 1) * P], xn2[:, p, t, :], ident)
                    last.then_inc(xn2T_ps, 1)
                if a is not None:
                    b, p, n = a
                    pe.wait_ge(xn_done, b + 1)
                    if not (isinstance(n, int) and n == 1 and p == 0):
                        pe.wait_ge(hT_done, b)
                    for t in range(NT):
                        last = nc.tensor.transpose(LNT[:, t * P:(t + 1) * P], xn[:, p, t, :], ident)
                    last.then_inc(xnT_ps, 1)

                def running_state(t):
                    b, p, n = bb
                    for u in range(t + 1):
                        pe.wait_ge(kv_done[u], b + 1)
                    for cc, (h0, h1) in enumerate(HEADS):
                        if t:
                            pe.wait_ge(cum_used[t - 1][cc], b + 1)
                        elif p == 1 or again(n):
                            pe.wait_ge(cum_used[NT - 1][cc], b)
                        elif cc == 0:
                            pe.wait_ge(gate_done, B // 2)
                        lo, hi = h0 * HE * HD, h1 * HE * HD
                        o = CUM[cc][:, 0:hi - lo]
                        for u in range(t):
                            mm(o, ones, kv[:, p, u, lo:hi], start=(u == 0), stop=False)
                        mm(o, tri, kv[:, p, t, lo:hi], start=(t == 0), stop=True).then_inc(cum_ps[t][cc], 1)

                def project_qkv(t):
                    b, p, n = a
                    if t == 0:
                        pe.wait_ge(hT_done, b + 1)
                        if not again(n) and p == 0:
                            pe.wait_ge(w_ld, 16 * 11)
                        else:
                            pe.wait_ge(qkv_done[NT - 1], b)
                    else:
                        pe.wait_ge(qkv_done[t - 1], b + 1)
                    mm(QKV[:, 0:3 * D], ones[0:1, :], bqkv[:], start=True, stop=False)
                    mm(QKV[:, 0:3 * D], hT[:, p, t * P:(t + 1) * P], wqkv[:], start=False,
                       stop=True).then_inc(qkv_ps[t], 1)

                if bb is not None:
                    running_state(0)
                if a is not None:
                    project_qkv(0)
                if c is not None:
                    b, p, n = c
                    pe.wait_ge(h2T_done, b + 1)
                    if not (isinstance(n, int) and n == 1 and p == 0):
                        pe.wait_ge(lo_done, b)
                    else:
                        pe.wait_ge(modcol_done, 1)
                    for t in range(NT):
                        mm(UB[:, t * D:(t + 1) * D], h2T[:, p, t * P:(t + 1) * P], w_in[:], start=True, stop=True)
                    mm(FFN[:, 0:L], w_in[:], h2T[:, p, :], start=True, stop=True).then_inc(u_ps, 1)
                if bb is not None:
                    running_state(1)
                if a is not None:
                    project_qkv(1)
                if c is not None:
                    b, p, n = c
                    pe.wait_ge(uT_done, b + 1)
                    if not again(n):
                        pe.wait_ge(w_small, 3)
                    for t in range(NT):
                        last = mm(FFN[:, t * E:(t + 1) * E], uT[:, p, t * P:(t + 1) * P], wrn[:], start=True, stop=True)
                    last.then_inc(logit_ps, 1)
                if bb is not None:
                    b, p, n = bb
                    pe.wait_ge(attn_done, b + 1)
                    if p == 1 or again(n):
                        pe.wait_ge(x1_done, b)
                    for t in range(NT):
                        last = nc.tensor.transpose(PROJ[:, t * P:(t + 1) * P], attn[:, p, t, :], ident)
                    last.then_inc(attnT_ps, 1)
                if c is not None:
                    b, p, n = c
                    pe.wait_ge(lr_done, b + 1)
                    pe.wait_ge(chosen_done, b + 1)
                    if p == 1 or again(n):
                        pe.wait_ge(count_done, b)
                    for t in range(NT):
                        o = FFN[:, (NT + t) * E:(NT + t + 1) * E]
                        mm(o, strict, chosen[:, p, t, :], start=True, stop=False)
                        for u in range(t):
                            mm(o, ones, chosen[:, p, u, :], start=False, stop=False)
                        last = mm(o, ones, count[:, p, :], start=False, stop=True)
                    last.then_inc(rank_ps, 1)
                if bb is not None:
                    b, p, n = bb
                    pe.wait_ge(attnT_done, b + 1)
                    pe.wait_ge(wo_done, b + 1)
                    if not again(n):
                        pe.wait_ge(gaob_done, 1)
                    for t in range(NT):
                        o = PROJ[:, t * D:(t + 1) * D]
                        mm(o, ones[0:1, :], gaob[:, bass.ds(b * D, D)], start=True, stop=False)
                        last = mm(o, attnT[:, p, t * P:(t + 1) * P], wo_ga[:, p, :], start=False, stop=True)
                    last.then_inc(x1_ps, 1)

            pipelined(pe, step)

            pe.wait_ge(count_done, B)
            mm(bk[0][:, 0:E], ones, count[:, 0, :], start=True, stop=True).then_inc(total_ps, 1)

            def turn(t, s, n):
                pe.wait_ge(slot_ld[s], 16 * n)
                if s >= 2 or again(n):
                    pe.wait_ge(hT3_done, t - 1)
                o = bk[s % 2][:].bitcast(F16)
                for j in range(2):
                    last = nc.tensor.transpose(o[:, j * P:(j + 1) * P], slots16[:, s, j * D:(j + 1) * D], ident16[:])
                last.then_inc(slotT_ps, 1)

            def gate_up(t, s, n):
                ex = pe.value_load(tile_expert[0:1, bass.ds(t, 1)], min_val=0, max_val=E - 1)
                pe.wait_ge(hT3_done, t + 1)
                hi, lo = hT3[:, s % 2, 0:P], hT3[:, s % 2, P:2 * P]
                for part, banks, done in ((0, 2, g_ps), (1, 4, u3_ps)):
                    if s >= 2 or again(n):
                        pe.wait_ge((sg_done, gu_done)[part], t - 1)
                    for f in range(FC):
                        o = bk[banks + s % 2][:, f * P:(f + 1) * P]
                        w = bass.ds(ex * F + (part * E * F + f * P), P)
                        mm(o, w_hi[:, w], hi, start=True, stop=False)
                        mm(o, w_hi[:, w], lo, start=False, stop=False)
                        last = mm(o, w_lo[:, w], hi, start=False, stop=True)
                    last.then_inc(done, 1)

            def down(t, s, n):
                ex = pe.value_load(tile_expert[0:1, bass.ds(t, 1)], min_val=0, max_val=E - 1)
                pe.wait_ge(gu_done, t + 1)
                if s >= 2 or again(n):
                    pe.wait_ge(y_done[(s + 2) % 4], n if s >= 2 else n - 1)
                for f in range(FC):
                    last = mm(bk[6 + s % 2][:, 0:D], gu[:, s % 2, f * P:(f + 1) * P],
                              wd[:, bass.ds(ex * (FC * D) + f * D, D)], start=(f == 0), stop=(f == FC - 1))
                last.then_inc(y_ps, 1)

            pe.wait_ge(table_done, 1)
            pe.wait_ge(wlo_done, 1)
            turn(0, 0, 1)
            gate_up(0, 0, 1)
            turn(1, 1, 1)
            for s in range(1, 4):
                gate_up(s, s, 1)
                down(s - 1, s - 1, 1)
                turn(s + 1, (s + 1) % 4, 1 if s < 3 else 2)
            with pe.Fori(1, TILES // 4 - 1) as i:
                for s in range(4):
                    gate_up(4 * i + s, s, i + 1)
                    down(4 * i + s - 1, (s + 3) % 4, i + 1 if s else i)
                    turn(4 * i + s + 1, (s + 1) % 4, i + 1 if s < 3 else i + 2)
            last_n = TILES // 4
            for s in range(4):
                gate_up(TILES - 4 + s, s, last_n)
                down(TILES - 4 + s - 1, (s + 3) % 4, last_n if s else last_n - 1)
                if s < 3:
                    turn(TILES - 4 + s + 1, s + 1, last_n)
            down(TILES - 1, 3, last_n)

            def stage_d(b, p, n):
                pe.wait_ge(mix_done, b + 1)
                if again(n):
                    pe.wait_ge(mixT_done, b - 1)
                for t in range(NT):
                    last = nc.tensor.transpose(bk[p][:, t * P:(t + 1) * P], mix[:, p, t, :], ident)
                last.then_inc(mixT_ps, 1)

            def stage_e(b, p, n):
                pe.wait_ge(mixT_done, b + 1)
                pe.wait_ge(wgb_done, b + 1)
                if again(n):
                    pe.wait_ge(ob_done, b - 1)
                for t in range(NT):
                    last = mm(bk[2 + p][:, t * D:(t + 1) * D], mixT[:, p, t * P:(t + 1) * P], wout_gb[:, p, :],
                              start=True, stop=True)
                last.then_inc(o_ps, 1)

            stage_d(0, 0, 1)
            stage_d(1, 1, 1)
            stage_e(0, 0, 1)
            with pe.Fori(1, B // 2) as i:
                stage_d(2 * i, 0, i + 1)
                stage_e(2 * i - 1, 1, i)
                stage_d(2 * i + 1, 1, i + 1)
                stage_e(2 * i, 0, i + 1)
            stage_e(B - 1, 1, B // 2)


def kernel(L0_attn_x, L0_attn_qkv_w, L0_attn_qkv_b, L0_attn_out_w, L0_attn_out_b, L0_ffn_W_in, L0_ffn_in_norm_w,
           L0_ffn_Wr, L0_ffn_expert_bias, L0_ffn_Wg, L0_ffn_Wu, L0_ffn_Wd, L0_ffn_enorm_w, L0_ffn_out_norm_w,
           L0_ffn_W_out, L0_c, L0_wmod):
    import concourse.bacc as bacc
    from concourse.bass_utils import run_bass_kernel_spmd

    def arr(a):
        return np.ascontiguousarray(np.asarray(a))

    def gate_first(w):
        return np.asarray(w).transpose(2, 0, 1).reshape(D, E * F)

    consts, place, filler = shape_constants()
    arrays = {
        "x": arr(L0_attn_x),
        "cT": arr(np.asarray(L0_c).T),
        "wmod": arr(L0_wmod),
        "qkv_wT": arr(np.asarray(L0_attn_qkv_w).T),
        "qkv_b": arr(np.asarray(L0_attn_qkv_b).reshape(1, 3 * D)),
        "out_wT": arr(np.asarray(L0_attn_out_w).T),
        "out_b": arr(np.asarray(L0_attn_out_b).reshape(1, D)),
        "w_inT": arr(np.asarray(L0_ffn_W_in).T),
        "in_norm": arr(np.asarray(L0_ffn_in_norm_w).reshape(D, 1)),
        "wrT": arr(np.asarray(L0_ffn_Wr).T),
        "e_bias": arr(np.asarray(L0_ffn_expert_bias).reshape(1, E)),
        "wguT": arr(np.concatenate([gate_first(L0_ffn_Wg), gate_first(L0_ffn_Wu)], axis=1)),
        "wdT": arr(np.asarray(L0_ffn_Wd).reshape(E, D, FC, P).transpose(3, 0, 2, 1).reshape(P, E * FC * D)),
        "e_norm": arr(np.asarray(L0_ffn_enorm_w).reshape(1, E * D)),
        "out_norm": arr(np.asarray(L0_ffn_out_norm_w).reshape(D, 1)),
        "w_outT": arr(np.asarray(L0_ffn_W_out).T),
        "consts": consts, "place": place, "filler": filler,
    }
    nc = bacc.Bacc("TRN2", target_bir_lowering=False, num_devices=1)
    args = {n: nc.dram_tensor(n, a.shape, mybir.dt.from_np(a.dtype), kind="ExternalInput").ap()
            for n, a in arrays.items()}
    out = nc.dram_tensor("out", (B, L, D), F32, kind="ExternalOutput").ap()
    block_kernel(nc, **args, out=out)
    r = run_bass_kernel_spmd(nc, [arrays], core_ids=[0])
    return r.results[0]["out"]
```

```python
from contextlib import ExitStack

import numpy as np

import concourse.bass as bass
from concourse import mybir

F32 = mybir.dt.float32
F16 = mybir.dt.float16
BF16 = mybir.dt.bfloat16
I32 = mybir.dt.int32
U32 = mybir.dt.uint32
ALU = mybir.AluOpType
ACT = mybir.ActivationFunctionType
AX = mybir.AxisListType

P = 128
B, L, D = 16, 256, 128
H, HD = 16, 8
NT = L // P
TOK = B * L
E, F, K = 8, 512, 2
FC = F // P
HE = HD + 1
STATE = HE * D
THIRD = HE // 3
R = 256
RB = R // P
REGION = TOK + R
TURN = 4
TILES = 40
SPARE = TILES - TOK * K // R
HROWS = E * REGION + SPARE * R
YROWS = TOK * K + (E + SPARE) * R
HW = D + 1
YW = D + 1
LN_EPS = 1e-5
F_EPS = 1e-6
RMS_EPS = float(np.finfo(np.float32).eps)
HSCALE = 2.0 ** 11
SA, CA, GA, SB, CB, GB = range(6)

C_ID, C_TRI, C_ONES, C_STRICT = 0, P, 2 * P, 3 * P
C_REG, C_IOTA = 4 * P, 4 * P + E
C_J = 4 * P + 2 * E
C_LOW = C_J + TOK // R
C_T = C_LOW + E * E
C_BLK = C_T + TILES
C_END = C_BLK + H


def shape_constants():
    c = np.zeros((P, C_END), np.float32)
    p = np.arange(P)
    c[:, C_ID:C_ID + P] = np.eye(P)
    c[:, C_TRI:C_TRI + P] = p[:, None] <= p[None, :]
    c[:, C_ONES:C_ONES + P] = 1
    c[:, C_STRICT:C_STRICT + P] = p[:, None] < p[None, :]
    c[:, C_REG:C_REG + E] = np.arange(E) * REGION
    c[:, C_IOTA:C_IOTA + E] = np.arange(E)
    c[:, C_J:C_J + TOK // R] = np.arange(TOK // R) * R
    c[:, C_LOW:C_LOW + E * E] = (np.arange(E)[:, None] > np.arange(E)[None, :]).ravel()
    c[:, C_T:C_T + TILES] = np.arange(TILES)
    c[:, C_BLK:C_BLK + H] = p[:, None] // HD == np.arange(H)[None, :]
    token = np.arange(TOK // P)[None, :, None] * P + p[:, None, None]
    place = (token * K + np.arange(K)).reshape(P, -1).astype(np.uint32)
    filler = np.zeros(((E + SPARE) * R, HW), np.uint32)
    filler[:, D] = TOK * K + np.arange((E + SPARE) * R)
    return c, place, filler


def block_kernel(nc, x, cT, wmod, qkv_wT, qkv_b, out_wT, out_b, w_inT, in_norm, wrT, e_bias, wguT, wdT,
                 e_norm, out_norm, w_outT, consts, place, filler, out):
    ctx = ExitStack()
    with ctx:
        def sb(name, shape, dt=F32):
            return ctx.enter_context(nc.sbuf_tensor(name, shape, dt))

        def sem(name):
            return ctx.enter_context(nc.semaphore(name))

        def two(name):
            return [sem(f"{name}{i}") for i in range(2)]

        def four(name):
            return [sem(f"{name}{i}") for i in range(4)]

        hbuf = nc.dram_tensor("dispatched", [HROWS, HW], U32, kind="Internal").ap()
        gbuf = nc.dram_tensor("gate_rows", [1, B * 2 * D], F32, kind="Internal").ap()
        ybuf = nc.dram_tensor("expert_rows", [YROWS, YW], F32, kind="Internal").ap()

        x_all = sb("x_all", [P, B * L])
        cst = sb("cst", [P, C_END])
        place_sb = sb("place_sb", [P, B * NT * K], U32)
        ident, tri, ones, strict = (cst[:, c:c + P] for c in (C_ID, C_TRI, C_ONES, C_STRICT))
        blk = cst[:, C_BLK:C_BLK + H]
        cT_sb = sb("cT_sb", [P, B])
        sc = sb("sc", [P, B])
        wmod_sb = sb("wmod_sb", [P, 6 * D])
        wqkv = sb("wqkv", [P, 3 * D])
        bkv = sb("bkv", [3, 2 * D])
        bkv_part = sb("bkv_part", [3, 3, 2 * D], BF16)
        bkv3 = sb("bkv3", [3, 2 * D], BF16)
        bq = sb("bq", [P, 1])
        wo = sb("wo", [P, D])
        bo = sb("bo", [P, D])
        bo_ga = sb("bo_ga", [P, 2, D])
        w_in = sb("w_in", [P, D])
        innorm = sb("innorm", [P, 1])
        wr = sb("wr", [P, E])
        wrn = sb("wrn", [P, E])
        ebias = sb("ebias", [P, E])
        wgu = sb("wgu", [P, 2 * E * F])
        w_hi = sb("w_hi", [P, 2 * E * F], F16)
        w_lo = sb("w_lo", [P, 2 * E * F], F16)
        wd = sb("wd", [P, E * FC * D])
        enorm = sb("enorm", [P, E * D])
        onorm = sb("onorm", [P, 1])
        wout = sb("wout", [P, D])
        woutn = sb("woutn", [P, D])
        mod_cols = sb("mod_cols", [P, 4 * B])
        gates_bc = sb("gates_bc", [P, B * 2 * D])
        eps_ln = sb("eps_ln", [P, 1])
        eps_f = sb("eps_f", [P, 1])
        eps_rms = sb("eps_rms", [P, 1])
        lsel_all = sb("lsel_all", [P, B * NT * K])
        ldiff = sb("ldiff", [P, B * NT])
        gate_all = sb("gate_all", [P, B * NT, K])

        gate_row, clamp_a, clamp_s = (sb(n, [B, 2 * D]) for n in ("gate_row", "clamp_a", "clamp_s"))

        st = sb("st", [P, 2, NT, 6])
        mv = sb("mv", [P, 2, NT, 2])
        sd = sb("sd", [P, 2, NT])
        rs = sb("rs", [P, 2, NT])
        nmr = sb("nmr", [P, 2, NT])
        xn = sb("xn", [P, 2, NT, D])
        hT = sb("hT", [P, 2, L])
        q_raw = sb("q_raw", [P, L])
        k_raw = sb("k_raw", [P, NT, D])
        qT = sb("qT", [P, 2, L])
        v = sb("v", [P, 2, NT, D])
        kv = sb("kv", [P, 2, NT, STATE])
        prod = sb("prod", [P, NT, STATE])
        s0blk = sb("s0blk", [P, HE, H])
        den = sb("den", [P, NT, H])
        rden = sb("rden", [P, NT, H])
        attn = sb("attn", [P, 2, NT, D])
        attnT = sb("attnT", [P, 2, L])
        wo_ga = sb("wo_ga", [P, 2, D])
        st2 = sb("st2", [P, 2, NT, 6])
        mv2 = sb("mv2", [P, 2, NT, 2])
        sd2 = sb("sd2", [P, 2, NT])
        rs2 = sb("rs2", [P, 2, NT])
        nmr2 = sb("nmr2", [P, 2, NT])
        xn2 = sb("xn2", [P, 2, NT, D])
        h2T = sb("h2T", [P, 2, L])
        junk = sb("junk", [P, D])
        ssq = sb("ssq", [P, 2, NT])
        rms = sb("rms", [P, 2, NT])
        rr = sb("rr", [P, 2, NT])
        rrs = sb("rrs", [P, 2, NT])
        uT = sb("uT", [P, 2, L])
        rows = sb("rows", [P, 2, NT, K, HW], U32)
        rows16 = rows[:].bitcast(F16)
        lr = sb("lr", [P, 2, NT, E])
        score = sb("score", [P, 2, NT, E])
        m8 = sb("m8", [P, 2, NT, 8])
        i8 = sb("i8", [P, 2, NT, 8], U32)
        i8f = sb("i8f", [P, 2, NT, K])
        oh = sb("oh", [P, 2, NT, K, E])
        ohl = sb("ohl", [P, 2, NT, K, E])
        chosen = sb("chosen", [P, 2, NT, E], BF16)
        chosen2 = sb("chosen2", [P, 2, E], BF16)
        count = sb("count", [P, 2, E], BF16)
        ones16 = sb("ones16", [P, P], BF16)
        strict16 = sb("strict16", [P, P], BF16)
        slot = sb("slot", [P, 2, NT, E])
        ohs = sb("ohs", [P, 2, NT, K, E])
        posf = sb("posf", [P, 2, NT, K])
        pos = sb("pos", [P, 2, NT * K], U32)

        spare = prod[0:1].rearrange("o t s -> o (t s)")
        tcmp, tge, tgn = (spare[:, a:a + n * m].rearrange("o (n m) -> o n m", m=m) for a, n, m in (
            (0, E, TOK // R), (E * TOK // R, TILES, E), (E * TOK // R + TILES * E, TILES, E)))
        wmax = sb("wmax", [P, 1])
        wmax_all = sb("wmax_all", [P, 1])
        wpow = sb("wpow", [P, 1])
        wscale = sb("wscale", [P, 1])
        descale = sb("descale", [P, 1])
        total = sb("total", [P, E])
        tail_f = sb("tail_f", [1, E])
        tail = sb("tail", [1, E], I32)
        ntile = sb("ntile", [1, E])
        tlow = sb("tlow", [1, E, E])
        tstart = sb("tstart", [1, E])
        tend = sb("tend", [1, E])
        texp = sb("texp", [1, TILES])
        tfirst = sb("tfirst", [1, TILES])
        trel = sb("trel", [1, TILES])
        trow_f = sb("trow_f", [1, TILES])
        tile_row = sb("tile_row", [1, TILES], I32)
        tile_expert = sb("tile_expert", [1, TILES], I32)

        slots = sb("slots", [P, 4, RB, HW], U32)
        slots16 = slots[:].bitcast(F16)
        ident16 = sb("ident16", [P, P], F16)
        hT3 = sb("hT3", [P, 2, 2 * R], F16)
        sg, gu = (kv[:, i].rearrange("p t s -> p (t s)")[:, 0:2 * F].rearrange("p (j f) -> p j f", f=F)
                  for i in range(2))
        to_place = sb("to_place", [P, TURN, RB], U32)
        yt = sb("yt", [P, 2, RB, YW])
        junk3 = sb("junk3", [P, D])

        rms4 = sb("rms4", [P, 2, NT, K])
        rinv4 = sb("rinv4", [P, 2, NT, K])
        coef = sb("coef", [P, 2, NT, K])
        ssq4 = sb("ssq4", [P, 2, NT])
        rms5 = sb("rms5", [P, 2, NT])
        rinv5 = sb("rinv5", [P, 2, NT])
        wout_gb = sb("wout_gb", [P, 2, D])
        half, mix, mixT, ob = (wgu[:, i * 2 * L:(i + 1) * 2 * L].rearrange("p (j t d) -> p j t d", j=2, t=NT)
                               for i in range(4))
        mixT = mixT.rearrange("p j t d -> p j (t d)")
        yb = wgu[:, 8 * L:8 * L + 2 * NT * K * YW].rearrange("p (j t w) -> p j t w", j=2, t=NT)

        bk = [ctx.enter_context(nc.psum_tensor(f"bank{i}", [P, 512], F32)) for i in range(8)]
        T, G, U, Y = bk[0:2], [b[:] for b in bk[2:4]], [b[:] for b in bk[4:6]], [b[:] for b in bk[6:8]]
        CUM = bk[0:3]
        TB, KV, ND, FFN, UB = bk[3:8]

        LOGITS = ND[:, NT * HE * H:NT * HE * H + NT * E]
        RANK = FFN[:, 0:NT * E]

        x_first, x_rest, c_ld, w_ld, moe_ld, filled = (
            sem(n) for n in ("x_first", "x_rest", "c_ld", "w_ld", "moe_ld", "filled"))
        eps_set = sem("eps_set")
        sc_done, modcol_ps, modcol_done = sem("sc_done"), sem("modcol_ps"), sem("modcol_done")
        gate_ps, clamp_1, clamp_2, clamp_3, gate_done, gates_out, gates_in = (
            sem(n) for n in ("gate_ps", "clamp_1", "clamp_2", "clamp_3", "gate_done", "gates_out", "gates_in"))
        bias_part = sem("bias_part")
        bo_done, xb_done = sem("bo_done"), sem("xb_done")
        w_small = sem("w_small")
        ln_mv, ln_sd, ln_rs, ln_nm, xn_done = (sem(n) for n in ("ln_mv", "ln_sd", "ln_rs", "ln_nm", "xn_done"))
        turn_ps, hT_done = sem("turn_ps"), sem("hT_done")
        kv_ps, q_ps, q_raw_done, k_raw_done, q_done, k_done = (
            sem(n) for n in ("kv_ps", "q_ps", "q_raw_done", "k_raw_done", "q_done", "k_done"))
        kv_done = [sem(f"kv_done_{t}") for t in range(NT)]
        cum_ps = [[sem(f"cum_ps_{t}_{c}") for c in range(3)] for t in range(NT)]
        cum_used = [[sem(f"cum_used_{t}_{c}") for c in range(3)] for t in range(NT)]
        nd_ps, den_done, rden_done, attn_done = (sem(n) for n in ("nd_ps", "den_done", "rden_done", "attn_done"))
        attnT_ps, attnT_done, wo_done, x1_ps, x1_done = (
            sem(n) for n in ("attnT_ps", "attnT_done", "wo_done", "x1_ps", "x1_done"))
        ln2_mv, ln2_sd, ln2_rs, ln2_nm, xn2_done = (
            sem(n) for n in ("ln2_mv", "ln2_sd", "ln2_rs", "ln2_nm", "xn2_done"))
        h2T_done, u_ps, uT_done, ssq_done, rms_done, rr_done, rrs_done = (
            sem(n) for n in ("h2T_done", "u_ps", "uT_done", "ssq_done", "rms_done", "rr_done", "rrs_done"))
        hi_done, lo_done, rows_done = (sem(n) for n in ("hi_done", "lo_done", "rows_done"))
        ln_st, ln2_st = two("ln_st"), sem("ln2_st")
        scattered, yb_ld, stored = two("scattered"), two("yb_ld"), two("stored")
        logit_ps, lr_done, score_done, max_done, idx_done, idxf_done, oh_done = (
            sem(n) for n in ("logit_ps", "lr_done", "score_done", "max_done", "idx_done", "idxf_done", "oh_done"))
        chosen_done, chosen2_done, count_done, ohl_done, lsel_done = (
            sem(n) for n in ("chosen_done", "chosen2_done", "count_done", "ohl_done", "lsel_done"))
        rank_ps, slot_done, ohs_done, posf_done, pos_done = (
            sem(n) for n in ("rank_ps", "slot_done", "ohs_done", "posf_done", "pos_done"))
        ph2, total_ps, tail_done, table_done, wmax_done, wall_done, wscale_done, whi_done, wlo_done = (
            sem(n) for n in ("ph2", "total_ps", "tail_done", "table_done", "wmax_done", "wall_done",
                             "wscale_done", "whi_done", "wlo_done"))
        gate_diff, gate_sig = sem("gate_diff"), sem("gate_sig")
        slot_ld, y_scat, y_done = four("slot_ld"), two("y_scat"), four("y_done")
        slotT_ps, hT3_done, g_ps, u3_ps, sg_done, gu_done, y_ps, ysq_done = (
            sem(n) for n in ("slotT_ps", "hT3_done", "g_ps", "u3_ps", "sg_done", "gu_done", "y_ps", "ysq_done"))
        rms4_done, rinv4_done, coef_done, half_done, mix_done, mixT_ps, mixT_done = (
            sem(n) for n in ("rms4_done", "rinv4_done", "coef_done", "half_done", "mix_done", "mixT_ps",
                             "mixT_done"))
        ssq4_done, rms5_done, rinv5_done, wgb_done, o_ps, ob_done = (
            sem(n) for n in ("ssq4_done", "rms5_done", "rinv5_done", "wgb_done", "o_ps", "ob_done"))

        block = ctx.enter_context(nc.Block())

        def again(n):
            return not (isinstance(n, int) and n <= 1)

        def again_turn(i):
            return not (isinstance(i, int) and i == 0)

        def pipelined(eng, step):
            def at(s):
                return (s, s % 2, s // 2 + 1) if 0 <= s < B else None
            stages = range(6)
            for s in range(8):
                step(*(at(s - g) for g in stages))
            with eng.Fori(5, B // 2 + 1) as m:
                for r in range(2):
                    step(*((2 * m - 2 + r - g, (r - g) % 2, m + (r - g) // 2) for g in stages))
            for s in range(B, B + 5):
                step(*(at(s - g) for g in stages))

        @block.sync
        def _(sp):
            xv = x.rearrange("b (t p) d -> p (b t) d", p=P)
            xs = x_all[:].rearrange("p (n d) -> p n d", d=D)
            sp.dma_start(xs[:, 0:2 * NT, :], xv[:, 0:2 * NT, :]).then_inc(x_first, 16)
            sp.dma_start(cT_sb[:], cT).then_inc(c_ld, 16)
            sp.dma_start(cst[:], consts).then_inc(c_ld, 16)
            sp.dma_start(wmod_sb[:], wmod).then_inc(c_ld, 16)
            sp.dma_start(wqkv[:], qkv_wT).then_inc(w_ld, 16)
            sp.dma_start(bkv[:], qkv_b[:, D:3 * D].to_broadcast([3, 2 * D])).then_inc(w_ld, 16)
            sp.dma_start(bq[:], qkv_b[:, 0:D].rearrange("o d -> d o"), allow_slow_non_contiguous=True).then_inc(w_ld, 16)
            sp.dma_start(wo[:], out_wT).then_inc(w_ld, 16)
            sp.dma_start(bo[:], out_b.to_broadcast([P, D])).then_inc(w_ld, 16)
            sp.dma_start(w_in[:], w_inT).then_inc(w_ld, 16)
            sp.dma_start(innorm[:], in_norm).then_inc(w_ld, 16)
            sp.dma_start(wr[:], wrT).then_inc(w_ld, 16)
            sp.dma_start(ebias[:], e_bias.to_broadcast([P, E])).then_inc(w_ld, 16)
            sp.dma_start(place_sb[:], place).then_inc(w_ld, 16)
            sp.dma_start(onorm[:], out_norm).then_inc(w_ld, 16)
            sp.dma_start(wout[:], w_outT).then_inc(w_ld, 16)
            sp.dma_start(xs[:, 2 * NT:, :], xv[:, 2 * NT:, :]).then_inc(x_rest, 16)
            sp.wait_ge(gate_done, 1)
            sp.dma_start(gbuf.rearrange("o (b g) -> (o b) g", b=B), gate_row[:]).then_inc(gates_out, 16)
            sp.wait_ge(gates_out, 16)
            sp.dma_start(gates_bc[:], gbuf.to_broadcast([P, B * 2 * D])).then_inc(gates_in, 16)
            sp.dma_start(wgu[:], wguT).then_inc(moe_ld, 16)
            sp.dma_start(wd[:], wdT).then_inc(moe_ld, 16)
            sp.dma_start(enorm[:], e_norm.to_broadcast([P, E * D])).then_inc(moe_ld, 16)
            sp.dma_start(hbuf[E * REGION:HROWS, :], filler[E * R:, :]).then_inc(filled, 16)

            sp.wait_ge(tail_done, 1)
            tail_regs = [sp.alloc_register(f"tail{e}") for e in range(E)]
            sp.load(tail_regs, tail[0:1, :])
            for e in range(E):
                row = sp.snap(tail_regs[e], min_val=0, max_val=E * REGION - R)
                sp.dma_start(hbuf[bass.ds(row, R), :], filler[e * R:(e + 1) * R, :]).then_inc(filled, 16)

            sp.wait_ge(scattered[0], 16 * NT * K * (B // 2))
            sp.wait_ge(scattered[1], 16 * NT * K * (B // 2))
            sp.wait_ge(filled, 16 * (E + 1))
            sp.wait_ge(table_done, 1)
            row_regs = [sp.alloc_register(f"tile_row{s}") for s in range(TURN)]

            def load_tiles(i):
                sp.load(row_regs, tile_row[0:1, bass.ds(TURN * i, TURN)])
                for s in range(TURN):
                    row = sp.snap(row_regs[s], min_val=0, max_val=HROWS - R)
                    if again_turn(i):
                        sp.wait_ge(hT3_done, TURN * i + s - 3)
                    sp.dma_start(slots[:, s], hbuf[bass.ds(row, R), :].rearrange("(p j) w -> p j w", j=RB)).then_inc(
                        slot_ld[s], 16)

            load_tiles(0)
            with sp.Fori(1, TILES // TURN) as i:
                load_tiles(i)

            for p in range(2):
                sp.wait_ge(y_scat[p], 16 * RB * (TILES // 2))

            def load_rows(b, p, n):
                if again(n):
                    sp.wait_ge(mix_done, b - 1)
                sp.dma_start(yb[:, p], ybuf[bass.ds(b * (L * K), L * K), :].rearrange(
                    "(t p k) w -> p t (k w)", p=P, k=K)).then_inc(yb_ld[p], 16)

            def store(b, p, n):
                sp.wait_ge(ob_done, b + 1)
                sp.dma_start(out[bass.ds(b, 1), :, :].rearrange("o (t p) d -> p (o t) d", p=P),
                             ob[:, p]).then_inc(stored[p], 16)

            load_rows(0, 0, 1)
            load_rows(1, 1, 1)
            with sp.Fori(1, B // 2) as i:
                for p in range(2):
                    load_rows(2 * i + p, p, i + 1)
                    store(2 * i - 2 + p, p, i)
            for p in range(2):
                store(B - 2 + p, p, B // 2)
            for p in range(2):
                sp.wait_ge(stored[p], 16 * (B // 2))

        @block.gpsimd
        def _(pool):
            nc.gpsimd.memset(eps_ln[:], LN_EPS)
            nc.gpsimd.memset(eps_f[:], F_EPS)
            nc.gpsimd.memset(eps_rms[:], RMS_EPS).then_inc(eps_set, 1)

            def alone():
                pool.wait_ge(eps_set, 1)

            def step(_nrm, qkv, att, _prj, _inp, rte):
                if rte is not None:
                    pool.wait_ge(x1_done, rte[0] + 1)
                if att is not None:
                    b, p, n = att
                    ga = gates_bc[:, bass.ds(b * 2 * D, D)]
                    if again(n):
                        pool.wait_ge(x1_ps, b - 1)
                    else:
                        pool.wait_ge(gates_in, 16)
                        pool.wait_ge(w_ld, 16 * 12)
                    nc.gpsimd.tensor_tensor(bo_ga[:, p, :], bo[:], ga, ALU.mult).then_inc(bo_done, 1)
                    nc.gpsimd.tensor_tensor(wo_ga[:, p, :], wo[:], ga, ALU.mult).then_inc(wo_done, 1)
                    pool.wait_ge(bo_done, b + 1)
                    pool.wait_ge(xn_done, b + 1)
                    xb = x_all[:, bass.ds(b * L, L)].rearrange("p (t d) -> p t d", d=D)
                    nc.gpsimd.tensor_tensor(xb, xb, bo_ga[:, p, :].unsqueeze(1).to_broadcast([P, NT, D]),
                                            ALU.add).then_inc(xb_done, 1)
                if qkv is not None:
                    b, p, n = qkv
                    pool.wait_ge(k_done, b + 1)
                    for t in range(NT):
                        kvt = kv[:, p, t, :].rearrange("p (e h d) -> p e h d", e=HE, d=HD)
                        k_in = kvt[:, HD:HE, :, :].to_broadcast([P, HD, H, HD])
                        v_in = v[:, p, t, :].rearrange("p (h e) -> p e h", e=HD).unsqueeze(3)
                        nc.gpsimd.tensor_tensor(kvt[:, 0:HD, :, :], k_in, v_in.to_broadcast([P, HD, H, HD]),
                                                ALU.mult).then_inc(kv_done[t], 1)
                if rte is not None:
                    b, p, n = rte
                    alone()
                    pool.wait_ge(lo_done, b + 1)
                    nc.gpsimd.tensor_copy(rows[:, p, :, 1, D // 2:D], rows[:, p, :, 0, D // 2:D])
                    nc.gpsimd.tensor_copy(rows[:, p, :, :, D:HW].rearrange("p t k o -> p (t k) o"),
                                          place_sb[:, bass.ds(b * NT * K, NT * K)].unsqueeze(2)).then_inc(rows_done, 1)
                    alone()
                    pool.wait_ge(pos_done, b + 1)
                    pool.wait_ge(rows_done, b + 1)
                    for t in range(NT):
                        for k in range(K):
                            pool.indirect_dma_start(
                                hbuf, bass.IndirectOffsetOnAxis(ap=pos[:, p, t * K + k:t * K + k + 1], axis=0),
                                rows[:, p, t, k, :], None).then_inc(scattered[p], 16)

            pipelined(pool, step)

            pool.wait_ge(wmax_done, 1)
            nc.gpsimd.partition_all_reduce(wmax_all[:], wmax[:], P, bass.bass_isa.ReduceOp.max).then_inc(wall_done, 1)

            with pool.Fori(1, TILES // TURN + 1) as n:
                for s in range(TURN):
                    alone()
                    pool.wait_ge(y_done[s], n)
                    for r in range(RB):
                        pool.indirect_dma_start(
                            ybuf, bass.IndirectOffsetOnAxis(ap=to_place[:, s, r:r + 1], axis=0),
                            yt[:, s % 2, r, :], None).then_inc(y_scat[s % 2], 16)

            def fold(b, p, n):
                if again(n):
                    pool.wait_ge(o_ps, b - 1)
                nc.gpsimd.tensor_tensor(wout_gb[:, p, :], woutn[:], gates_bc[:, bass.ds(b * 2 * D + D, D)],
                                        ALU.mult).then_inc(wgb_done, 1)

            pool.wait_ge(w_small, 2)
            for p in range(2):
                fold(p, p, 1)
            with pool.Fori(1, B // 2) as i:
                for p in range(2):
                    fold(2 * i + p, p, i + 1)

        @block.scalar
        def _(act):
            act.wait_ge(c_ld, 48)
            nc.scalar.activation(sc[:], cT_sb[:], ACT.Silu).then_inc(sc_done, 1)
            act.wait_ge(eps_set, 1)

            def norm(b, p, rs_, nmr_, xn_, nm_done, done):
                act.wait_ge(nm_done, b + 1)
                for t in range(NT):
                    last = nc.scalar.activation(xn_[:, p, t, :], x_all[:, bass.ds(b * L + t * P, P)], ACT.Identity,
                                                bias=nmr_[:, p, t:t + 1], scale=rs_[:, p, t:t + 1])
                last.then_inc(done, 1)

            def step(nrm, qkv, att, prj, inp, rte):
                if qkv is not None:
                    b, p, n = qkv
                    if not again(n):
                        act.wait_ge(modcol_done, 1)
                    act.wait_ge(turn_ps, b + 1)
                    nc.scalar.activation(hT[:, p, :], TB[:, L:2 * L], ACT.Identity,
                                         bias=mod_cols[:, bass.ds(b, 1)],
                                         scale=mod_cols[:, bass.ds(B + b, 1)]).then_inc(hT_done, 1)
                if inp is not None:
                    b, p, n = inp
                    act.wait_ge(turn_ps, b + 4)
                    nc.scalar.activation(h2T[:, p, :], TB[:, 0:L], ACT.Identity,
                                         bias=mod_cols[:, bass.ds(2 * B + b, 1)],
                                         scale=mod_cols[:, bass.ds(3 * B + b, 1)]).then_inc(h2T_done, 1)
                if nrm is not None:
                    b, p, n = nrm
                    act.wait_ge(ln_mv, b + 1)
                    nc.scalar.activation(sd[:, p, :], mv[:, p, :, 1], ACT.Sqrt,
                                         bias=eps_ln[:]).then_inc(ln_sd, 1)
                if rte is not None:
                    b, p, n = rte
                    act.wait_ge(rrs_done, b + 1)
                    if again(n):
                        act.wait_ge(scattered[p], 16 * NT * K * (n - 1))
                    for t in range(NT):
                        last = nc.scalar.activation(
                            rows16[:, p, t, :, 0:D], UB[:, t * D:(t + 1) * D].unsqueeze(1).to_broadcast([P, K, D]),
                            ACT.Copy, scale=rrs[:, p, t:t + 1])
                    last.then_inc(hi_done, 1)
                if qkv is not None:
                    b, p, n = qkv
                    act.wait_ge(kv_ps, b + 1)
                    if again(n):
                        act.wait_ge(cum_ps[NT - 1][2], b - 1)
                    kvb = KV[:].rearrange("p (t o d) -> p t o d", o=2, d=D)
                    nc.scalar.activation(k_raw[:], kvb[:, :, 0, :], ACT.Relu).then_inc(k_raw_done, 1)
                    nc.scalar.activation(v[:, p], kvb[:, :, 1, :], ACT.Copy)
                    act.wait_ge(k_raw_done, b + 1)
                    nc.scalar.activation(kv[:, p, :, HD * D:HE * D], k_raw[:], ACT.Identity,
                                         bias=eps_f[:]).then_inc(k_done, 1)
                if prj is not None:
                    b, p, n = prj
                    act.wait_ge(attnT_ps, b + 1)
                    nc.scalar.activation(attnT[:, p, :], FFN[:, L:2 * L], ACT.Copy).then_inc(attnT_done, 1)
                if qkv is not None:
                    b, p, n = qkv
                    act.wait_ge(q_ps, b + 1)
                    if again(n):
                        act.wait_ge(nd_ps, b - 1)
                    nc.scalar.activation(q_raw[:], TB[:, 0:L], ACT.Relu, bias=bq[:]).then_inc(q_raw_done, 1)
                    act.wait_ge(q_raw_done, b + 1)
                    nc.scalar.activation(qT[:, p, :], q_raw[:], ACT.Identity, bias=eps_f[:]).then_inc(q_done, 1)
                if nrm is not None:
                    norm(nrm[0], nrm[1], rs, nmr, xn, ln_nm, xn_done)
                if prj is not None:
                    b, p, n = prj
                    act.wait_ge(ln2_mv, b + 1)
                    nc.scalar.activation(sd2[:, p, :], mv2[:, p, :, 1], ACT.Sqrt,
                                         bias=eps_ln[:]).then_inc(ln2_sd, 1)
                if inp is not None:
                    b, p, n = inp
                    act.wait_ge(u_ps, b + 1)
                    nc.scalar.activation(uT[:, p, :], UB[:, L:2 * L], ACT.Copy).then_inc(uT_done, 1)
                    for t in range(NT):
                        last = nc.scalar.activation(junk[:], UB[:, t * D:(t + 1) * D], ACT.Square,
                                                    accum_out=ssq[:, p, t:t + 1])
                        last.then_inc(ssq_done, 1)
                        act.wait_ge(ssq_done, NT * b + t + 1)
                    nc.scalar.activation(rms[:, p, :], ssq[:, p, :], ACT.Sqrt, bias=eps_rms[:],
                                         scale=1.0 / D).then_inc(rms_done, 1)
                if prj is not None:
                    norm(prj[0], prj[1], rs2, nmr2, xn2, ln2_nm, xn2_done)

            pipelined(act, step)

            act.wait_ge(wscale_done, 2)
            nc.scalar.activation(w_hi[:], wgu[:], ACT.Copy, scale=wscale[:]).then_inc(whi_done, 1)
            act.wait_ge(gate_diff, 1)
            nc.scalar.activation(gate_all[:, :, 0], ldiff[:], ACT.Sigmoid)
            nc.scalar.activation(gate_all[:, :, 1], ldiff[:], ACT.Sigmoid, scale=-1.0).then_inc(gate_sig, 1)

            def gate(t, s, i, h):
                act.wait_ge(g_ps, 2 * t + h + 1)
                if s or again_turn(i):
                    act.wait_ge(gu_done, 2 * t + h - 1)
                nc.scalar.activation(sg[:, h, :], G[h], ACT.Silu, scale=descale[:]).then_inc(sg_done, 1)

            def square(t, s, i):
                act.wait_ge(y_ps, t + 1)
                if s >= 2 or again_turn(i):
                    act.wait_ge(y_scat[s % 2], 16 * RB * (TURN // 2 * i + s // 2))
                for r in range(RB):
                    if not (isinstance(t, int) and t == 0 and r == 0):
                        act.wait_ge(ysq_done, RB * t + r)
                    nc.scalar.activation(junk3[:], Y[s % 2][:, r * D:(r + 1) * D], ACT.Square,
                                         accum_out=yt[:, s % 2, r, D:YW]).then_inc(ysq_done, 1)

            def turn_of_tiles(i, first=False):
                for s in range(TURN):
                    gate(TURN * i + s, s, i, 0)
                    if s:
                        square(TURN * i + s - 1, s - 1, i)
                    elif not first:
                        square(TURN * i - 1, TURN - 1, i - 1)
                    gate(TURN * i + s, s, i, 1)

            turn_of_tiles(0, first=True)
            with act.Fori(1, TILES // TURN) as i:
                turn_of_tiles(i)
            square(TILES - 1, TURN - 1, TILES // TURN - 1)

            def stage_d(b, p, n):
                act.wait_ge(yb_ld[p], 16 * n)
                nc.scalar.activation(rms4[:, p], yb[:, p].rearrange("p t (k w) -> p t k w", k=K)[:, :, :, D], ACT.Sqrt,
                                     bias=eps_rms[:], scale=1.0 / D).then_inc(rms4_done, 1)

            def stage_e(b, p, n):
                act.wait_ge(mix_done, b + 1)
                for t in range(NT):
                    nc.scalar.activation(junk[:], mix[:, p, t, :], ACT.Square,
                                         accum_out=ssq4[:, p, t:t + 1]).then_inc(ssq4_done, 1)
                    act.wait_ge(ssq4_done, NT * b + t + 1)
                nc.scalar.activation(rms5[:, p, :], ssq4[:, p, :], ACT.Sqrt, bias=eps_rms[:],
                                     scale=1.0 / D).then_inc(rms5_done, 1)
                act.wait_ge(mixT_ps, b + 1)
                nc.scalar.activation(mixT[:, p, :], bk[p][:, 0:L], ACT.Copy).then_inc(mixT_done, 1)

            stage_d(0, 0, 1)
            stage_d(1, 1, 1)
            stage_e(0, 0, 1)
            with act.Fori(1, B // 2) as i:
                stage_d(2 * i, 0, i + 1)
                stage_e(2 * i - 1, 1, i)
                stage_d(2 * i + 1, 1, i + 1)
                stage_e(2 * i, 0, i + 1)
            stage_e(B - 1, 1, B // 2)

        @block.vector
        def _(dve):
            dve.wait_ge(w_ld, 16 * 12)
            nc.vector.tensor_scalar(wrn[:], wr[:], innorm[:], None, ALU.mult).then_inc(w_small, 1)
            nc.vector.tensor_scalar(woutn[:], wout[:], onorm[:], None, ALU.mult).then_inc(w_small, 1)
            nc.vector.memset(count[:, 0, :], 0.0)
            nc.vector.tensor_copy(ones16[:], ones)
            nc.vector.tensor_copy(strict16[:], strict).then_inc(w_small, 1)
            dve.wait_ge(modcol_ps, 1)
            mc = mod_cols[:].rearrange("p (g k b) -> p g k b", g=2, k=2)
            mp = UB[:, 0:4 * B].rearrange("p (g k b) -> p g k b", g=2, k=2)
            nc.vector.tensor_copy(mc[:, :, 0, :], mp[:, :, 0, :])
            nc.vector.tensor_scalar(mc[:, :, 1, :], mp[:, :, 1, :], 1.0, None, ALU.add).then_inc(modcol_done, 1)

            g = CUM[0][0:B, 0:2 * D]
            dve.wait_ge(gate_ps, 1)
            nc.vector.tensor_scalar(clamp_a[:], g, -1.0, 0.25, ALU.mult, ALU.max).then_inc(clamp_1, 1)
            nc.vector.tensor_scalar(clamp_s[:], g, 0.0, 2.0, ALU.is_ge, ALU.mult).then_inc(clamp_2, 1)
            dve.wait_ge(clamp_1, 1)
            nc.vector.tensor_tensor(clamp_a[:], clamp_a[:], g, ALU.max).then_inc(clamp_3, 1)
            dve.wait_ge(clamp_2, 1)
            dve.wait_ge(clamp_3, 1)
            nc.vector.scalar_tensor_tensor(gate_row[:], clamp_s[:], -1.0, clamp_a[:],
                                           ALU.add, ALU.mult).then_inc(gate_done, 1)
            for i in range(3):
                nc.vector.tensor_copy(bkv_part[:, i], bkv[:]).then_inc(bias_part, 1)
                dve.wait_ge(bias_part, 2 * i + 1)
                nc.vector.tensor_tensor(bkv[:], bkv[:], bkv_part[:, i], ALU.subtract).then_inc(bias_part, 1)
                dve.wait_ge(bias_part, 2 * i + 2)
            nc.vector.tensor_scalar(bkv3[:], bkv_part[:, 0], ident[0:3, 0:1], None, ALU.mult).then_inc(bias_part, 1)
            for i in range(1, 3):
                dve.wait_ge(bias_part, 6 + i)
                nc.vector.scalar_tensor_tensor(bkv3[:], bkv_part[:, i], ident[0:3, i:i + 1], bkv3[:],
                                               ALU.mult, ALU.add).then_inc(bias_part, 1)

            def alone():
                dve.wait_ge(w_small, 3)

            def norm_stats(b, st_, st_done, p):
                for t in range(NT):
                    last = nc.vector.bn_stats(st_[:, p, t, :], x_all[:, bass.ds(b * L + t * P, P)])
                last.then_inc(st_done, 1)

            def norm_mean(st_, mv_, st_done, st_count, mv_done, p):
                alone()
                dve.wait_ge(st_done, st_count)
                for t in range(NT):
                    last = nc.vector.bn_aggr(mv_[:, p, t, :], st_[:, p, t, :])
                last.then_inc(mv_done, 1)

            def norm_inv(b, sd_, rs_, sd_done, rs_done, p):
                dve.wait_ge(sd_done, b + 1)
                nc.vector.reciprocal(rs_[:, p, :], sd_[:, p, :]).then_inc(rs_done, 1)

            def norm_shift(b, mv_, rs_, nmr_, rs_done, nm_done, p):
                dve.wait_ge(rs_done, b + 1)
                nc.vector.scalar_tensor_tensor(nmr_[:, p, :], mv_[:, p, :, 0], -1.0, rs_[:, p, :],
                                               ALU.mult, ALU.mult).then_inc(nm_done, 1)

            def running_products(att, t):
                b, p, n = att
                if t == 0:
                    dve.wait_ge(q_done, b + 1)
                for cc in range(3):
                    dve.wait_ge(cum_ps[t][cc], b + 1)
                    if cc == 0 and t == 0 and (again(n) or p == 1):
                        dve.wait_ge(nd_ps, b)
                    cum = CUM[cc][:, 0:THIRD * P].rearrange("p (e i) -> p e i", i=P)
                    if t == 0:
                        nc.vector.tensor_tensor(s0blk[:, cc * THIRD:(cc + 1) * THIRD, :],
                                                cum[:, :, P - 1:P].to_broadcast([P, THIRD, H]),
                                                blk.unsqueeze(1).to_broadcast([P, THIRD, H]), ALU.mult)
                    nc.vector.tensor_tensor(
                        prod[:, t, cc * THIRD * P:(cc + 1) * THIRD * P].rearrange("p (e i) -> p e i", i=P), cum,
                        qT[:, p, t * P:(t + 1) * P].unsqueeze(1).to_broadcast([P, THIRD, P]),
                        ALU.mult).then_inc(cum_used[t][cc], 1)

            def logits(b, p):
                dve.wait_ge(logit_ps, b + 1)
                nc.vector.tensor_tensor(lr[:, p], LOGITS.rearrange("p (t e) -> p t e", e=E),
                                        rr[:, p, :].unsqueeze(2).to_broadcast([P, NT, E]),
                                        ALU.mult).then_inc(lr_done, 1)

            def scores(b, p):
                dve.wait_ge(lr_done, b + 1)
                nc.vector.tensor_tensor(score[:, p], lr[:, p], ebias[:].unsqueeze(1).to_broadcast([P, NT, E]),
                                        ALU.add).then_inc(score_done, 1)

            def best(b, p):
                alone()
                dve.wait_ge(score_done, b + 1)
                for t in range(NT):
                    last = nc.vector.max(m8[:, p, t, :], score[:, p, t, :])
                last.then_inc(max_done, 1)

            def best_index(b, p):
                alone()
                dve.wait_ge(max_done, b + 1)
                for t in range(NT):
                    last = nc.vector.max_index(i8[:, p, t, :], m8[:, p, t, :], score[:, p, t, :])
                last.then_inc(idx_done, 1)

            def index_values(b, p):
                dve.wait_ge(idx_done, b + 1)
                nc.vector.tensor_copy(i8f[:, p], i8[:, p, :, 0:K]).then_inc(idxf_done, 1)

            def one_hot(b, p):
                dve.wait_ge(idxf_done, b + 1)
                iota = cst[:, C_IOTA:C_IOTA + E].unsqueeze(1).unsqueeze(1).to_broadcast([P, NT, K, E])
                nc.vector.tensor_tensor(oh[:, p], iota, i8f[:, p].unsqueeze(3).to_broadcast([P, NT, K, E]),
                                        ALU.is_equal).then_inc(oh_done, 1)

            def chosen_experts(b, p):
                dve.wait_ge(oh_done, b + 1)
                nc.vector.tensor_tensor(chosen[:, p], oh[:, p, :, 0, :], oh[:, p, :, 1, :],
                                        ALU.add).then_inc(chosen_done, 1)

            def chosen_logits(b, p):
                nc.vector.tensor_tensor(ohl[:, p], oh[:, p], lr[:, p].unsqueeze(2).to_broadcast([P, NT, K, E]),
                                        ALU.mult).then_inc(ohl_done, 1)
                dve.wait_ge(chosen_done, b + 1)
                nc.vector.tensor_tensor(chosen2[:, p], chosen[:, p, 0, :], chosen[:, p, 1, :],
                                        ALU.add).then_inc(chosen2_done, 1)

            def keep_logits_and_count(b, p):
                dve.wait_ge(ohl_done, b + 1)
                nc.vector.tensor_reduce(lsel_all[:, bass.ds(b * NT * K, NT * K)],
                                        ohl[:, p].rearrange("p t k e -> p (t k) e"), AX.X,
                                        ALU.add).then_inc(lsel_done, 1)
                dve.wait_ge(chosen2_done, b + 1)
                nc.vector.tensor_tensor(count[:, 1 - p, :], count[:, p, :], chosen2[:, p],
                                        ALU.add).then_inc(count_done, 1)

            def slots_of_experts(b, p):
                dve.wait_ge(rank_ps, b + 1)
                nc.vector.tensor_tensor(
                    slot[:, p], RANK.rearrange("p (t e) -> p t e", e=E),
                    cst[:, C_REG:C_REG + E].unsqueeze(1).to_broadcast([P, NT, E]), ALU.add).then_inc(slot_done, 1)

            def chosen_slots(b, p):
                dve.wait_ge(slot_done, b + 1)
                nc.vector.tensor_tensor(ohs[:, p], oh[:, p], slot[:, p].unsqueeze(2).to_broadcast([P, NT, K, E]),
                                        ALU.mult).then_inc(ohs_done, 1)

            def slot_sums(b, p):
                dve.wait_ge(ohs_done, b + 1)
                nc.vector.tensor_reduce(posf[:, p], ohs[:, p], AX.X, ALU.add).then_inc(posf_done, 1)

            def positions(b, p, n):
                dve.wait_ge(posf_done, b + 1)
                if again(n):
                    dve.wait_ge(scattered[p], 16 * NT * K * (n - 1))
                nc.vector.tensor_copy(pos[:, p, :], posf[:, p].rearrange("p t k -> p (t k)")).then_inc(pos_done, 1)

            def low_halves(b, p):
                dve.wait_ge(hi_done, b + 1)
                for t in range(NT):
                    last = nc.vector.scalar_tensor_tensor(
                        rows16[:, p, t, 0, D:2 * D], UB[:, t * D:(t + 1) * D], rrs[:, p, t:t + 1],
                        rows16[:, p, t, 0, 0:D], ALU.mult, ALU.subtract)
                last.then_inc(lo_done, 1)

            def step(nrm, _qkv, att, prj, inp, rte):
                nb, np_, nn = nrm or (None,) * 3
                jb, jp, _jn = prj or (None,) * 3
                rb, rp, rn = rte or (None,) * 3
                nd = ND[:, 0:NT * HE * H].rearrange("p (t e h) -> p t e h", e=HE, h=H)
                if nrm is not None:
                    if isinstance(nb, int):
                        dve.wait_ge(x_first if nb < 2 else x_rest, 16)
                    norm_stats(nb, st, ln_st[np_], np_)
                if prj is not None:
                    dve.wait_ge(nd_ps, jb + 1)
                    nc.vector.tensor_scalar(den[:], nd[:, :, HD, :], F_EPS, None, ALU.max).then_inc(den_done, 1)
                if nrm is not None:
                    norm_mean(st, mv, ln_st[np_], nn, ln_mv, np_)
                if rte is not None:
                    dve.wait_ge(rms_done, rb + 1)
                    nc.vector.reciprocal(rr[:, rp, :], rms[:, rp, :]).then_inc(rr_done, 1)
                if prj is not None:
                    dve.wait_ge(den_done, jb + 1)
                    nc.vector.reciprocal(rden[:], den[:]).then_inc(rden_done, 1)
                if rte is not None:
                    dve.wait_ge(rr_done, rb + 1)
                    nc.vector.tensor_scalar(rrs[:, rp, :], rr[:, rp, :], HSCALE, None, ALU.mult).then_inc(rrs_done, 1)
                if prj is not None:
                    dve.wait_ge(rden_done, jb + 1)
                    nc.vector.tensor_tensor(attn[:, jp].rearrange("p t (h e) -> p t e h", e=HD), nd[:, :, 0:HD, :],
                                            rden[:].unsqueeze(2).to_broadcast([P, NT, HD, H]),
                                            ALU.mult).then_inc(attn_done, 1)
                if att is not None:
                    running_products(att, 0)
                if rte is not None:
                    logits(rb, rp)
                if rte is not None:
                    scores(rb, rp)
                    low_halves(rb, rp)
                    best(rb, rp)
                if nrm is not None:
                    norm_inv(nb, sd, rs, ln_sd, ln_rs, np_)
                if rte is not None:
                    best_index(rb, rp)
                if nrm is not None:
                    norm_shift(nb, mv, rs, nmr, ln_rs, ln_nm, np_)
                if rte is not None:
                    index_values(rb, rp)
                if att is not None:
                    running_products(att, 1)
                if prj is not None:
                    dve.wait_ge(x1_ps, jb + 1)
                    dve.wait_ge(xb_done, jb + 1)
                    xb = x_all[:, bass.ds(jb * L, L)]
                    nc.vector.tensor_tensor(xb, FFN[:, 0:L], xb, ALU.add).then_inc(x1_done, 1)
                if rte is not None:
                    one_hot(rb, rp)
                if prj is not None:
                    alone()
                    dve.wait_ge(x1_done, jb + 1)
                    norm_stats(jb, st2, ln2_st, jp)
                if rte is not None:
                    chosen_experts(rb, rp)
                if prj is not None:
                    norm_mean(st2, mv2, ln2_st, jb + 1, ln2_mv, jp)
                if rte is not None:
                    chosen_logits(rb, rp)
                if rte is not None:
                    slots_of_experts(rb, rp)
                if prj is not None:
                    norm_inv(jb, sd2, rs2, ln2_sd, ln2_rs, jp)
                if rte is not None:
                    chosen_slots(rb, rp)
                if prj is not None:
                    norm_shift(jb, mv2, rs2, nmr2, ln2_rs, ln2_nm, jp)
                if rte is not None:
                    slot_sums(rb, rp)
                    keep_logits_and_count(rb, rp)
                    positions(rb, rp, rn)

            pipelined(dve, step)

            chain = [0]

            def then(ins):
                chain[0] += 1
                ins.then_inc(ph2, 1)
                dve.wait_ge(ph2, chain[0])

            dve.wait_ge(total_ps, 1)
            then(nc.vector.tensor_copy(total[:], bk[0][:, 0:E]))
            then(nc.vector.tensor_tensor(tail_f[:], total[0:1, :], cst[0:1, C_REG:C_REG + E], ALU.add))
            nc.vector.tensor_copy(tail[:], tail_f[:]).then_inc(tail_done, 1)
            nj = TOK // R
            then(nc.vector.tensor_tensor(tcmp, total[0:1, :].unsqueeze(2).to_broadcast([1, E, nj]),
                                         cst[0:1, C_J:C_J + nj].unsqueeze(1).to_broadcast([1, E, nj]), ALU.is_gt))
            then(nc.vector.tensor_reduce(ntile[:], tcmp, AX.X, ALU.add))
            then(nc.vector.tensor_tensor(tlow[:], cst[0:1, C_LOW:C_LOW + E * E].rearrange("o (a b) -> o a b", b=E),
                                         ntile[:].unsqueeze(1).to_broadcast([1, E, E]), ALU.mult))
            then(nc.vector.tensor_reduce(tstart[:], tlow[:], AX.X, ALU.add))
            then(nc.vector.tensor_tensor(tend[:], tstart[:], ntile[:], ALU.add))
            tt = cst[0:1, C_T:C_T + TILES]
            then(nc.vector.tensor_tensor(tge, tt.unsqueeze(2).to_broadcast([1, TILES, E]),
                                         tend[:].unsqueeze(1).to_broadcast([1, TILES, E]), ALU.is_ge))
            then(nc.vector.tensor_reduce(texp[:], tge, AX.X, ALU.add))
            then(nc.vector.tensor_tensor(tgn, tge, ntile[:].unsqueeze(1).to_broadcast([1, TILES, E]), ALU.mult))
            then(nc.vector.tensor_reduce(tfirst[:], tgn, AX.X, ALU.add))
            then(nc.vector.tensor_tensor(trel[:], tt, tfirst[:], ALU.subtract))
            then(nc.vector.tensor_scalar(trel[:], trel[:], float(R), None, ALU.mult))
            then(nc.vector.scalar_tensor_tensor(trow_f[:], texp[:], float(REGION), trel[:], ALU.mult, ALU.add))
            then(nc.vector.tensor_copy(tile_row[:], trow_f[:]))
            then(nc.vector.tensor_scalar(texp[:], texp[:], float(E - 1), None, ALU.min))
            nc.vector.tensor_copy(tile_expert[:], texp[:]).then_inc(table_done, 1)
            lv = lsel_all[:].rearrange("p (n k) -> p n k", k=K)
            nc.vector.tensor_tensor(ldiff[:], lv[:, :, 0], lv[:, :, 1], ALU.subtract).then_inc(gate_diff, 1)
            dve.wait_ge(moe_ld, 48)
            nc.vector.tensor_copy(ident16[:], ident)
            then(nc.vector.tensor_scalar(wgu[:], wgu[:], innorm[:], None, ALU.mult))
            nc.vector.tensor_reduce(wmax[:], wgu[:], AX.X, ALU.max, apply_absolute_value=True).then_inc(wmax_done, 1)
            dve.wait_ge(wall_done, 1)
            then(nc.vector.tensor_scalar(wmax_all[:], wmax_all[:], 1e-30, None, ALU.max))
            then(nc.vector.tensor_scalar(wpow[:].bitcast(I32), wmax_all[:].bitcast(I32), 0x7F800000, None,
                                         ALU.bitwise_and))
            then(nc.vector.reciprocal(wscale[:], wpow[:]))
            nc.vector.tensor_scalar(descale[:], wpow[:], 2.0 ** -14 / HSCALE, None, ALU.mult).then_inc(wscale_done, 1)
            nc.vector.tensor_scalar(wscale[:], wscale[:], 2.0 ** 14, None, ALU.mult).then_inc(wscale_done, 1)
            dve.wait_ge(whi_done, 1)
            nc.vector.scalar_tensor_tensor(w_lo[:], wgu[:], wscale[:], w_hi[:], ALU.mult,
                                           ALU.subtract).then_inc(wlo_done, 1)

            dve.wait_ge(table_done, 1)
            ex_regs = [dve.alloc_register(f"dve_expert{j}") for j in range(4)]
            last_ex = dve.alloc_register("dve_last_expert")

            def experts(t):
                dve.load(ex_regs, tile_expert[0:1, bass.ds(t, 4)])
                return [dve.snap(r, min_val=0, max_val=E - 1) for r in ex_regs]


            def put_hT(t, s, i):
                dve.wait_ge(slotT_ps, t + 1)
                if s >= 2 or again_turn(i):
                    dve.wait_ge(u3_ps, 2 * t - 2)
                if again_turn(i):
                    dve.wait_ge(y_scat[s % 2], 16 * RB * (TURN // 2 * i + s // 2 - 1))
                nc.vector.tensor_copy(to_place[:, s, :].unsqueeze(2), slots[:, s, :, D:HW])
                nc.vector.tensor_copy(hT3[:, s % 2, :], T[s % 2][:].bitcast(F16)[:, 0:2 * R]).then_inc(hT3_done, 1)

            def gated(t, s, i, h):
                dve.wait_ge(u3_ps, 2 * t + h + 1)
                dve.wait_ge(sg_done, 2 * t + h + 1)
                if s or again_turn(i):
                    dve.wait_ge(y_ps, t)
                nc.vector.scalar_tensor_tensor(gu[:, h, :], U[h], descale[:], sg[:, h, :],
                                               ALU.mult, ALU.mult).then_inc(gu_done, 1)

            def weigh(t, s, i, e):
                dve.wait_ge(ysq_done, RB * (t + 1))
                if s >= 2 or again_turn(i):
                    dve.wait_ge(y_scat[s % 2], 16 * RB * (TURN // 2 * i + s // 2))
                row = enorm[:, bass.ds(e * D, D)]
                nc.vector.tensor_tensor(yt[:, s % 2, :, 0:D], Y[s % 2][:, 0:RB * D].rearrange("p (r d) -> p r d", d=D),
                                        row.unsqueeze(1).to_broadcast([P, RB, D]), ALU.mult).then_inc(y_done[s], 1)

            def turn_of_tiles(i, first=False, last=False):
                ex, ahead = experts(TURN * i), None if first else dve.snap(last_ex, min_val=0, max_val=E - 1)
                for s in range(TURN):
                    gated(TURN * i + s, s, i, 0)
                    if s:
                        weigh(TURN * i + s - 1, s - 1, i, ex[s - 1])
                    elif not first:
                        weigh(TURN * i - 1, TURN - 1, i - 1, ahead)
                    gated(TURN * i + s, s, i, 1)
                    if s < TURN - 2:
                        put_hT(TURN * i + s + 2, s + 2, i)
                    elif not last:
                        put_hT(TURN * i + s + 2, s + 2 - TURN, i + 1)
                dve.reg_mov(last_ex, ex[TURN - 1])

            put_hT(0, 0, 0)
            put_hT(1, 1, 0)
            turn_of_tiles(0, first=True)
            with dve.Fori(1, TILES // TURN - 1) as i:
                turn_of_tiles(i)
            turn_of_tiles(TILES // TURN - 1, last=True)
            weigh(TILES - 1, TURN - 1, TILES // TURN - 1, dve.snap(last_ex, min_val=0, max_val=E - 1))

            def stage_d(b, p, n):
                dve.wait_ge(rms4_done, b + 1)
                nc.vector.reciprocal(rinv4[:, p], rms4[:, p]).then_inc(rinv4_done, 1)
                dve.wait_ge(rinv4_done, b + 1)
                nc.vector.tensor_tensor(coef[:, p].rearrange("p t k -> p (t k)"),
                                        rinv4[:, p].rearrange("p t k -> p (t k)"),
                                        gate_all[:].rearrange("p n k -> p (n k)")[:, bass.ds(b * NT * K, NT * K)],
                                        ALU.mult).then_inc(coef_done, 1)
                dve.wait_ge(coef_done, b + 1)
                for t in range(NT):
                    last = nc.vector.tensor_scalar(half[:, p, t, :], yb[:, p, t, 0:D], coef[:, p, t, 0:1], None, ALU.mult)
                last.then_inc(half_done, 1)
                dve.wait_ge(half_done, b + 1)
                if again(n):
                    dve.wait_ge(mixT_ps, b - 1)
                    dve.wait_ge(ssq4_done, NT * (b - 1))
                for t in range(NT):
                    last = nc.vector.scalar_tensor_tensor(mix[:, p, t, :], yb[:, p, t, YW:YW + D], coef[:, p, t, 1:2],
                                                          half[:, p, t, :], ALU.mult, ALU.add)
                last.then_inc(mix_done, 1)

            def stage_e(b, p, n):
                dve.wait_ge(rms5_done, b + 1)
                nc.vector.reciprocal(rinv5[:, p, :], rms5[:, p, :]).then_inc(rinv5_done, 1)
                dve.wait_ge(rinv5_done, b + 1)
                dve.wait_ge(o_ps, b + 1)
                if again(n):
                    dve.wait_ge(stored[p], 16 * (n - 1))
                for t in range(NT):
                    last = nc.vector.scalar_tensor_tensor(
                        ob[:, p, t, :], bk[2 + p][:, t * D:(t + 1) * D], rinv5[:, p, t:t + 1],
                        x_all[:, bass.ds(b * L + t * P, P)], ALU.mult, ALU.add)
                last.then_inc(ob_done, 1)

            dve.wait_ge(gate_sig, 1)
            stage_d(0, 0, 1)
            stage_d(1, 1, 1)
            stage_e(0, 0, 1)
            with dve.Fori(1, B // 2) as i:
                stage_d(2 * i, 0, i + 1)
                stage_e(2 * i - 1, 1, i)
                stage_d(2 * i + 1, 1, i + 1)
                stage_e(2 * i, 0, i + 1)
            stage_e(B - 1, 1, B // 2)

        @block.tensor
        def _(pe):
            mm = nc.tensor.matmul
            pe.wait_ge(sc_done, 1)
            for j, part in enumerate((SA, CA, SB, CB)):
                last = mm(UB[:, j * B:(j + 1) * B], wmod_sb[:, part * D:(part + 1) * D], sc[:], start=True, stop=True)
            last.then_inc(modcol_ps, 1)
            wv = wmod_sb[:].rearrange("p (g k d) -> p g k d", g=2, k=3)[:, :, 2, :]
            mm(CUM[0][0:B, 0:2 * D].rearrange("p (g d) -> p g d", g=2), sc[:], wv, start=True,
               stop=True).then_inc(gate_ps, 1)

            def first(b):
                return isinstance(b, int) and b == 0

            def done_by(b):
                return min(b, B) if isinstance(b, int) else b

            def running_state(att, t):
                b, p, n = att
                pe.wait_ge(kv_done[t], b + 1)
                for cc in range(3):
                    if t:
                        pe.wait_ge(cum_used[t - 1][cc], b + 1)
                    elif not first(b):
                        pe.wait_ge(cum_used[NT - 1][cc], b)
                    elif cc == 0:
                        pe.wait_ge(gate_done, 1)
                    for j in range(THIRD):
                        e = cc * THIRD + j
                        last = mm(CUM[cc][:, j * P:(j + 1) * P], kv[:, p, t, e * D:(e + 1) * D], tri,
                                  start=True, stop=True)
                    last.then_inc(cum_ps[t][cc], 1)

            def head_sums(att, t):
                b, p, n = att
                o = ND[:, t * HE * H:(t + 1) * HE * H]
                pe.wait_ge(cum_used[t][2], b + 1)
                if t == 0:
                    if not first(b):
                        pe.wait_ge(attn_done, b)
                else:
                    mm(o, qT[:, p, t * P:(t + 1) * P], s0blk[:].rearrange("p e h -> p (e h)"), start=True, stop=False)
                for e in range(HE):
                    last = mm(o[:, e * H:(e + 1) * H], prod[:, t, e * P:(e + 1) * P], blk, start=(t == 0),
                              stop=(t == 0 or e == HE - 1))
                if t == NT - 1:
                    last.then_inc(nd_ps, 1)

            def step(_nrm, qkv, att, prj, inp, rte):
                if inp is not None:
                    b, p, n = inp
                    pe.wait_ge(xn2_done, b + 1)
                    pe.wait_ge(q_done, done_by(b + 3))
                    for t in range(NT):
                        last = nc.tensor.transpose(TB[:, t * P:(t + 1) * P], xn2[:, p, t, :], ident)
                if qkv is not None:
                    b, p, n = qkv
                    pe.wait_ge(xn_done, b + 1)
                    if not first(b):
                        pe.wait_ge(q_done, b)
                    for t in range(NT):
                        last = nc.tensor.transpose(TB[:, L + t * P:L + (t + 1) * P], xn[:, p, t, :], ident)
                if inp is not None or qkv is not None:
                    last.then_inc(turn_ps, 1)
                if att is not None:
                    running_state(att, 0)
                if qkv is not None:
                    b, p, n = qkv
                    pe.wait_ge(hT_done, b + 1)
                    if first(b):
                        pe.wait_ge(w_ld, 16 * 12)
                        pe.wait_ge(bias_part, 9)
                        pe.wait_ge(w_small, 3)
                    else:
                        pe.wait_ge(k_done, b)
                    for t in range(NT):
                        o = KV[:, t * 2 * D:(t + 1) * 2 * D]
                        mm(o, ones16[0:3, :], bkv3[:], start=True, stop=False)
                        last = mm(o, hT[:, p, t * P:(t + 1) * P], wqkv[:, D:3 * D], start=False, stop=True)
                    last.then_inc(kv_ps, 1)
                if prj is not None:
                    b, p, n = prj
                    pe.wait_ge(attn_done, b + 1)
                    if not first(b):
                        pe.wait_ge(x1_done, b)
                    if isinstance(b, int) and b < 3:
                        pass
                    else:
                        pe.wait_ge(slot_done, b - 2)
                    for t in range(NT):
                        last = nc.tensor.transpose(FFN[:, L + t * P:L + (t + 1) * P], attn[:, p, t, :], ident)
                    last.then_inc(attnT_ps, 1)
                if rte is not None:
                    b, p, n = rte
                    pe.wait_ge(attn_done, done_by(b + 3))
                    pe.wait_ge(uT_done, b + 1)
                    if first(b):
                        pe.wait_ge(w_small, 3)
                    for t in range(NT):
                        last = mm(LOGITS[:, t * E:(t + 1) * E], uT[:, p, t * P:(t + 1) * P], wrn[:],
                                  start=True, stop=True)
                    last.then_inc(logit_ps, 1)
                if qkv is not None:
                    b, p, n = qkv
                    if inp is not None:
                        pe.wait_ge(h2T_done, inp[0] + 1)
                    mm(TB[:, 0:L], wqkv[:, 0:D], hT[:, p, :], start=True, stop=True).then_inc(q_ps, 1)
                if att is not None:
                    running_state(att, 1)
                if prj is not None:
                    b, p, n = prj
                    pe.wait_ge(attnT_done, b + 1)
                    pe.wait_ge(wo_done, b + 1)
                    for t in range(NT):
                        o = FFN[:, t * D:(t + 1) * D]
                        last = mm(o, attnT[:, p, t * P:(t + 1) * P], wo_ga[:, p, :], start=True, stop=True)
                    last.then_inc(x1_ps, 1)
                if inp is not None:
                    b, p, n = inp
                    pe.wait_ge(h2T_done, b + 1)
                    if not first(b):
                        pe.wait_ge(lo_done, b)
                    else:
                        pe.wait_ge(modcol_done, 1)
                    for t in range(NT):
                        mm(UB[:, t * D:(t + 1) * D], h2T[:, p, t * P:(t + 1) * P], w_in[:], start=True, stop=True)
                    mm(UB[:, L:2 * L], w_in[:], h2T[:, p, :], start=True, stop=True).then_inc(u_ps, 1)
                if att is not None:
                    if rte is not None:
                        pe.wait_ge(lr_done, rte[0] + 1)
                    head_sums(att, 0)
                if rte is not None:
                    b, p, n = rte
                    pe.wait_ge(chosen_done, b + 1)
                    pe.wait_ge(x1_done, done_by(b + 3))
                    if not first(b):
                        pe.wait_ge(count_done, b)
                    for t in range(NT):
                        o = RANK[:, t * E:(t + 1) * E]
                        mm(o, strict16[:], chosen[:, p, t, :], start=True, stop=False)
                        for u in range(t):
                            mm(o, ones16[:], chosen[:, p, u, :], start=False, stop=False)
                        last = mm(o, ones16[:], count[:, p, :], start=False, stop=True)
                    last.then_inc(rank_ps, 1)
                if att is not None:
                    head_sums(att, 1)

            pipelined(pe, step)

            pe.wait_ge(count_done, B)
            mm(bk[0][:, 0:E], ones16[:], count[:, 0, :], start=True, stop=True).then_inc(total_ps, 1)

            pe.wait_ge(table_done, 1)
            ex_regs = [pe.alloc_register(f"pe_expert{j}") for j in range(4)]
            last_ex = pe.alloc_register("pe_last_expert")

            def experts(t):
                pe.load(ex_regs, tile_expert[0:1, bass.ds(t, 4)])
                return [pe.snap(r, min_val=0, max_val=E - 1) for r in ex_regs]


            def transpose_rows(t, s, i):
                pe.wait_ge(slot_ld[s], 16 * (i + 1))
                if s >= 2 or again_turn(i):
                    pe.wait_ge(hT3_done, t - 1)
                o = T[s % 2][:].bitcast(F16)
                for half in range(2):
                    for r in range(RB):
                        last = nc.tensor.transpose(o[:, half * R + r * P:half * R + (r + 1) * P],
                                                   slots16[:, s, r, half * D:(half + 1) * D], ident16[:])
                last.then_inc(slotT_ps, 1)

            def gate_up(t, s, i, e, h):
                if h == 0:
                    pe.wait_ge(hT3_done, t + 1)
                hi, lo = hT3[:, s % 2, 0:R], hT3[:, s % 2, R:2 * R]
                for part, banks, done in ((0, G, g_ps), (1, U, u3_ps)):
                    if s or again_turn(i):
                        pe.wait_ge((sg_done, gu_done)[part], 2 * t + h - 1)
                    for c in range(FC // 2):
                        o = banks[h][:, c * R:(c + 1) * R]
                        w = bass.ds(e * F + (part * E * F + (h * (FC // 2) + c) * P), P)
                        mm(o, w_hi[:, w], hi, start=True, stop=False)
                        mm(o, w_hi[:, w], lo, start=False, stop=False)
                        last = mm(o, w_lo[:, w], hi, start=False, stop=True)
                    last.then_inc(done, 1)

            def down(t, s, i, e):
                pe.wait_ge(gu_done, 2 * t + 2)
                if s >= 2 or again_turn(i):
                    pe.wait_ge(y_done[(s + 2) % TURN], i + 1 if s >= 2 else i)
                for r in range(RB):
                    for f in range(FC):
                        h, c = f // (FC // 2), f % (FC // 2)
                        last = mm(Y[s % 2][:, r * D:(r + 1) * D], gu[:, h, c * R + r * P:c * R + (r + 1) * P],
                                  wd[:, bass.ds(e * (FC * D) + f * D, D)], start=(f == 0), stop=(f == FC - 1))
                last.then_inc(y_ps, 1)

            def turn_of_tiles(i, first=False, last=False):
                ex, ahead = experts(TURN * i), None if first else pe.snap(last_ex, min_val=0, max_val=E - 1)
                for s in range(TURN):
                    gate_up(TURN * i + s, s, i, ex[s], 0)
                    if s:
                        down(TURN * i + s - 1, s - 1, i, ex[s - 1])
                    elif not first:
                        down(TURN * i - 1, TURN - 1, i - 1, ahead)
                    gate_up(TURN * i + s, s, i, ex[s], 1)
                    if s < TURN - 2:
                        transpose_rows(TURN * i + s + 2, s + 2, i)
                    elif not last:
                        transpose_rows(TURN * i + s + 2, s + 2 - TURN, i + 1)
                pe.reg_mov(last_ex, ex[TURN - 1])

            pe.wait_ge(wlo_done, 1)
            transpose_rows(0, 0, 0)
            transpose_rows(1, 1, 0)
            turn_of_tiles(0, first=True)
            with pe.Fori(1, TILES // TURN - 1) as i:
                turn_of_tiles(i)
            turn_of_tiles(TILES // TURN - 1, last=True)
            down(TILES - 1, TURN - 1, TILES // TURN - 1, pe.snap(last_ex, min_val=0, max_val=E - 1))

            def stage_d(b, p, n):
                pe.wait_ge(mix_done, b + 1)
                if again(n):
                    pe.wait_ge(mixT_done, b - 1)
                for t in range(NT):
                    last = nc.tensor.transpose(bk[p][:, t * P:(t + 1) * P], mix[:, p, t, :], ident)
                last.then_inc(mixT_ps, 1)

            def stage_e(b, p, n):
                pe.wait_ge(mixT_done, b + 1)
                pe.wait_ge(wgb_done, b + 1)
                if again(n):
                    pe.wait_ge(ob_done, b - 1)
                for t in range(NT):
                    last = mm(bk[2 + p][:, t * D:(t + 1) * D], mixT[:, p, t * P:(t + 1) * P], wout_gb[:, p, :],
                              start=True, stop=True)
                last.then_inc(o_ps, 1)

            stage_d(0, 0, 1)
            stage_d(1, 1, 1)
            stage_e(0, 0, 1)
            with pe.Fori(1, B // 2) as i:
                stage_d(2 * i, 0, i + 1)
                stage_e(2 * i - 1, 1, i)
                stage_d(2 * i + 1, 1, i + 1)
                stage_e(2 * i, 0, i + 1)
            stage_e(B - 1, 1, B // 2)


def kernel(L0_attn_x, L0_attn_qkv_w, L0_attn_qkv_b, L0_attn_out_w, L0_attn_out_b, L0_ffn_W_in, L0_ffn_in_norm_w,
           L0_ffn_Wr, L0_ffn_expert_bias, L0_ffn_Wg, L0_ffn_Wu, L0_ffn_Wd, L0_ffn_enorm_w, L0_ffn_out_norm_w,
           L0_ffn_W_out, L0_c, L0_wmod):
    import concourse.bacc as bacc
    from concourse.bass_utils import run_bass_kernel_spmd

    def arr(a):
        return np.ascontiguousarray(np.asarray(a))

    def gate_first(w):
        return np.asarray(w).transpose(2, 0, 1).reshape(D, E * F)

    consts, place, filler = shape_constants()
    arrays = {
        "x": arr(L0_attn_x),
        "cT": arr(np.asarray(L0_c).T),
        "wmod": arr(L0_wmod),
        "qkv_wT": arr(np.asarray(L0_attn_qkv_w).T),
        "qkv_b": arr(np.asarray(L0_attn_qkv_b).reshape(1, 3 * D)),
        "out_wT": arr(np.asarray(L0_attn_out_w).T),
        "out_b": arr(np.asarray(L0_attn_out_b).reshape(1, D)),
        "w_inT": arr(np.asarray(L0_ffn_W_in).T),
        "in_norm": arr(np.asarray(L0_ffn_in_norm_w).reshape(D, 1)),
        "wrT": arr(np.asarray(L0_ffn_Wr).T),
        "e_bias": arr(np.asarray(L0_ffn_expert_bias).reshape(1, E)),
        "wguT": arr(np.concatenate([gate_first(L0_ffn_Wg), gate_first(L0_ffn_Wu)], axis=1)),
        "wdT": arr(np.asarray(L0_ffn_Wd).reshape(E, D, FC, P).transpose(3, 0, 2, 1).reshape(P, E * FC * D)),
        "e_norm": arr(np.asarray(L0_ffn_enorm_w).reshape(1, E * D)),
        "out_norm": arr(np.asarray(L0_ffn_out_norm_w).reshape(D, 1)),
        "w_outT": arr(np.asarray(L0_ffn_W_out).T),
        "consts": consts, "place": place, "filler": filler,
    }
    nc = bacc.Bacc("TRN2", target_bir_lowering=False, num_devices=1)
    args = {n: nc.dram_tensor(n, a.shape, mybir.dt.from_np(a.dtype), kind="ExternalInput").ap()
            for n, a in arrays.items()}
    out = nc.dram_tensor("out", (B, L, D), F32, kind="ExternalOutput").ap()
    block_kernel(nc, **args, out=out)
    r = run_bass_kernel_spmd(nc, [arrays], core_ids=[0])
    return r.results[0]["out"]
```

```python
from contextlib import ExitStack

import numpy as np

import concourse.bass as bass
from concourse import mybir

F32 = mybir.dt.float32
F16 = mybir.dt.float16
BF16 = mybir.dt.bfloat16
I32 = mybir.dt.int32
U32 = mybir.dt.uint32
ALU = mybir.AluOpType
ACT = mybir.ActivationFunctionType
AX = mybir.AxisListType

P = 128
B, L, D = 16, 256, 128
H, HD = 16, 8
NT = L // P
TOK = B * L
E, F, K = 8, 512, 2
FC = F // P
HE = HD + 1
STATE = HE * D
THIRD = HE // 3
R = 256
RB = R // P
REGION = TOK + R
TURN = 4
TILES = (TOK * K + E * (R - 1)) // R
TURNS = -(-TILES // TURN)
SPARE = TILES - TOK * K // R
HROWS = E * REGION + SPARE * R
YROWS = TOK * K + (E + SPARE) * R
HW = D + 1
LN_EPS = 1e-5
F_EPS = 1e-6
RMS_EPS = float(np.finfo(np.float32).eps)
YW = D + 1
HSCALE = 2.0 ** 11
SA, CA, GA, SB, CB, GB = range(6)
WN = 8
WC = 2 * E * F // WN

C_ID, C_TRI, C_ONES, C_STRICT = 0, P, 2 * P, 3 * P
C_REG, C_IOTA = 4 * P, 4 * P + E
C_J = 4 * P + 2 * E
C_LOW = C_J + TOK // R
C_T = C_LOW + E * E
C_SEL = C_T + TURNS * TURN
C_END = C_SEL + 2 * P - H


def shape_constants():
    c = np.zeros((P, C_END), np.float32)
    p = np.arange(P)
    c[:, C_ID:C_ID + P] = np.eye(P)
    c[:, C_TRI:C_TRI + P] = p[:, None] <= p[None, :]
    c[:, C_ONES:C_ONES + P] = 1
    c[:, C_STRICT:C_STRICT + P] = p[:, None] < p[None, :]
    c[:, C_REG:C_REG + E] = np.arange(E) * REGION
    c[:, C_IOTA:C_IOTA + E] = np.arange(E)
    c[:, C_J:C_J + TOK // R] = np.arange(TOK // R) * R
    c[:, C_LOW:C_LOW + E * E] = (np.arange(E)[:, None] > np.arange(E)[None, :]).ravel()
    c[:, C_T:C_T + TURNS * TURN] = np.arange(TURNS * TURN)
    blk = p[:, None] // HD == np.arange(H)[None, :]
    c[:, C_SEL + P - H:C_SEL + P] = blk
    token = np.arange(TOK // P)[None, :, None] * P + p[:, None, None]
    place = (token * K + np.arange(K)).reshape(P, -1).astype(np.uint32)
    filler = np.zeros(((E + SPARE) * R, HW), np.uint32)
    filler[:, D] = TOK * K + np.arange((E + SPARE) * R)
    return c, place, filler


W_QKV, W_OUT = 0, 3 * D
W_IN = W_OUT + D
W_R = W_IN + D
W_IN_ROWS = W_R + E
W_LAST = W_IN_ROWS + D
W_BQ, W_INNORM, W_ONORM = (W_LAST + D + i for i in range(3))
W_END = W_ONORM + 1


def block_kernel(nc, x, c_wmod, weights_all, qkv_b, out_b, e_bias, wguT, wdT, e_norm, consts, place, filler, out):
    ctx = ExitStack()
    with ctx:
        def sb(name, shape, dt=F32):
            return ctx.enter_context(nc.sbuf_tensor(name, shape, dt))

        def sem(name):
            return ctx.enter_context(nc.semaphore(name))

        def two(name):
            return [sem(f"{name}{i}") for i in range(2)]

        def four(name):
            return [sem(f"{name}{i}") for i in range(4)]

        hbuf = nc.dram_tensor("dispatched", [HROWS, HW], U32, kind="Internal").ap()
        gbuf = nc.dram_tensor("gate_rows", [1, B * 2 * D], F32, kind="Internal").ap()
        ybuf = nc.dram_tensor("expert_rows", [YROWS, YW], F32, kind="Internal").ap()

        x_all = sb("x_all", [P, B * L])
        cst = sb("cst", [P, C_END])
        place_sb = sb("place_sb", [P, B * NT * K], U32)
        ident, tri, ones, strict = (cst[:, c:c + P] for c in (C_ID, C_TRI, C_ONES, C_STRICT))
        blk = cst[:, C_SEL + P - H:C_SEL + P]
        sel = [cst[:, C_SEL + P - H - e * H:C_SEL + 2 * P - H - e * H] for e in range(HD)]
        c_wmod_sb = sb("c_wmod_sb", [P, B + 6 * D])
        cT_sb, wmod_sb = c_wmod_sb[:, 0:B], c_wmod_sb[:, B:B + 6 * D]
        sc = sb("sc", [P, B])
        small = sb("small", [P, W_END])
        wqkv, wo, wr, w_in_rows, wout = (small[:, c:c + n] for c, n in (
            (W_QKV, 3 * D), (W_OUT, D), (W_R, E), (W_IN_ROWS, D), (W_LAST, D)))
        w_in = small[:, W_IN:W_IN + D + E]
        bq, innorm, onorm = (small[:, c:c + 1] for c in (W_BQ, W_INNORM, W_ONORM))
        bkv = sb("bkv", [3, 2 * D])
        bkv_part = sb("bkv_part", [3, 3, 2 * D], BF16)
        bkv3 = sb("bkv3", [3, 2 * D], BF16)
        bo = sb("bo", [P, D])
        bo_ga = sb("bo_ga", [P, 2, D])
        wrn = sb("wrn", [P, E])
        ebias = sb("ebias", [P, E])
        late = sb("late", [P, max(2 * E * F, B * NT * K * YW)])
        wgu = late[:, 0:2 * E * F]
        w_hi = sb("w_hi", [P, 2 * E * F], F16)
        w_lo = sb("w_lo", [P, 2 * E * F], F16)
        wd = sb("wd", [P, E * FC * D])
        enorm = sb("enorm", [P, E * D])
        woutn = sb("woutn", [P, D])
        mod_cols = sb("mod_cols", [P, 4 * B])
        gates_bc = sb("gates_bc", [P, B * 2 * D])
        eps_ln = sb("eps_ln", [P, 1])
        eps_f = sb("eps_f", [P, 1])
        eps_rms = sb("eps_rms", [P, 1])
        lsel_all = sb("lsel_all", [P, B * NT * K])
        ldiff = sb("ldiff", [P, B * NT])
        gate_all = sb("gate_all", [P, B * NT, K])

        gate_row, clamp_a, clamp_s = (sb(n, [B, 2 * D]) for n in ("gate_row", "clamp_a", "clamp_s"))

        st = sb("st", [P, 2, NT, 6])
        mv = sb("mv", [P, 2, NT, 2])
        sd = sb("sd", [P, 2, NT])
        rs = sb("rs", [P, 2, NT])
        nmr = sb("nmr", [P, 2, NT])
        xn = sb("xn", [P, 2, NT, D])
        hT = sb("hT", [P, 2, L])
        q_raw = sb("q_raw", [P, L])
        k_raw = sb("k_raw", [P, NT, D])
        qT = sb("qT", [P, 2, L])
        v = sb("v", [P, 2, NT, D])
        kv = sb("kv", [P, 2, NT, STATE])
        prod = sb("prod", [P, NT, STATE])
        s0 = sb("s0", [P, HE])
        den = sb("den", [P, NT, H])
        rden = sb("rden", [P, NT, H])
        rden_e = sb("rden_e", [P, NT, HD, H])
        rdenT = sb("rdenT", [P, L])
        attnT = sb("attnT", [P, 2, L])
        wo_ga = sb("wo_ga", [P, 2, D])
        st2 = sb("st2", [P, 2, NT, 6])
        mv2 = sb("mv2", [P, 2, NT, 2])
        sd2 = sb("sd2", [P, 2, NT])
        rs2 = sb("rs2", [P, 2, NT])
        nmr2 = sb("nmr2", [P, 2, NT])
        xn2 = sb("xn2", [P, 2, NT, D])
        h2T = sb("h2T", [P, 2, L])
        junk = sb("junk", [P, D])
        ssq = sb("ssq", [P, 2, NT])
        rms = sb("rms", [P, 2, NT])
        rr = sb("rr", [P, 2, NT])
        rrs = sb("rrs", [P, 2, NT])
        rows = sb("rows", [P, 2, NT, K, HW], U32)
        rows16 = rows[:].bitcast(F16)
        lr = sb("lr", [P, 2, NT, E])
        score = sb("score", [P, 2, NT, E])
        m8 = sb("m8", [P, 2, NT, 8])
        i8 = sb("i8", [P, 2, NT, 8], U32)
        i8f = sb("i8f", [P, 2, NT, K])
        oh = sb("oh", [P, 2, NT, K, E])
        ohl = sb("ohl", [P, 2, NT, K, E])
        chosen = sb("chosen", [P, 2, NT, E], BF16)
        chosen2 = sb("chosen2", [P, 2, E], BF16)
        count = sb("count", [P, 2, E], BF16)
        ones16 = sb("ones16", [P, P], BF16)
        strict16 = sb("strict16", [P, P], BF16)
        slot = sb("slot", [P, 2, NT, E])
        ohs = sb("ohs", [P, 2, NT, K, E])
        posf = sb("posf", [P, 2, NT, K])
        pos = sb("pos", [P, 2, NT * K], U32)

        spare = prod[0:1].rearrange("o t s -> o (t s)")
        tcmp, tge, tgn = (spare[:, a:a + n * m].rearrange("o (n m) -> o n m", m=m) for a, n, m in (
            (0, E, TOK // R), (E * TOK // R, TURNS * TURN, E), (E * TOK // R + TURNS * TURN * E, TURNS * TURN, E)))
        wmaxs = sb("wmaxs", [P, WN])
        innorm_abs = sb("innorm_abs", [P, 1])
        w_by = sb("w_by", [P, 1])
        wmax = sb("wmax", [P, 1])
        wmax_all = sb("wmax_all", [P, 1])
        wpow = sb("wpow", [P, 1])
        wscale = sb("wscale", [P, 1])
        descale = sb("descale", [P, 1])
        total = sb("total", [P, E])
        tail_f = sb("tail_f", [1, E])
        tail = sb("tail", [1, E], I32)
        ntile = sb("ntile", [1, E])
        tlow = sb("tlow", [1, E, E])
        tstart = sb("tstart", [1, E])
        tend = sb("tend", [1, E])
        texp = sb("texp", [1, TURNS * TURN])
        tfirst = sb("tfirst", [1, TURNS * TURN])
        trel = sb("trel", [1, TURNS * TURN])
        trow_f = sb("trow_f", [1, TURNS * TURN])
        tile_row = sb("tile_row", [1, TURNS * TURN], I32)
        tile_expert = sb("tile_expert", [1, TURNS * TURN], I32)

        LAST = TILES - (TURNS - 1) * TURN
        slots = sb("slots", [P, 4, RB, HW], U32)
        slots16 = slots[:].bitcast(F16)
        ident16 = sb("ident16", [P, P], F16)
        hT3 = sb("hT3", [P, 2, 2 * R], F16)
        sg, gu = (kv[:, i].rearrange("p t s -> p (t s)")[:, 0:2 * F].rearrange("p (j f) -> p j f", f=F)
                  for i in range(2))
        to_place = sb("to_place", [P, TURN, RB], U32)
        yt = sb("yt", [P, 2, RB, YW])
        junk3 = sb("junk3", [P, D])

        yb = late[:, 0:B * NT * K * YW].rearrange("p (n k w) -> p n k w", k=K, w=YW)
        half, mix, mixT, ob = (prod[:].rearrange("p t s -> p (t s)")[:, i * 2 * L:(i + 1) * 2 * L].rearrange(
            "p (j t d) -> p j t d", j=2, t=NT) for i in range(4))
        mixT = mixT.rearrange("p j t d -> p j (t d)")
        rms4, rinv4, coef = (sb(n, [P, B * NT, K]) for n in ("rms4", "rinv4", "coef"))
        ssq4 = sb("ssq4", [P, 2, NT])
        rms5 = sb("rms5", [P, 2, NT])
        rinv5 = sb("rinv5", [P, 2, NT])

        bk = [ctx.enter_context(nc.psum_tensor(f"bank{i}", [P, 512], F32)) for i in range(8)]
        T, G, U, Y = bk[0:2], [b[:] for b in bk[2:4]], [b[:] for b in bk[4:6]], [b[:] for b in bk[6:8]]
        CUM = bk[0:3]
        TB, KV, ND, FFN, UB = bk[3:8]

        LOADS = [(0, 2), (2, 4), (4, 8), (8, B)]
        DEN = CUM[2][:, THIRD * P:THIRD * P + NT * H]
        RANK = FFN[:, L:L + NT * E]
        UL = UB[:, 0:NT * (D + E)].rearrange("p (t d) -> p t d", t=NT)

        x_first, x_rest, c_ld, bkv_ld, w_ld, wgu_ld, moe_ld, filled = (
            sem(n) for n in ("x_first", "x_rest", "c_ld", "bkv_ld", "w_ld", "wgu_ld", "moe_ld", "filled"))
        eps_set = sem("eps_set")
        sc_done, modcol_ps, modcol_done = sem("sc_done"), sem("modcol_ps"), sem("modcol_done")
        gate_ps, clamp_1, clamp_2, clamp_3, gate_done, gates_out, gates_in = (
            sem(n) for n in ("gate_ps", "clamp_1", "clamp_2", "clamp_3", "gate_done", "gates_out", "gates_in"))
        bias_part = sem("bias_part")
        bo_done, xb_done = sem("bo_done"), sem("xb_done")
        w_small, router_ps, router_done = sem("w_small"), sem("router_ps"), sem("router_done")
        ln_mv, ln_sd, ln_rs, ln_nm, xn_done = (sem(n) for n in ("ln_mv", "ln_sd", "ln_rs", "ln_nm", "xn_done"))
        turn_ps, hT_done = sem("turn_ps"), sem("hT_done")
        kv_ps, q_ps, q_raw_done, k_raw_done, q_done, k_done = (
            sem(n) for n in ("kv_ps", "q_ps", "q_raw_done", "k_raw_done", "q_done", "k_done"))
        kv_done = [sem(f"kv_done_{t}") for t in range(NT)]
        cum_ps = [[sem(f"cum_ps_{t}_{c}") for c in range(3)] for t in range(NT)]
        cum_used = [[sem(f"cum_used_{t}_{c}") for c in range(3)] for t in range(NT)]
        s0_done, nd_ps, den_done, rden_done, rden_e_done, rdenT_ps, rdenT_done = (sem(n) for n in ("s0_done", "nd_ps", "den_done", "rden_done", "rden_e_done", "rdenT_ps", "rdenT_done"))
        attnT_done, wo_done, x1_ps, x1_done = (sem(n) for n in ("attnT_done", "wo_done", "x1_ps", "x1_done"))
        ln2_mv, ln2_sd, ln2_rs, ln2_nm, xn2_done = (
            sem(n) for n in ("ln2_mv", "ln2_sd", "ln2_rs", "ln2_nm", "xn2_done"))
        h2T_done, u_ps, ssq_done, rms_done, rr_done, rrs_done = (
            sem(n) for n in ("h2T_done", "u_ps", "ssq_done", "rms_done", "rr_done", "rrs_done"))
        hi_done, lo_done, rows_done = (sem(n) for n in ("hi_done", "lo_done", "rows_done"))
        ln_st, ln2_st = two("ln_st"), sem("ln2_st")
        scattered, yb_ld, stored = two("scattered"), [sem(f"yb_ld{i}") for i in range(4)], two("stored")
        lr_done, score_done, max_done, idx_done, idxf_done, oh_done = (
            sem(n) for n in ("lr_done", "score_done", "max_done", "idx_done", "idxf_done", "oh_done"))
        chosen_done, chosen2_done, count_done, ohl_done, lsel_done = (
            sem(n) for n in ("chosen_done", "chosen2_done", "count_done", "ohl_done", "lsel_done"))
        rank_ps, slot_done, ohs_done, posf_done, pos_done = (
            sem(n) for n in ("rank_ps", "slot_done", "ohs_done", "posf_done", "pos_done"))
        ph2, total_ps, tail_done, table_done, wmaxs_done, wmax_done, wall_done, wscale_done, whi_done, wlo_done = (
            sem(n) for n in ("ph2", "total_ps", "tail_done", "table_done", "wmaxs_done", "wmax_done", "wall_done",
                             "wscale_done", "whi_done", "wlo_done"))
        gate_diff, gate_sig = sem("gate_diff"), sem("gate_sig")
        slot_ld, y_scat, y_done = four("slot_ld"), two("y_scat"), four("y_done")
        slotT_ps, hT3_done, g_ps, u3_ps, sg_done, gu_done, y_ps, ysq_done = (
            sem(n) for n in ("slotT_ps", "hT3_done", "g_ps", "u3_ps", "sg_done", "gu_done", "y_ps", "ysq_done"))
        rms4_done, rinv4_done, coef_done = sem("rms4_done"), sem("rinv4_done"), sem("coef_done")
        half_done, mix_done, mixT_ps, mixT_done = (sem(n) for n in ("half_done", "mix_done", "mixT_ps", "mixT_done"))
        ssq4_done, rms5_done, rinv5_done, wgb_done, o_ps, ob_done = (
            sem(n) for n in ("ssq4_done", "rms5_done", "rinv5_done", "wgb_done", "o_ps", "ob_done"))

        SCALE_STEP = B - WN - 1
        MAX_STEPS = range(SCALE_STEP - 4, SCALE_STEP)

        block = ctx.enter_context(nc.Block())

        def yb_of(b, t, k):
            return yb[:, bass.ds(b * NT + t, 1), k, 0:D].rearrange("p o d -> p (o d)")

        def again(n):
            return not (isinstance(n, int) and n <= 1)

        def batch_of_turn(i, j):
            return 4 * i + j, j % 2, 2 * i + j // 2 + 1

        def again_turn(i):
            return not (isinstance(i, int) and i == 0)

        def pipelined(eng, step):
            def at(s):
                return (s, s % 2, s // 2 + 1) if 0 <= s < B else None
            stages = range(6)
            for s in range(B - WN):
                step(*(at(s - g) for g in stages))
            with eng.Fori((B - WN) // 2 + 1, B // 2 + 1) as m:
                for r in range(2):
                    step(*((2 * m - 2 + r - g, (r - g) % 2, m + (r - g) // 2) for g in stages))
            for s in range(B, B + 5):
                step(*(at(s - g) for g in stages))

        @block.sync
        def _(sp):
            xv = x.rearrange("b (t p) d -> p (b t) d", p=P)
            xs = x_all[:].rearrange("p (n d) -> p n d", d=D)
            sp.dma_start(c_wmod_sb[:], c_wmod).then_inc(c_ld, 16)
            sp.dma_start(xs[:, 0:2 * NT, :], xv[:, 0:2 * NT, :]).then_inc(x_first, 16)
            sp.dma_start(bkv[:], qkv_b[:, D:3 * D].to_broadcast([3, 2 * D])).then_inc(bkv_ld, 16)
            sp.dma_start(cst[:], consts).then_inc(w_ld, 16)
            sp.dma_start(small[:], weights_all).then_inc(w_ld, 16)
            sp.dma_start(bo[:], out_b.to_broadcast([P, D])).then_inc(w_ld, 16)
            sp.dma_start(ebias[:], e_bias.to_broadcast([P, E])).then_inc(w_ld, 16)
            sp.dma_start(place_sb[:], place).then_inc(w_ld, 16)
            sp.dma_start(xs[:, 2 * NT:, :], xv[:, 2 * NT:, :]).then_inc(x_rest, 16)
            sp.wait_ge(gate_done, 1)
            sp.dma_start(gbuf.rearrange("o (b g) -> (o b) g", b=B), gate_row[:]).then_inc(gates_out, 16)
            sp.wait_ge(gates_out, 16)
            sp.dma_start(gates_bc[:], gbuf.to_broadcast([P, B * 2 * D])).then_inc(gates_in, 16)
            sp.dma_start(wgu, wguT).then_inc(wgu_ld, 16)
            sp.dma_start(wd[:], wdT).then_inc(moe_ld, 16)
            sp.dma_start(enorm[:], e_norm.to_broadcast([P, E * D])).then_inc(moe_ld, 16)
            sp.dma_start(hbuf[E * REGION:HROWS, :], filler[E * R:, :]).then_inc(filled, 16)

            sp.wait_ge(tail_done, 1)
            tail_regs = [sp.alloc_register(f"tail{e}") for e in range(E // 2)]
            sp.load(tail_regs, tail[0:1, 0:E // 2])
            for e in range(E // 2):
                row = sp.snap(tail_regs[e], min_val=0, max_val=E * REGION - R)
                sp.dma_start(hbuf[bass.ds(row, R), :], filler[e * R:(e + 1) * R, :]).then_inc(filled, 16)

            sp.wait_ge(scattered[0], 16 * NT * K * (B // 2))
            sp.wait_ge(scattered[1], 16 * NT * K * (B // 2))
            sp.wait_ge(filled, 16 * (E + 1))
            sp.wait_ge(table_done, 1)
            row_regs = [sp.alloc_register(f"tile_row{s}") for s in range(TURN)]

            def load_tiles(i, tiles=TURN):
                sp.load(row_regs, tile_row[0:1, bass.ds(TURN * i, TURN)])
                for s in range(tiles):
                    row = sp.snap(row_regs[s], min_val=0, max_val=HROWS - R)
                    if again_turn(i):
                        sp.wait_ge(hT3_done, TURN * i + s - 3)
                    sp.dma_start(slots[:, s], hbuf[bass.ds(row, R), :].rearrange("(p j) w -> p j w", j=RB)).then_inc(
                        slot_ld[s], 16)

            load_tiles(0)
            with sp.Fori(1, TURNS - 1) as i:
                load_tiles(i)
            load_tiles(TURNS - 1, LAST)

            for p in range(2):
                sp.wait_ge(y_scat[p], 16 * RB * ((TILES + 1 - p) // 2))

            for i, (first, end) in enumerate(LOADS):
                sp.dma_start(yb[:, first * NT:end * NT], ybuf[first * L * K:end * L * K, :].rearrange(
                    "(n p k) w -> p n k w", p=P, k=K)).then_inc(yb_ld[i], 16)

            def store(b, p):
                sp.wait_ge(ob_done, b + 1)
                sp.dma_start(out[bass.ds(b, 1), :, :].rearrange("o (t p) d -> p (o t) d", p=P),
                             ob[:, p]).then_inc(stored[p], 16)

            with sp.Fori(0, B // 2) as i:
                for p in range(2):
                    store(2 * i + p, p)
            for p in range(2):
                sp.wait_ge(stored[p], 16 * (B // 2))

        @block.gpsimd
        def _(pool):
            nc.gpsimd.memset(eps_ln[:], LN_EPS)
            nc.gpsimd.memset(eps_f[:], F_EPS)
            nc.gpsimd.memset(eps_rms[:], RMS_EPS).then_inc(eps_set, 1)
            pool.wait_ge(bkv_ld, 16)
            for i in range(3):
                nc.gpsimd.tensor_copy(bkv_part[:, i], bkv[:]).then_inc(bias_part, 1)
                pool.wait_ge(bias_part, 2 * i + 1)
                nc.gpsimd.tensor_tensor(bkv[:], bkv[:], bkv_part[:, i], ALU.subtract).then_inc(bias_part, 1)
                pool.wait_ge(bias_part, 2 * i + 2)
            pool.wait_ge(w_ld, 16 * 5)
            for i in range(3):
                nc.gpsimd.tensor_tensor(bkv_part[:, i], bkv_part[:, i], ident[0:3, i:i + 1].to_broadcast([3, 2 * D]),
                                        ALU.mult).then_inc(bias_part, 1)
            pool.wait_ge(bias_part, 8)
            nc.gpsimd.tensor_tensor(bkv3[:], bkv_part[:, 0], bkv_part[:, 1], ALU.add).then_inc(bias_part, 1)
            pool.wait_ge(bias_part, 10)
            nc.gpsimd.tensor_tensor(bkv3[:], bkv3[:], bkv_part[:, 2], ALU.add).then_inc(bias_part, 1)

            def alone():
                pool.wait_ge(eps_set, 1)

            def step(nrm, qkv, att, _prj, _inp, rte):
                if nrm is not None and isinstance(nrm[0], int) and nrm[0] == SCALE_STEP:
                    pool.wait_ge(wmax_done, 1)
                    nc.gpsimd.partition_all_reduce(wmax_all[:], wmax[:], P,
                                                   bass.bass_isa.ReduceOp.max).then_inc(wall_done, 1)
                if rte is not None:
                    pool.wait_ge(x1_done, rte[0] + 1)
                if att is not None:
                    b, p, n = att
                    ga = gates_bc[:, bass.ds(b * 2 * D, D)]
                    if again(n):
                        pool.wait_ge(x1_ps, b - 1)
                    else:
                        pool.wait_ge(gates_in, 16)
                        pool.wait_ge(w_ld, 16 * 5)
                    nc.gpsimd.tensor_tensor(bo_ga[:, p, :], bo[:], ga, ALU.mult).then_inc(bo_done, 1)
                    nc.gpsimd.tensor_tensor(wo_ga[:, p, :], wo, ga, ALU.mult).then_inc(wo_done, 1)
                    pool.wait_ge(bo_done, b + 1)
                    pool.wait_ge(xn_done, b + 1)
                    xb = x_all[:, bass.ds(b * L, L)].rearrange("p (t d) -> p t d", d=D)
                    nc.gpsimd.tensor_tensor(xb, xb, bo_ga[:, p, :].unsqueeze(1).to_broadcast([P, NT, D]),
                                            ALU.add).then_inc(xb_done, 1)
                if qkv is not None:
                    b, p, n = qkv
                    pool.wait_ge(k_done, b + 1)
                    for t in range(NT):
                        kvt = kv[:, p, t, :].rearrange("p (e h d) -> p e h d", e=HE, d=HD)
                        k_in = kvt[:, HD:HE, :, :].to_broadcast([P, HD, H, HD])
                        v_in = v[:, p, t, :].rearrange("p (h e) -> p e h", e=HD).unsqueeze(3)
                        nc.gpsimd.tensor_tensor(kvt[:, 0:HD, :, :], k_in, v_in.to_broadcast([P, HD, H, HD]),
                                                ALU.mult).then_inc(kv_done[t], 1)
                if rte is not None:
                    b, p, n = rte
                    alone()
                    pool.wait_ge(lo_done, b + 1)
                    nc.gpsimd.tensor_copy(rows[:, p, :, 1, D // 2:D], rows[:, p, :, 0, D // 2:D])
                    nc.gpsimd.tensor_copy(rows[:, p, :, :, D:HW].rearrange("p t k o -> p (t k) o"),
                                          place_sb[:, bass.ds(b * NT * K, NT * K)].unsqueeze(2)).then_inc(rows_done, 1)
                    alone()
                    pool.wait_ge(pos_done, b + 1)
                    pool.wait_ge(rows_done, b + 1)
                    for t in range(NT):
                        for k in range(K):
                            pool.indirect_dma_start(
                                hbuf, bass.IndirectOffsetOnAxis(ap=pos[:, p, t * K + k:t * K + k + 1], axis=0),
                                rows[:, p, t, k, :], None).then_inc(scattered[p], 16)

            pipelined(pool, step)

            pool.wait_ge(w_small, 2)
            gb = gates_bc[:].rearrange("p (b g d) -> p b g d", g=2, d=D)[:, :, 1, :]
            nc.gpsimd.tensor_tensor(gb, gb, woutn[:].unsqueeze(1).to_broadcast([P, B, D]), ALU.mult).then_inc(wgb_done, 1)

            def scatter_tile(s, n):
                alone()
                pool.wait_ge(y_done[s], n)
                for r in range(RB):
                    pool.indirect_dma_start(
                        ybuf, bass.IndirectOffsetOnAxis(ap=to_place[:, s, r:r + 1], axis=0),
                        yt[:, s % 2, r, :], None).then_inc(y_scat[s % 2], 16)

            with pool.Fori(1, TURNS) as n:
                for s in range(TURN):
                    scatter_tile(s, n)
            for s in range(LAST):
                scatter_tile(s, TURNS)

            def halve(b, p, n):
                if again(n):
                    pool.wait_ge(mix_done, b - 1)
                nc.gpsimd.tensor_tensor(half[:, p], yb[:, bass.ds(b * NT, NT), 0, 0:D],
                                        coef[:, bass.ds(b * NT, NT), 0:1].to_broadcast([P, NT, D]),
                                        ALU.mult).then_inc(half_done, 1)

            pool.wait_ge(coef_done, 1)
            for i in range(2):
                for j in range(4):
                    for g, (first, _) in enumerate(LOADS):
                        if first == 4 * i + j and g:
                            pool.wait_ge(coef_done, g + 1)
                    halve(*batch_of_turn(i, j))
            pool.wait_ge(coef_done, len(LOADS))
            with pool.Fori(2, B // 4) as i:
                for j in range(4):
                    halve(*batch_of_turn(i, j))

        @block.scalar
        def _(act):
            act.wait_ge(c_ld, 16)
            nc.scalar.activation(sc[:], cT_sb, ACT.Silu).then_inc(sc_done, 1)
            act.wait_ge(eps_set, 1)
            nc.scalar.activation(junk[:, 0:1], eps_ln[:], ACT.Sqrt)

            def norm(b, p, rs_, nmr_, xn_, nm_done, done):
                act.wait_ge(nm_done, b + 1)
                for t in range(NT):
                    last = nc.scalar.activation(xn_[:, p, t, :], x_all[:, bass.ds(b * L + t * P, P)], ACT.Identity,
                                                bias=nmr_[:, p, t:t + 1], scale=rs_[:, p, t:t + 1])
                last.then_inc(done, 1)

            def step(nrm, qkv, att, prj, inp, rte):
                if qkv is not None:
                    b, p, n = qkv
                    if not again(n):
                        act.wait_ge(modcol_done, 1)
                    act.wait_ge(turn_ps, b + 1)
                    nc.scalar.activation(hT[:, p, :], TB[:, L:2 * L], ACT.Identity,
                                         bias=mod_cols[:, bass.ds(b, 1)],
                                         scale=mod_cols[:, bass.ds(B + b, 1)]).then_inc(hT_done, 1)
                if inp is not None:
                    b, p, n = inp
                    act.wait_ge(turn_ps, b + 4)
                    nc.scalar.activation(h2T[:, p, :], TB[:, 0:L], ACT.Identity,
                                         bias=mod_cols[:, bass.ds(2 * B + b, 1)],
                                         scale=mod_cols[:, bass.ds(3 * B + b, 1)]).then_inc(h2T_done, 1)
                if nrm is not None:
                    b, p, n = nrm
                    act.wait_ge(ln_mv, b + 1)
                    nc.scalar.activation(sd[:, p, :], mv[:, p, :, 1], ACT.Sqrt,
                                         bias=eps_ln[:]).then_inc(ln_sd, 1)
                if prj is not None:
                    b, p, n = prj
                    act.wait_ge(rden_done, b + 1)
                    if again(n) or p == 1:
                        act.wait_ge(rdenT_ps, b)
                    nc.scalar.activation(rden_e[:], rden[:].unsqueeze(2).to_broadcast([P, NT, HD, H]),
                                         ACT.Copy).then_inc(rden_e_done, 1)
                if rte is not None:
                    b, p, n = rte
                    act.wait_ge(rrs_done, b + 1)
                    if again(n):
                        act.wait_ge(scattered[p], 16 * NT * K * (n - 1))
                    for t in range(NT):
                        last = nc.scalar.activation(
                            rows16[:, p, t, :, 0:D], UL[:, t, 0:D].unsqueeze(1).to_broadcast([P, K, D]),
                            ACT.Copy, scale=rrs[:, p, t:t + 1])
                    last.then_inc(hi_done, 1)
                if prj is not None:
                    b, p, n = prj
                    act.wait_ge(rdenT_ps, b + 1)
                    if again(n) or p == 1:
                        act.wait_ge(attnT_done, b)
                    nc.scalar.activation(rdenT[:], ND[:, L:2 * L], ACT.Copy).then_inc(rdenT_done, 1)
                if qkv is not None:
                    b, p, n = qkv
                    act.wait_ge(kv_ps, b + 1)
                    if again(n):
                        act.wait_ge(cum_ps[NT - 1][2], b - 1)
                    kvb = KV[:].rearrange("p (t o d) -> p t o d", o=2, d=D)
                    nc.scalar.activation(k_raw[:], kvb[:, :, 0, :], ACT.Relu).then_inc(k_raw_done, 1)
                    nc.scalar.activation(v[:, p], kvb[:, :, 1, :], ACT.Copy)
                    act.wait_ge(k_raw_done, b + 1)
                    nc.scalar.activation(kv[:, p, :, HD * D:HE * D], k_raw[:], ACT.Identity,
                                         bias=eps_f[:]).then_inc(k_done, 1)
                if qkv is not None:
                    b, p, n = qkv
                    act.wait_ge(q_ps, b + 1)
                    if again(n):
                        act.wait_ge(nd_ps, b - 1)
                    nc.scalar.activation(q_raw[:], TB[:, 0:L], ACT.Relu, bias=bq).then_inc(q_raw_done, 1)
                    act.wait_ge(q_raw_done, b + 1)
                    nc.scalar.activation(qT[:, p, :], q_raw[:], ACT.Identity, bias=eps_f[:]).then_inc(q_done, 1)
                if nrm is not None:
                    norm(nrm[0], nrm[1], rs, nmr, xn, ln_nm, xn_done)
                if nrm is not None and not isinstance(nrm[0], int):
                    act.wait_ge(wscale_done, 1)
                    w = bass.ds(nrm[0] * WC - (SCALE_STEP + 1) * WC, WC)
                    nc.scalar.activation(w_hi[:, w], wgu[:, w], ACT.Copy, scale=w_by[:]).then_inc(whi_done, 1)
                if prj is not None:
                    b, p, n = prj
                    act.wait_ge(ln2_mv, b + 1)
                    nc.scalar.activation(sd2[:, p, :], mv2[:, p, :, 1], ACT.Sqrt,
                                         bias=eps_ln[:]).then_inc(ln2_sd, 1)
                if inp is not None:
                    b, p, n = inp
                    act.wait_ge(u_ps, b + 1)
                    for t in range(NT):
                        last = nc.scalar.activation(junk[:], UL[:, t, 0:D], ACT.Square,
                                                    accum_out=ssq[:, p, t:t + 1])
                        last.then_inc(ssq_done, 1)
                        act.wait_ge(ssq_done, NT * b + t + 1)
                    nc.scalar.activation(rms[:, p, :], ssq[:, p, :], ACT.Sqrt, bias=eps_rms[:],
                                         scale=1.0 / D).then_inc(rms_done, 1)
                if prj is not None:
                    norm(prj[0], prj[1], rs2, nmr2, xn2, ln2_nm, xn2_done)

            pipelined(act, step)

            act.wait_ge(tail_done, 1)
            tail_regs = [act.alloc_register(f"act_tail{e}") for e in range(E // 2)]
            act.load(tail_regs, tail[0:1, E // 2:E])
            for e in range(E // 2, E):
                row = act.snap(tail_regs[e - E // 2], min_val=0, max_val=E * REGION - R)
                act.dma_start(hbuf[bass.ds(row, R), :], filler[e * R:(e + 1) * R, :]).then_inc(filled, 16)

            act.wait_ge(gate_diff, 1)
            nc.scalar.activation(gate_all[:, :, 0], ldiff[:], ACT.Sigmoid)
            nc.scalar.activation(gate_all[:, :, 1], ldiff[:], ACT.Sigmoid, scale=-1.0).then_inc(gate_sig, 1)

            def gate(t, s, i, h):
                act.wait_ge(g_ps, 2 * t + h + 1)
                if s or again_turn(i):
                    act.wait_ge(gu_done, 2 * t + h - 1)
                nc.scalar.activation(sg[:, h, :], G[h], ACT.Silu, scale=descale[:]).then_inc(sg_done, 1)

            def square(t, s, i):
                act.wait_ge(y_ps, t + 1)
                if s >= 2 or again_turn(i):
                    act.wait_ge(y_scat[s % 2], 16 * RB * (TURN // 2 * i + s // 2))
                for r in range(RB):
                    if not (isinstance(t, int) and t == 0 and r == 0):
                        act.wait_ge(ysq_done, RB * t + r)
                    nc.scalar.activation(junk3[:], Y[s % 2][:, r * D:(r + 1) * D], ACT.Square,
                                         accum_out=yt[:, s % 2, r, D:YW]).then_inc(ysq_done, 1)

            def turn_of_tiles(i, first=False, tiles=TURN):
                for s in range(tiles):
                    gate(TURN * i + s, s, i, 0)
                    if s:
                        square(TURN * i + s - 1, s - 1, i)
                    elif not first:
                        square(TURN * i - 1, TURN - 1, i - 1)
                    gate(TURN * i + s, s, i, 1)

            turn_of_tiles(0, first=True)
            with act.Fori(1, TURNS - 1) as i:
                turn_of_tiles(i)
            turn_of_tiles(TURNS - 1, tiles=LAST)
            square(TILES - 1, LAST - 1, TURNS - 1)

            def rms_of_rows(g):
                act.wait_ge(yb_ld[g], 16)
                w = slice(LOADS[g][0] * NT, LOADS[g][1] * NT)
                nc.scalar.activation(rms4[:, w], yb[:, w, :, D], ACT.Sqrt, bias=eps_rms[:],
                                     scale=1.0 / D).then_inc(rms4_done, 1)

            def norm_out(b, p, n):
                act.wait_ge(mix_done, b + 1)
                if again(n):
                    act.wait_ge(rinv5_done, b - 1)
                for t in range(NT):
                    nc.scalar.activation(junk[:], mix[:, p, t, :], ACT.Square,
                                         accum_out=ssq4[:, p, t:t + 1]).then_inc(ssq4_done, 1)
                    act.wait_ge(ssq4_done, NT * b + t + 1)
                act.wait_ge(mixT_ps, b + 1)
                if again(n):
                    act.wait_ge(o_ps, b - 1)
                nc.scalar.activation(mixT[:, p, :], bk[p][:, 0:L], ACT.Copy).then_inc(mixT_done, 1)
                nc.scalar.activation(rms5[:, p, :], ssq4[:, p, :], ACT.Sqrt, bias=eps_rms[:],
                                     scale=1.0 / D).then_inc(rms5_done, 1)

            rms_of_rows(0)
            for b in range(8):
                norm_out(*batch_of_turn(0, b))
                if b in (0, 2, 5):
                    rms_of_rows((0, 2, 5).index(b) + 1)
            with act.Fori(2, B // 4) as i:
                for j in range(4):
                    norm_out(*batch_of_turn(i, j))

        @block.vector
        def _(dve):
            dve.wait_ge(modcol_ps, 1)
            mc = mod_cols[:].rearrange("p (g k b) -> p g k b", g=2, k=2)
            mp = UB[:, 0:4 * B].rearrange("p (g k b) -> p g k b", g=2, k=2)
            nc.vector.tensor_copy(mc[:, :, 0, :], mp[:, :, 0, :])
            nc.vector.tensor_scalar(mc[:, :, 1, :], mp[:, :, 1, :], 1.0, None, ALU.add).then_inc(modcol_done, 1)

            g = CUM[0][0:B, 0:2 * D]
            dve.wait_ge(gate_ps, 1)
            nc.vector.tensor_scalar(clamp_a[:], g, -1.0, 0.25, ALU.mult, ALU.max).then_inc(clamp_1, 1)
            nc.vector.tensor_scalar(clamp_s[:], g, 0.0, 2.0, ALU.is_ge, ALU.mult).then_inc(clamp_2, 1)
            dve.wait_ge(clamp_1, 1)
            nc.vector.tensor_tensor(clamp_a[:], clamp_a[:], g, ALU.max).then_inc(clamp_3, 1)
            dve.wait_ge(clamp_2, 1)
            dve.wait_ge(clamp_3, 1)
            nc.vector.scalar_tensor_tensor(gate_row[:], clamp_s[:], -1.0, clamp_a[:],
                                           ALU.add, ALU.mult).then_inc(gate_done, 1)
            dve.wait_ge(w_ld, 16 * 5)
            nc.vector.tensor_scalar(wrn[:], wr, innorm, None, ALU.mult).then_inc(w_small, 1)
            nc.vector.tensor_scalar(woutn[:], wout, onorm, None, ALU.mult).then_inc(w_small, 1)
            nc.vector.tensor_copy(ident16[:], ident)
            nc.vector.tensor_scalar(innorm_abs[:], innorm, -1.0, innorm, ALU.mult, ALU.max)
            nc.vector.memset(count[:, 0, :], 0.0)
            nc.vector.tensor_copy(ones16[:], ones)
            nc.vector.tensor_copy(strict16[:], strict).then_inc(w_small, 1)
            dve.wait_ge(router_ps, 1)
            nc.vector.tensor_copy(w_in[:, D:D + E], ND[:, 0:E]).then_inc(router_done, 1)

            def alone():
                dve.wait_ge(w_small, 3)

            def norm_stats(b, st_, st_done, p):
                for t in range(NT):
                    last = nc.vector.bn_stats(st_[:, p, t, :], x_all[:, bass.ds(b * L + t * P, P)])
                last.then_inc(st_done, 1)

            def norm_mean(st_, mv_, st_done, st_count, mv_done, p):
                alone()
                dve.wait_ge(st_done, st_count)
                for t in range(NT):
                    last = nc.vector.bn_aggr(mv_[:, p, t, :], st_[:, p, t, :])
                last.then_inc(mv_done, 1)

            def norm_inv(b, sd_, rs_, sd_done, rs_done, p):
                dve.wait_ge(sd_done, b + 1)
                nc.vector.reciprocal(rs_[:, p, :], sd_[:, p, :]).then_inc(rs_done, 1)

            def norm_shift(b, mv_, rs_, nmr_, rs_done, nm_done, p):
                dve.wait_ge(rs_done, b + 1)
                nc.vector.scalar_tensor_tensor(nmr_[:, p, :], mv_[:, p, :, 0], -1.0, rs_[:, p, :],
                                               ALU.mult, ALU.mult).then_inc(nm_done, 1)

            def running_products(att, t):
                b, p, n = att
                if t == 0:
                    dve.wait_ge(q_done, b + 1)
                for cc in range(3):
                    dve.wait_ge(cum_ps[t][cc], b + 1)
                    if cc == 0 and t == 0 and (again(n) or p == 1):
                        dve.wait_ge(nd_ps, b)
                    cum = CUM[cc][:, 0:THIRD * P].rearrange("p (e i) -> p e i", i=P)
                    if t == 0:
                        nc.vector.tensor_copy(s0[:, cc * THIRD:(cc + 1) * THIRD].unsqueeze(2),
                                              cum[:, :, P - 1:P]).then_inc(s0_done, 1)
                        nc.vector.tensor_tensor(
                            prod[:, t, cc * THIRD * P:(cc + 1) * THIRD * P].rearrange("p (e i) -> p e i", i=P), cum,
                            qT[:, p, t * P:(t + 1) * P].unsqueeze(1).to_broadcast([P, THIRD, P]),
                            ALU.mult).then_inc(cum_used[t][cc], 1)
                    else:
                        if cc == 0:
                            dve.wait_ge(s0_done, 3 * b + 3)
                        for j in range(THIRD):
                            e = cc * THIRD + j
                            last = nc.vector.scalar_tensor_tensor(
                                prod[:, t, e * P:(e + 1) * P], cum[:, j, :], s0[:, e:e + 1],
                                qT[:, p, t * P:(t + 1) * P], ALU.add, ALU.mult)
                        last.then_inc(cum_used[t][cc], 1)

            def logits(b, p):
                dve.wait_ge(hi_done, b + 1)
                nc.vector.tensor_tensor(lr[:, p], UL[:, :, D:D + E],
                                        rr[:, p, :].unsqueeze(2).to_broadcast([P, NT, E]),
                                        ALU.mult).then_inc(lr_done, 1)

            def scores(b, p):
                dve.wait_ge(lr_done, b + 1)
                nc.vector.tensor_tensor(score[:, p], lr[:, p], ebias[:].unsqueeze(1).to_broadcast([P, NT, E]),
                                        ALU.add).then_inc(score_done, 1)

            def best(b, p):
                alone()
                dve.wait_ge(score_done, b + 1)
                for t in range(NT):
                    last = nc.vector.max(m8[:, p, t, :], score[:, p, t, :])
                last.then_inc(max_done, 1)

            def best_index(b, p):
                alone()
                dve.wait_ge(max_done, b + 1)
                for t in range(NT):
                    last = nc.vector.max_index(i8[:, p, t, :], m8[:, p, t, :], score[:, p, t, :])
                last.then_inc(idx_done, 1)

            def index_values(b, p):
                dve.wait_ge(idx_done, b + 1)
                nc.vector.tensor_copy(i8f[:, p], i8[:, p, :, 0:K]).then_inc(idxf_done, 1)

            def one_hot(b, p):
                dve.wait_ge(idxf_done, b + 1)
                iota = cst[:, C_IOTA:C_IOTA + E].unsqueeze(1).unsqueeze(1).to_broadcast([P, NT, K, E])
                nc.vector.tensor_tensor(oh[:, p], iota, i8f[:, p].unsqueeze(3).to_broadcast([P, NT, K, E]),
                                        ALU.is_equal).then_inc(oh_done, 1)

            def chosen_experts(b, p):
                dve.wait_ge(oh_done, b + 1)
                nc.vector.tensor_tensor(chosen[:, p], oh[:, p, :, 0, :], oh[:, p, :, 1, :],
                                        ALU.add).then_inc(chosen_done, 1)

            def chosen_logits(b, p):
                nc.vector.tensor_tensor(ohl[:, p], oh[:, p], lr[:, p].unsqueeze(2).to_broadcast([P, NT, K, E]),
                                        ALU.mult).then_inc(ohl_done, 1)
                dve.wait_ge(chosen_done, b + 1)
                nc.vector.tensor_tensor(chosen2[:, p], chosen[:, p, 0, :], chosen[:, p, 1, :],
                                        ALU.add).then_inc(chosen2_done, 1)

            def keep_logits_and_count(b, p):
                dve.wait_ge(ohl_done, b + 1)
                nc.vector.tensor_reduce(lsel_all[:, bass.ds(b * NT * K, NT * K)],
                                        ohl[:, p].rearrange("p t k e -> p (t k) e"), AX.X,
                                        ALU.add).then_inc(lsel_done, 1)
                dve.wait_ge(chosen2_done, b + 1)
                nc.vector.tensor_tensor(count[:, 1 - p, :], count[:, p, :], chosen2[:, p],
                                        ALU.add).then_inc(count_done, 1)

            def slots_of_experts(b, p):
                dve.wait_ge(rank_ps, b + 1)
                nc.vector.tensor_tensor(
                    slot[:, p], RANK.rearrange("p (t e) -> p t e", e=E),
                    cst[:, C_REG:C_REG + E].unsqueeze(1).to_broadcast([P, NT, E]), ALU.add).then_inc(slot_done, 1)

            def chosen_slots(b, p):
                dve.wait_ge(slot_done, b + 1)
                nc.vector.tensor_tensor(ohs[:, p], oh[:, p], slot[:, p].unsqueeze(2).to_broadcast([P, NT, K, E]),
                                        ALU.mult).then_inc(ohs_done, 1)

            def slot_sums(b, p):
                dve.wait_ge(ohs_done, b + 1)
                nc.vector.tensor_reduce(posf[:, p], ohs[:, p], AX.X, ALU.add).then_inc(posf_done, 1)

            def positions(b, p, n):
                dve.wait_ge(posf_done, b + 1)
                if again(n):
                    dve.wait_ge(scattered[p], 16 * NT * K * (n - 1))
                nc.vector.tensor_copy(pos[:, p, :], posf[:, p].rearrange("p t k -> p (t k)")).then_inc(pos_done, 1)

            def low_halves(b, p):
                for t in range(NT):
                    last = nc.vector.scalar_tensor_tensor(
                        rows16[:, p, t, 0, D:2 * D], UL[:, t, 0:D], rrs[:, p, t:t + 1],
                        rows16[:, p, t, 0, 0:D], ALU.mult, ALU.subtract)
                last.then_inc(lo_done, 1)

            chain = [0]

            def then(ins):
                chain[0] += 1
                ins.then_inc(ph2, 1)
                dve.wait_ge(ph2, chain[0])

            def weights(s):
                if isinstance(s, int) and s in MAX_STEPS:
                    if s == MAX_STEPS[0]:
                        dve.wait_ge(wgu_ld, 16)
                    n = WN // len(MAX_STEPS)
                    for c in range((s - MAX_STEPS[0]) * n, (s - MAX_STEPS[0] + 1) * n):
                        nc.vector.tensor_reduce(wmaxs[:, c:c + 1], wgu[:, c * WC:(c + 1) * WC], AX.X, ALU.max,
                                                apply_absolute_value=True).then_inc(wmaxs_done, 1)
                    if s == MAX_STEPS[-1]:
                        dve.wait_ge(wmaxs_done, WN)
                        then(nc.vector.tensor_reduce(wmax[:], wmaxs[:], AX.X, ALU.max))
                        nc.vector.tensor_tensor(wmax[:], wmax[:], innorm_abs[:], ALU.mult).then_inc(wmax_done, 1)
                elif isinstance(s, int) and s == SCALE_STEP:
                    dve.wait_ge(wall_done, 1)
                    then(nc.vector.tensor_scalar(wmax_all[:], wmax_all[:], 1e-30, None, ALU.max))
                    then(nc.vector.tensor_scalar(wpow[:].bitcast(I32), wmax_all[:].bitcast(I32), 0x7F800000, None,
                                                 ALU.bitwise_and))
                    then(nc.vector.reciprocal(wscale[:], wpow[:]))
                    then(nc.vector.tensor_scalar(descale[:], wpow[:], 2.0 ** -14 / HSCALE, None, ALU.mult))
                    nc.vector.tensor_scalar(w_by[:], wscale[:], 2.0 ** 14, innorm, ALU.mult,
                                            ALU.mult).then_inc(wscale_done, 1)
                elif not isinstance(s, int):
                    dve.wait_ge(whi_done, s - SCALE_STEP)
                    w = bass.ds(s * WC - (SCALE_STEP + 1) * WC, WC)
                    nc.vector.scalar_tensor_tensor(w_lo[:, w], wgu[:, w], w_by[:], w_hi[:, w], ALU.mult,
                                                   ALU.subtract).then_inc(wlo_done, 1)

            def step(nrm, _qkv, att, prj, inp, rte):
                nb, np_, nn = nrm or (None,) * 3
                jb, jp, _jn = prj or (None,) * 3
                rb, rp, rn = rte or (None,) * 3
                if nrm is not None:
                    if isinstance(nb, int):
                        dve.wait_ge(x_first if nb < 2 else x_rest, 16)
                    norm_stats(nb, st, ln_st[np_], np_)
                if prj is not None:
                    dve.wait_ge(nd_ps, jb + 1)
                    nc.vector.tensor_scalar(den[:], DEN.rearrange("p (t h) -> p t h", h=H), F_EPS, None,
                                            ALU.max).then_inc(den_done, 1)
                if nrm is not None:
                    norm_mean(st, mv, ln_st[np_], nn, ln_mv, np_)
                if rte is not None:
                    dve.wait_ge(rms_done, rb + 1)
                    nc.vector.reciprocal(rr[:, rp, :], rms[:, rp, :]).then_inc(rr_done, 1)
                if prj is not None:
                    dve.wait_ge(den_done, jb + 1)
                    nc.vector.reciprocal(rden[:], den[:]).then_inc(rden_done, 1)
                if rte is not None:
                    dve.wait_ge(rr_done, rb + 1)
                    nc.vector.tensor_scalar(rrs[:, rp, :], rr[:, rp, :], HSCALE, None, ALU.mult).then_inc(rrs_done, 1)
                if att is not None:
                    running_products(att, 0)
                if prj is not None:
                    dve.wait_ge(rdenT_done, jb + 1)
                    if again(_jn):
                        dve.wait_ge(x1_ps, jb - 1)
                    nc.vector.tensor_tensor(attnT[:, jp, :], ND[:, 0:L], rdenT[:], ALU.mult).then_inc(attnT_done, 1)
                if rte is not None:
                    logits(rb, rp)
                if rte is not None:
                    scores(rb, rp)
                    low_halves(rb, rp)
                    best(rb, rp)
                if nrm is not None:
                    norm_inv(nb, sd, rs, ln_sd, ln_rs, np_)
                if rte is not None:
                    best_index(rb, rp)
                if nrm is not None:
                    norm_shift(nb, mv, rs, nmr, ln_rs, ln_nm, np_)
                if rte is not None:
                    index_values(rb, rp)
                if att is not None:
                    running_products(att, 1)
                if prj is not None:
                    dve.wait_ge(x1_ps, jb + 1)
                    dve.wait_ge(xb_done, jb + 1)
                    xb = x_all[:, bass.ds(jb * L, L)]
                    nc.vector.tensor_tensor(xb, FFN[:, 0:L], xb, ALU.add).then_inc(x1_done, 1)
                if rte is not None:
                    one_hot(rb, rp)
                if prj is not None:
                    alone()
                    dve.wait_ge(x1_done, jb + 1)
                    norm_stats(jb, st2, ln2_st, jp)
                if rte is not None:
                    chosen_experts(rb, rp)
                if prj is not None:
                    norm_mean(st2, mv2, ln2_st, jb + 1, ln2_mv, jp)
                if rte is not None:
                    chosen_logits(rb, rp)
                if rte is not None:
                    slots_of_experts(rb, rp)
                if prj is not None:
                    norm_inv(jb, sd2, rs2, ln2_sd, ln2_rs, jp)
                if rte is not None:
                    chosen_slots(rb, rp)
                if prj is not None:
                    norm_shift(jb, mv2, rs2, nmr2, ln2_rs, ln2_nm, jp)
                if rte is not None:
                    slot_sums(rb, rp)
                    keep_logits_and_count(rb, rp)
                    positions(rb, rp, rn)
                if nrm is not None:
                    weights(nb)

            pipelined(dve, step)

            dve.wait_ge(total_ps, 1)
            then(nc.vector.tensor_copy(total[:], bk[0][:, 0:E]))
            then(nc.vector.tensor_tensor(tail_f[:], total[0:1, :], cst[0:1, C_REG:C_REG + E], ALU.add))
            nc.vector.tensor_copy(tail[:], tail_f[:]).then_inc(tail_done, 1)
            nj = TOK // R
            then(nc.vector.tensor_tensor(tcmp, total[0:1, :].unsqueeze(2).to_broadcast([1, E, nj]),
                                         cst[0:1, C_J:C_J + nj].unsqueeze(1).to_broadcast([1, E, nj]), ALU.is_gt))
            then(nc.vector.tensor_reduce(ntile[:], tcmp, AX.X, ALU.add))
            then(nc.vector.tensor_tensor(tlow[:], cst[0:1, C_LOW:C_LOW + E * E].rearrange("o (a b) -> o a b", b=E),
                                         ntile[:].unsqueeze(1).to_broadcast([1, E, E]), ALU.mult))
            then(nc.vector.tensor_reduce(tstart[:], tlow[:], AX.X, ALU.add))
            then(nc.vector.tensor_tensor(tend[:], tstart[:], ntile[:], ALU.add))
            tt = cst[0:1, C_T:C_T + TURNS * TURN]
            then(nc.vector.tensor_tensor(tge, tt.unsqueeze(2).to_broadcast([1, TURNS * TURN, E]),
                                         tend[:].unsqueeze(1).to_broadcast([1, TURNS * TURN, E]), ALU.is_ge))
            then(nc.vector.tensor_reduce(texp[:], tge, AX.X, ALU.add))
            then(nc.vector.tensor_tensor(tgn, tge, ntile[:].unsqueeze(1).to_broadcast([1, TURNS * TURN, E]), ALU.mult))
            then(nc.vector.tensor_reduce(tfirst[:], tgn, AX.X, ALU.add))
            then(nc.vector.tensor_tensor(trel[:], tt, tfirst[:], ALU.subtract))
            then(nc.vector.tensor_scalar(trel[:], trel[:], float(R), None, ALU.mult))
            then(nc.vector.scalar_tensor_tensor(trow_f[:], texp[:], float(REGION), trel[:], ALU.mult, ALU.add))
            then(nc.vector.tensor_copy(tile_row[:], trow_f[:]))
            then(nc.vector.tensor_scalar(texp[:], texp[:], float(E - 1), None, ALU.min))
            nc.vector.tensor_copy(tile_expert[:], texp[:]).then_inc(table_done, 1)
            lv = lsel_all[:].rearrange("p (n k) -> p n k", k=K)
            nc.vector.tensor_tensor(ldiff[:], lv[:, :, 0], lv[:, :, 1], ALU.subtract).then_inc(gate_diff, 1)

            dve.wait_ge(moe_ld, 32)
            dve.wait_ge(table_done, 1)
            ex_regs = [dve.alloc_register(f"dve_expert{j}") for j in range(4)]
            last_ex = dve.alloc_register("dve_last_expert")

            def experts(t):
                dve.load(ex_regs, tile_expert[0:1, bass.ds(t, 4)])
                return [dve.snap(r, min_val=0, max_val=E - 1) for r in ex_regs]


            def put_hT(t, s, i):
                dve.wait_ge(slotT_ps, t + 1)
                if s >= 2 or again_turn(i):
                    dve.wait_ge(u3_ps, 2 * t - 2)
                if again_turn(i):
                    dve.wait_ge(y_scat[s % 2], 16 * RB * (TURN // 2 * i + s // 2 - 1))
                nc.vector.tensor_copy(to_place[:, s, :].unsqueeze(2), slots[:, s, :, D:HW])
                nc.vector.tensor_copy(hT3[:, s % 2, :], T[s % 2][:].bitcast(F16)[:, 0:2 * R]).then_inc(hT3_done, 1)

            def gated(t, s, i, h):
                dve.wait_ge(u3_ps, 2 * t + h + 1)
                dve.wait_ge(sg_done, 2 * t + h + 1)
                if s or again_turn(i):
                    dve.wait_ge(y_ps, t)
                nc.vector.scalar_tensor_tensor(gu[:, h, :], U[h], descale[:], sg[:, h, :],
                                               ALU.mult, ALU.mult).then_inc(gu_done, 1)

            def weigh(t, s, i, e):
                dve.wait_ge(ysq_done, RB * (t + 1))
                if s >= 2 or again_turn(i):
                    dve.wait_ge(y_scat[s % 2], 16 * RB * (TURN // 2 * i + s // 2))
                row = enorm[:, bass.ds(e * D, D)]
                nc.vector.tensor_tensor(yt[:, s % 2, :, 0:D], Y[s % 2][:, 0:RB * D].rearrange("p (r d) -> p r d", d=D),
                                        row.unsqueeze(1).to_broadcast([P, RB, D]), ALU.mult).then_inc(y_done[s], 1)

            def turn_of_tiles(i, first=False, last=False):
                ex, ahead = experts(TURN * i), None if first else dve.snap(last_ex, min_val=0, max_val=E - 1)
                for s in range(LAST if last else TURN):
                    gated(TURN * i + s, s, i, 0)
                    if s:
                        weigh(TURN * i + s - 1, s - 1, i, ex[s - 1])
                    elif not first:
                        weigh(TURN * i - 1, TURN - 1, i - 1, ahead)
                    gated(TURN * i + s, s, i, 1)
                    if s < (LAST if last else TURN) - 2:
                        put_hT(TURN * i + s + 2, s + 2, i)
                    elif not last:
                        put_hT(TURN * i + s + 2, s + 2 - TURN, i + 1)
                dve.reg_mov(last_ex, ex[(LAST if last else TURN) - 1])

            put_hT(0, 0, 0)
            put_hT(1, 1, 0)
            turn_of_tiles(0, first=True)
            with dve.Fori(1, TURNS - 1) as i:
                turn_of_tiles(i)
            turn_of_tiles(TURNS - 1, last=True)
            weigh(TILES - 1, LAST - 1, TURNS - 1, dve.snap(last_ex, min_val=0, max_val=E - 1))

            def coefficients(g):
                w = slice(LOADS[g][0] * NT, LOADS[g][1] * NT)
                dve.wait_ge(rms4_done, g + 1)
                nc.vector.reciprocal(rinv4[:, w], rms4[:, w]).then_inc(rinv4_done, 1)
                dve.wait_ge(rinv4_done, g + 1)
                nc.vector.tensor_tensor(coef[:, w], rinv4[:, w], gate_all[:, w], ALU.mult).then_inc(coef_done, 1)
                dve.wait_ge(coef_done, g + 1)

            def mix_experts(b, p, n):
                dve.wait_ge(half_done, b + 1)
                if again(n):
                    dve.wait_ge(mixT_ps, b - 1)
                    dve.wait_ge(ssq4_done, NT * (b - 1))
                for t in range(NT):
                    last = nc.vector.scalar_tensor_tensor(
                        mix[:, p, t, :], yb_of(b, t, 1), coef[:, bass.ds(b * NT + t, 1), 1],
                        half[:, p, t, :], ALU.mult, ALU.add)
                last.then_inc(mix_done, 1)

            def rms_out(b, p, n):
                dve.wait_ge(rms5_done, b + 1)
                nc.vector.reciprocal(rinv5[:, p, :], rms5[:, p, :]).then_inc(rinv5_done, 1)

            def add_out(b, p, n):
                dve.wait_ge(rinv5_done, b + 1)
                dve.wait_ge(o_ps, b + 1)
                if again(n):
                    dve.wait_ge(stored[p], 16 * (n - 1))
                for t in range(NT):
                    last = nc.vector.scalar_tensor_tensor(
                        ob[:, p, t, :], bk[2 + p][:, t * D:(t + 1) * D], rinv5[:, p, t:t + 1],
                        x_all[:, bass.ds(b * L + t * P, P)], ALU.mult, ALU.add)
                last.then_inc(ob_done, 1)

            dve.wait_ge(gate_sig, 1)
            coefficients(0)
            mix_experts(*batch_of_turn(0, 0))
            mix_experts(*batch_of_turn(0, 1))

            def turn_of_batches(i, batches):
                for j in batches:
                    before = batch_of_turn(i, j - 2)
                    rms_out(*before)
                    mix_experts(*batch_of_turn(i, j))
                    add_out(*before)

            coefficients(1)
            turn_of_batches(0, (2, 3))
            coefficients(2)
            turn_of_batches(1, (0, 1, 2))
            coefficients(3)
            turn_of_batches(1, (3,))
            with dve.Fori(2, B // 4) as i:
                turn_of_batches(i, range(4))
            for b in (B - 2, B - 1):
                rms_out(*batch_of_turn(0, b))
                add_out(*batch_of_turn(0, b))

        @block.tensor
        def _(pe):
            mm = nc.tensor.matmul
            pe.wait_ge(sc_done, 1)
            for j, part in enumerate((SA, CA, SB, CB)):
                last = mm(UB[:, j * B:(j + 1) * B], wmod_sb[:, part * D:(part + 1) * D], sc[:], start=True, stop=True)
            last.then_inc(modcol_ps, 1)
            wv = wmod_sb.rearrange("p (g k d) -> p g k d", g=2, k=3)[:, :, 2, :]
            mm(CUM[0][0:B, 0:2 * D].rearrange("p (g d) -> p g d", g=2), sc[:], wv, start=True,
               stop=True).then_inc(gate_ps, 1)

            pe.wait_ge(w_small, 1)
            mm(ND[:, 0:E], w_in_rows, wrn[:], start=True, stop=True).then_inc(router_ps, 1)

            def first(b):
                return isinstance(b, int) and b == 0

            def done_by(b):
                return min(b, B) if isinstance(b, int) else b

            def running_state(att, t):
                b, p, n = att
                pe.wait_ge(kv_done[t], b + 1)
                for cc in range(3):
                    if t:
                        pe.wait_ge(cum_used[t - 1][cc], b + 1)
                    elif not first(b):
                        pe.wait_ge(cum_used[NT - 1][cc], b)
                    elif cc == 0:
                        pe.wait_ge(gate_done, 1)
                    if t == 0 and cc == 2 and not first(b):
                        pe.wait_ge(den_done, b)
                    for j in range(THIRD):
                        e = cc * THIRD + j
                        last = mm(CUM[cc][:, j * P:(j + 1) * P], kv[:, p, t, e * D:(e + 1) * D], tri,
                                  start=True, stop=True)
                    last.then_inc(cum_ps[t][cc], 1)

            def head_sums(att, t):
                b, p, n = att
                num = ND[:, t * P:(t + 1) * P]
                pe.wait_ge(cum_used[t][2], b + 1)
                if t == 0:
                    if not first(b):
                        pe.wait_ge(attnT_done, b)
                    else:
                        pe.wait_ge(router_done, 1)
                for e in range(HD):
                    mm(num, sel[e], prod[:, t, e * P:(e + 1) * P], start=(e == 0), stop=(e == HD - 1))
                if t == NT - 1:
                    for u in range(NT):
                        last = mm(DEN[:, u * H:(u + 1) * H], prod[:, u, HD * P:HE * P], blk, start=True, stop=True)
                    last.then_inc(nd_ps, 1)

            def step(_nrm, qkv, att, prj, inp, rte):
                if inp is not None:
                    b, p, n = inp
                    pe.wait_ge(xn2_done, b + 1)
                    pe.wait_ge(q_done, done_by(b + 3))
                    for t in range(NT):
                        last = nc.tensor.transpose(TB[:, t * P:(t + 1) * P], xn2[:, p, t, :], ident)
                if qkv is not None:
                    b, p, n = qkv
                    pe.wait_ge(xn_done, b + 1)
                    if not first(b):
                        pe.wait_ge(q_done, b)
                    for t in range(NT):
                        last = nc.tensor.transpose(TB[:, L + t * P:L + (t + 1) * P], xn[:, p, t, :], ident)
                if inp is not None or qkv is not None:
                    last.then_inc(turn_ps, 1)
                if att is not None:
                    running_state(att, 0)
                if prj is not None:
                    pe.wait_ge(rden_e_done, prj[0] + 1)
                    for t in range(NT):
                        last = nc.tensor.transpose(ND[:, L + t * P:L + (t + 1) * P],
                                                   rden_e[:, t].rearrange("p e h -> p (e h)"), ident)
                    last.then_inc(rdenT_ps, 1)
                if qkv is not None:
                    b, p, n = qkv
                    pe.wait_ge(hT_done, b + 1)
                    if first(b):
                        pe.wait_ge(w_ld, 16 * 5)
                        pe.wait_ge(bias_part, 11)
                        pe.wait_ge(w_small, 3)
                    else:
                        pe.wait_ge(k_done, b)
                    for t in range(NT):
                        o = KV[:, t * 2 * D:(t + 1) * 2 * D]
                        mm(o, ones16[0:3, :], bkv3[:], start=True, stop=False)
                        last = mm(o, hT[:, p, t * P:(t + 1) * P], wqkv[:, D:3 * D], start=False, stop=True)
                    last.then_inc(kv_ps, 1)
                if qkv is not None:
                    b, p, n = qkv
                    if inp is not None:
                        pe.wait_ge(h2T_done, inp[0] + 1)
                    mm(TB[:, 0:L], wqkv[:, 0:D], hT[:, p, :], start=True, stop=True).then_inc(q_ps, 1)
                if att is not None:
                    running_state(att, 1)
                if prj is not None:
                    b, p, n = prj
                    pe.wait_ge(attnT_done, b + 1)
                    pe.wait_ge(wo_done, b + 1)
                    if not first(b):
                        pe.wait_ge(x1_done, b)
                    if rte is not None and not first(rte[0]):
                        pe.wait_ge(slot_done, rte[0])
                    for t in range(NT):
                        o = FFN[:, t * D:(t + 1) * D]
                        last = mm(o, attnT[:, p, t * P:(t + 1) * P], wo_ga[:, p, :], start=True, stop=True)
                    last.then_inc(x1_ps, 1)
                if inp is not None:
                    b, p, n = inp
                    pe.wait_ge(h2T_done, b + 1)
                    if not first(b):
                        pe.wait_ge(lo_done, b)
                    else:
                        pe.wait_ge(modcol_done, 1)
                    for t in range(NT):
                        last = mm(UL[:, t, :], h2T[:, p, t * P:(t + 1) * P], w_in, start=True, stop=True)
                    last.then_inc(u_ps, 1)
                if att is not None:
                    head_sums(att, 0)
                if rte is not None:
                    b, p, n = rte
                    pe.wait_ge(chosen_done, b + 1)
                    pe.wait_ge(x1_done, done_by(b + 3))
                    if not first(b):
                        pe.wait_ge(slot_done, b)
                        pe.wait_ge(count_done, b)
                    for t in range(NT):
                        o = RANK[:, t * E:(t + 1) * E]
                        mm(o, strict16[:], chosen[:, p, t, :], start=True, stop=False)
                        for u in range(t):
                            mm(o, ones16[:], chosen[:, p, u, :], start=False, stop=False)
                        last = mm(o, ones16[:], count[:, p, :], start=False, stop=True)
                    last.then_inc(rank_ps, 1)
                if att is not None:
                    head_sums(att, 1)

            pipelined(pe, step)

            pe.wait_ge(count_done, B)
            mm(bk[0][:, 0:E], ones16[:], count[:, 0, :], start=True, stop=True).then_inc(total_ps, 1)

            pe.wait_ge(table_done, 1)
            ex_regs = [pe.alloc_register(f"pe_expert{j}") for j in range(4)]
            last_ex = pe.alloc_register("pe_last_expert")

            def experts(t):
                pe.load(ex_regs, tile_expert[0:1, bass.ds(t, 4)])
                return [pe.snap(r, min_val=0, max_val=E - 1) for r in ex_regs]


            def transpose_rows(t, s, i):
                pe.wait_ge(slot_ld[s], 16 * (i + 1))
                if s >= 2 or again_turn(i):
                    pe.wait_ge(hT3_done, t - 1)
                o = T[s % 2][:].bitcast(F16)
                for half in range(2):
                    for r in range(RB):
                        last = nc.tensor.transpose(o[:, half * R + r * P:half * R + (r + 1) * P],
                                                   slots16[:, s, r, half * D:(half + 1) * D], ident16[:])
                last.then_inc(slotT_ps, 1)

            def gate_up(t, s, i, e, h):
                if h == 0:
                    pe.wait_ge(hT3_done, t + 1)
                hi, lo = hT3[:, s % 2, 0:R], hT3[:, s % 2, R:2 * R]
                for part, banks, done in ((0, G, g_ps), (1, U, u3_ps)):
                    if s or again_turn(i):
                        pe.wait_ge((sg_done, gu_done)[part], 2 * t + h - 1)
                    for c in range(FC // 2):
                        o = banks[h][:, c * R:(c + 1) * R]
                        w = bass.ds(e * F + (part * E * F + (h * (FC // 2) + c) * P), P)
                        mm(o, w_hi[:, w], hi, start=True, stop=False)
                        mm(o, w_hi[:, w], lo, start=False, stop=False)
                        last = mm(o, w_lo[:, w], hi, start=False, stop=True)
                    last.then_inc(done, 1)

            def down(t, s, i, e):
                pe.wait_ge(gu_done, 2 * t + 2)
                if s >= 2 or again_turn(i):
                    pe.wait_ge(y_done[(s + 2) % TURN], i + 1 if s >= 2 else i)
                for r in range(RB):
                    for f in range(FC):
                        h, c = f // (FC // 2), f % (FC // 2)
                        last = mm(Y[s % 2][:, r * D:(r + 1) * D], gu[:, h, c * R + r * P:c * R + (r + 1) * P],
                                  wd[:, bass.ds(e * (FC * D) + f * D, D)], start=(f == 0), stop=(f == FC - 1))
                last.then_inc(y_ps, 1)

            def turn_of_tiles(i, first=False, last=False):
                ex, ahead = experts(TURN * i), None if first else pe.snap(last_ex, min_val=0, max_val=E - 1)
                for s in range(LAST if last else TURN):
                    gate_up(TURN * i + s, s, i, ex[s], 0)
                    if s:
                        down(TURN * i + s - 1, s - 1, i, ex[s - 1])
                    elif not first:
                        down(TURN * i - 1, TURN - 1, i - 1, ahead)
                    gate_up(TURN * i + s, s, i, ex[s], 1)
                    if s < (LAST if last else TURN) - 2:
                        transpose_rows(TURN * i + s + 2, s + 2, i)
                    elif not last:
                        transpose_rows(TURN * i + s + 2, s + 2 - TURN, i + 1)
                pe.reg_mov(last_ex, ex[(LAST if last else TURN) - 1])

            pe.wait_ge(wlo_done, WN)
            pe.wait_ge(moe_ld, 32)
            transpose_rows(0, 0, 0)
            transpose_rows(1, 1, 0)
            turn_of_tiles(0, first=True)
            with pe.Fori(1, TURNS - 1) as i:
                turn_of_tiles(i)
            turn_of_tiles(TURNS - 1, last=True)
            down(TILES - 1, LAST - 1, TURNS - 1, pe.snap(last_ex, min_val=0, max_val=E - 1))

            def stage_d(b, p, n):
                pe.wait_ge(mix_done, b + 1)
                if again(n):
                    pe.wait_ge(mixT_done, b - 1)
                for t in range(NT):
                    last = nc.tensor.transpose(bk[p][:, t * P:(t + 1) * P], mix[:, p, t, :], ident)
                last.then_inc(mixT_ps, 1)

            def stage_e(b, p, n):
                pe.wait_ge(mixT_done, b + 1)
                if again(n):
                    pe.wait_ge(ob_done, b - 1)
                for t in range(NT):
                    last = mm(bk[2 + p][:, t * D:(t + 1) * D], mixT[:, p, t * P:(t + 1) * P],
                              gates_bc[:, bass.ds(b * 2 * D + D, D)], start=True, stop=True)
                last.then_inc(o_ps, 1)

            pe.wait_ge(wgb_done, 1)
            def turn_of_batches(i, batches=range(4)):
                for j in batches:
                    stage_d(*batch_of_turn(i, j))
                    stage_e(*batch_of_turn(i, j - 1))

            stage_d(*batch_of_turn(0, 0))
            turn_of_batches(0, range(1, 4))
            turn_of_batches(1)
            with pe.Fori(2, B // 4) as i:
                turn_of_batches(i)
            stage_e(*batch_of_turn(0, B - 1))


def kernel(L0_attn_x, L0_attn_qkv_w, L0_attn_qkv_b, L0_attn_out_w, L0_attn_out_b, L0_ffn_W_in, L0_ffn_in_norm_w,
           L0_ffn_Wr, L0_ffn_expert_bias, L0_ffn_Wg, L0_ffn_Wu, L0_ffn_Wd, L0_ffn_enorm_w, L0_ffn_out_norm_w,
           L0_ffn_W_out, L0_c, L0_wmod):
    import concourse.bacc as bacc
    from concourse.bass_utils import run_bass_kernel_spmd

    def arr(a):
        return np.ascontiguousarray(np.asarray(a))

    def gate_first(w):
        return np.asarray(w).transpose(2, 0, 1).reshape(D, E * F)

    consts, place, filler = shape_constants()
    qkv_w, qkv_b = np.asarray(L0_attn_qkv_w), np.asarray(L0_attn_qkv_b)
    small = [qkv_w.T,
             np.asarray(L0_attn_out_w).T.reshape(H, HD, D).transpose(1, 0, 2).reshape(D, D),
             np.asarray(L0_ffn_W_in).T, np.asarray(L0_ffn_Wr).T, np.asarray(L0_ffn_W_in), np.asarray(L0_ffn_W_out).T,
             qkv_b[0:D].reshape(D, 1), np.asarray(L0_ffn_in_norm_w).reshape(D, 1),
             np.asarray(L0_ffn_out_norm_w).reshape(D, 1)]
    arrays = {
        "x": arr(L0_attn_x),
        "c_wmod": arr(np.concatenate([np.asarray(L0_c).T, np.asarray(L0_wmod)], axis=1)),
        "weights_all": arr(np.concatenate(small, axis=1)),
        "qkv_b": arr(qkv_b.reshape(1, 3 * D)),
        "out_b": arr(np.asarray(L0_attn_out_b).reshape(1, D)),
        "e_bias": arr(np.asarray(L0_ffn_expert_bias).reshape(1, E)),
        "wguT": arr(np.concatenate([gate_first(L0_ffn_Wg), gate_first(L0_ffn_Wu)], axis=1)),
        "wdT": arr(np.asarray(L0_ffn_Wd).reshape(E, D, FC, P).transpose(3, 0, 2, 1).reshape(P, E * FC * D)),
        "e_norm": arr(np.asarray(L0_ffn_enorm_w).reshape(1, E * D)),
        "consts": consts, "place": place, "filler": filler,
    }
    nc = bacc.Bacc("TRN2", target_bir_lowering=False, num_devices=1)
    args = {n: nc.dram_tensor(n, a.shape, mybir.dt.from_np(a.dtype), kind="ExternalInput").ap()
            for n, a in arrays.items()}
    out = nc.dram_tensor("out", (B, L, D), F32, kind="ExternalOutput").ap()
    block_kernel(nc, **args, out=out)
    r = run_bass_kernel_spmd(nc, [arrays], core_ids=[0])
    return r.results[0]["out"]
```
